# Optimizing a Trainium2 kernel written in Bass

```python
import numpy as np
import jax
import jax.numpy as jnp

def _softmax(x, axis=-1):
    return jax.nn.softmax(x, axis=axis)

def _gelu(x):
    return jax.nn.gelu(x, approximate=True)

def _silu(x):
    return jax.nn.silu(x)

def _sigmoid(x):
    return jax.nn.sigmoid(x)

def _layernorm(x, axis=-1, eps=1e-05):
    m = jnp.mean(x, axis=axis, keepdims=True)
    v = jnp.var(x, axis=axis, keepdims=True)
    return (x - m) / jnp.sqrt(v + eps)

def _scatter_add(tgt, idx, src, axis=0):
    return tgt.at[idx].add(src)

def _segment_sum(src, seg, n):
    return jax.ops.segment_sum(src, seg, n)
kernel_name = 'mk_seq_preln_d2_jaxref_r8_5289cd'

def setup_inputs(seed: int=0):
    np.random.seed(seed)
    _w = jnp.asarray

    def _L0_attn_setup():
        import jax, jax.numpy as jnp
        import numpy as np
        B, S, D, H = (2, 256, 256, 16)
        HD = D // H

        def _alibi_slopes(num_heads):
            ratio = 2.0 ** (-8.0 / num_heads)
            return ratio ** jnp.arange(1, num_heads + 1, dtype=jnp.float32)
        key = jax.random.key(seed)
        ks = jax.random.split(key, 9)
        sd = 1.0 / np.sqrt(D)
        inp = {'x': jax.random.normal(ks[0], (B, S, D), dtype=jnp.float32)}
        for i, name in enumerate(['Wq', 'Wk', 'Wv', 'Wo']):
            inp[name] = jax.random.normal(ks[1 + i], (D, D), dtype=jnp.float32) * sd
        for i, name in enumerate(['bq', 'bk', 'bv', 'bo']):
            inp[name] = jax.random.normal(ks[5 + i], (D,), dtype=jnp.float32) * 0.02
        return inp
    _L0_attn_in = _L0_attn_setup()

    def _L0_ffn_setup():
        import jax, jax.numpy as jnp
        import numpy as np
        TOPK = 2
        NORM_TOPK = True
        SCALE = 1.0
        EPS = 1e-09
        key = jax.random.key(seed)
        ks = jax.random.split(key, 9)
        h, i, E = (256, 128, 16)
        std = 0.02
        return {'x': jax.random.normal(ks[0], (1, 256, h), jnp.float32), 'Wr': jax.random.normal(ks[1], (E, h), jnp.float32) * std, 'bias': jnp.zeros((E,), jnp.float32), 'Wg': jax.random.normal(ks[2], (E, h, i), jnp.float32) * std, 'Wu': jax.random.normal(ks[3], (E, h, i), jnp.float32) * std, 'Wd': jax.random.normal(ks[4], (E, i, h), jnp.float32) * std, 'sWg': jax.random.normal(ks[5], (h, i), jnp.float32) * std, 'sWu': jax.random.normal(ks[6], (h, i), jnp.float32) * std, 'sWd': jax.random.normal(ks[7], (i, h), jnp.float32) * std}
    _L0_ffn_in = _L0_ffn_setup()

    def _L1_attn_setup():
        import jax, jax.numpy as jnp
        import numpy as np
        HIDDEN_DIM = 256
        NUM_HEAD = 16
        HEAD_DIM = HIDDEN_DIM // NUM_HEAD
        key = jax.random.key(seed)
        k0, k1, k2, k3, k4 = jax.random.split(key, 5)
        B, S = (2, 256)
        scale = 1.0 / np.sqrt(HIDDEN_DIM)
        return {'hidden_states': jax.random.normal(k0, (B, S, HIDDEN_DIM), dtype=jnp.float32), 'W_attn': jax.random.normal(k1, (HIDDEN_DIM, 3 * HIDDEN_DIM), dtype=jnp.float32) * scale, 'b_attn': jax.random.normal(k2, (3 * HIDDEN_DIM,), dtype=jnp.float32) * 0.02, 'W_proj': jax.random.normal(k3, (HIDDEN_DIM, HIDDEN_DIM), dtype=jnp.float32) * scale, 'b_proj': jax.random.normal(k4, (HIDDEN_DIM,), dtype=jnp.float32) * 0.02}
    _L1_attn_in = _L1_attn_setup()

    def _L1_ffn_setup():
        import jax, jax.numpy as jnp
        import numpy as np
        NUM_EXPERTS = 32
        TOP_K = 8
        THRESHOLD = 0.8
        HIDDEN = 256
        INTER = 96
        key = jax.random.key(seed)
        k1, k2, k3, k4 = jax.random.split(key, 4)
        hidden_states = jax.random.normal(k1, (2, 128, HIDDEN), jnp.float32)
        gate_weight = jax.random.normal(k2, (NUM_EXPERTS, HIDDEN), jnp.float32) * 0.02
        gate_up_proj = jax.random.normal(k3, (NUM_EXPERTS, 2 * INTER, HIDDEN), jnp.float32) * 0.02
        down_proj = jax.random.normal(k4, (NUM_EXPERTS, HIDDEN, INTER), jnp.float32) * 0.02
        return {'hidden_states': hidden_states, 'gate_weight': gate_weight, 'gate_up_proj': gate_up_proj, 'down_proj': down_proj}
    _L1_ffn_in = _L1_ffn_setup()
    _d = {'L0_attn_x': _L0_attn_in['x'], 'L0_attn_Wq': _L0_attn_in['Wq'], 'L0_attn_bq': _L0_attn_in['bq'], 'L0_attn_Wk': _L0_attn_in['Wk'], 'L0_attn_bk': _L0_attn_in['bk'], 'L0_attn_Wv': _L0_attn_in['Wv'], 'L0_attn_bv': _L0_attn_in['bv'], 'L0_attn_Wo': _L0_attn_in['Wo'], 'L0_attn_bo': _L0_attn_in['bo'], 'L0_ffn_Wr': _L0_ffn_in['Wr'], 'L0_ffn_bias': _L0_ffn_in['bias'], 'L0_ffn_Wg': _L0_ffn_in['Wg'], 'L0_ffn_Wu': _L0_ffn_in['Wu'], 'L0_ffn_Wd': _L0_ffn_in['Wd'], 'L0_ffn_sWg': _L0_ffn_in['sWg'], 'L0_ffn_sWu': _L0_ffn_in['sWu'], 'L0_ffn_sWd': _L0_ffn_in['sWd'], 'L1_attn_W_attn': _L1_attn_in['W_attn'], 'L1_attn_b_attn': _L1_attn_in['b_attn'], 'L1_attn_W_proj': _L1_attn_in['W_proj'], 'L1_attn_b_proj': _L1_attn_in['b_proj'], 'L1_ffn_gate_weight': _L1_ffn_in['gate_weight'], 'L1_ffn_gate_up_proj': _L1_ffn_in['gate_up_proj'], 'L1_ffn_down_proj': _L1_ffn_in['down_proj']}
    _x0 = _d['L0_attn_x']
    _d['L0_attn_x'] = jax.random.normal(jax.random.fold_in(jax.random.key(seed), 1), (8, 512, 256), dtype=_x0.dtype)
    del _x0
    return _d

def reference(L0_attn_x, L0_attn_Wq, L0_attn_bq, L0_attn_Wk, L0_attn_bk, L0_attn_Wv, L0_attn_bv, L0_attn_Wo, L0_attn_bo, L0_ffn_Wr, L0_ffn_bias, L0_ffn_Wg, L0_ffn_Wu, L0_ffn_Wd, L0_ffn_sWg, L0_ffn_sWu, L0_ffn_sWd, L1_attn_W_attn, L1_attn_b_attn, L1_attn_W_proj, L1_attn_b_proj, L1_ffn_gate_weight, L1_ffn_gate_up_proj, L1_ffn_down_proj):

    def _L0_attn_ref(x, Wq, bq, Wk, bk, Wv, bv, Wo, bo):
        import jax, jax.numpy as jnp
        import numpy as np
        B, S, D, H = (2, 256, 256, 16)
        HD = D // H

        def _alibi_slopes(num_heads):
            ratio = 2.0 ** (-8.0 / num_heads)
            return ratio ** jnp.arange(1, num_heads + 1, dtype=jnp.float32)
        b, s, d = x.shape

        def proj(W, bias):
            return (x @ W + bias).reshape(b, s, H, HD).transpose(0, 2, 1, 3)
        q, k, v = (proj(Wq, bq), proj(Wk, bk), proj(Wv, bv))
        scores = jnp.einsum('bhqd,bhkd->bhqk', q, k) / jnp.sqrt(jnp.float32(HD))
        distances = jnp.arange(1 - s, 1, dtype=jnp.float32)
        bias = _alibi_slopes(H)[None, :, None, None] * distances[None, None, None, :]
        scores = scores + bias
        causal = jnp.tril(jnp.ones((s, s), dtype=bool))[None, None]
        scores = jnp.where(causal, scores, jnp.finfo(scores.dtype).min)
        attn = jax.nn.softmax(scores, axis=-1)
        ctx = jnp.einsum('bhqk,bhkd->bhqd', attn, v)
        ctx = ctx.transpose(0, 2, 1, 3).reshape(b, s, d)
        return ctx @ Wo + bo

    def _L0_ffn_ref(x, Wr, bias, Wg, Wu, Wd, sWg, sWu, sWd):
        import jax, jax.numpy as jnp
        import numpy as np
        TOPK = 2
        NORM_TOPK = True
        SCALE = 1.0
        EPS = 1e-09
        b, s, h = x.shape
        E = Wr.shape[0]
        xt = x.reshape(b * s, h)
        logits = xt @ Wr.T + bias
        probs = jax.nn.softmax(logits, axis=-1)
        topk_val, topk_idx = jax.lax.top_k(probs, TOPK)
        if NORM_TOPK:
            w = topk_val / (jnp.sum(topk_val, axis=-1, keepdims=True) + EPS)
        else:
            w = topk_val
        w = w * SCALE
        g = jnp.einsum('th,ehi->tei', xt, Wg)
        u = jnp.einsum('th,ehi->tei', xt, Wu)
        y = jnp.einsum('tei,eih->teh', jax.nn.silu(g) * u, Wd)
        oh = jax.nn.one_hot(topk_idx, E, dtype=x.dtype)
        routed = jnp.einsum('tke,tk,teh->th', oh, w, y)
        shared = jax.nn.silu(xt @ sWg) * (xt @ sWu) @ sWd
        return (routed + shared).reshape(b, s, h)

    def _L1_attn_ref(hidden_states, W_attn, b_attn, W_proj, b_proj):
        import jax, jax.numpy as jnp
        import numpy as np
        HIDDEN_DIM = 256
        NUM_HEAD = 16
        HEAD_DIM = HIDDEN_DIM // NUM_HEAD
        B, S, D = hidden_states.shape
        H, Hd = (NUM_HEAD, HEAD_DIM)
        qkv = hidden_states @ W_attn + b_attn
        q, k, v = jnp.split(qkv, 3, axis=-1)

        def heads(x):
            return x.reshape(B, S, H, Hd).transpose(0, 2, 1, 3)
        q, k, v = (heads(q), heads(k), heads(v))
        scores = jnp.einsum('bhsd,bhtd->bhst', q, k) / jnp.sqrt(jnp.float32(Hd))
        causal = jnp.tril(jnp.ones((S, S), dtype=bool))
        scores = jnp.where(causal, scores, -jnp.inf)
        probs = jax.nn.softmax(scores, axis=-1)
        out = jnp.einsum('bhst,bhtd->bhsd', probs, v)
        out = out.transpose(0, 2, 1, 3).reshape(B, S, D)
        return out @ W_proj + b_proj

    def _L1_ffn_ref(hidden_states, gate_weight, gate_up_proj, down_proj):
        import jax, jax.numpy as jnp
        import numpy as np
        NUM_EXPERTS = 32
        TOP_K = 8
        THRESHOLD = 0.8
        HIDDEN = 256
        INTER = 96
        B, S, H = hidden_states.shape
        x = hidden_states.reshape(-1, H)
        logits = x @ gate_weight.T
        probs = jax.nn.softmax(logits.astype(jnp.float32), axis=-1).astype(logits.dtype)
        top_vals, top_idx = jax.lax.top_k(probs, TOP_K)
        renorm = top_vals / jnp.clip(jnp.sum(top_vals, axis=-1, keepdims=True), 1e-12)
        cum = jnp.cumsum(renorm, axis=-1)
        num_keep = jnp.minimum(jnp.sum((cum < THRESHOLD).astype(jnp.int32), axis=-1) + 1, TOP_K)
        active = jnp.arange(TOP_K)[None, :] < num_keep[:, None]
        rw = top_vals * active.astype(top_vals.dtype)
        rw = rw / jnp.clip(jnp.sum(rw, axis=-1, keepdims=True), 1e-12)
        combine = jnp.sum(jax.nn.one_hot(top_idx, NUM_EXPERTS, dtype=rw.dtype) * rw[..., None], axis=1)

        def body(acc, params):
            w_gu, w_d, ce = params
            gu = x @ w_gu.T
            g, u = jnp.split(gu, 2, axis=-1)
            h = jax.nn.silu(g) * u
            return (acc + h @ w_d.T * ce[:, None], None)
        out, _ = jax.lax.scan(body, jnp.zeros_like(x), (gate_up_proj, down_proj, combine.T))
        return out.reshape(B, S, H)
    x = L0_attn_x
    x = x + _L0_attn_ref(_layernorm(x, axis=-1), L0_attn_Wq, L0_attn_bq, L0_attn_Wk, L0_attn_bk, L0_attn_Wv, L0_attn_bv, L0_attn_Wo, L0_attn_bo)
    x = x + _L0_ffn_ref(_layernorm(x, axis=-1), L0_ffn_Wr, L0_ffn_bias, L0_ffn_Wg, L0_ffn_Wu, L0_ffn_Wd, L0_ffn_sWg, L0_ffn_sWu, L0_ffn_sWd)
    x = x + _L1_attn_ref(_layernorm(x, axis=-1), L1_attn_W_attn, L1_attn_b_attn, L1_attn_W_proj, L1_attn_b_proj)
    x = x + _L1_ffn_ref(_layernorm(x, axis=-1), L1_ffn_gate_weight, L1_ffn_gate_up_proj, L1_ffn_down_proj)
    return x

_drawn_inputs = setup_inputs


def setup_inputs(seed=0):
    import zlib

    import numpy as np

    out = dict(_drawn_inputs(seed))
    spreads = {'L0_ffn_bias': (0.0, 0.8)}
    factors = {'L0_attn_bq': 8.0,
     'L0_attn_bk': 64.0,
     'L0_ffn_Wr': 7.585,
     'L0_ffn_Wg': 7.056,
     'L0_ffn_Wu': 6.962,
     'L0_ffn_Wd': 6.959,
     'L0_ffn_sWg': 5.061,
     'L0_ffn_sWu': 4.949,
     'L0_ffn_sWd': 4.978,
     'L1_attn_b_proj': 3.145,
     'L1_ffn_gate_weight': 8.0,
     'L1_ffn_gate_up_proj': 8.0,
     'L1_ffn_down_proj': 8.0,
     'L1_attn_b_attn': 2.942}
    for name, (base, spread) in spreads.items():
        noise = np.random.default_rng([zlib.crc32(name.encode()), seed]).standard_normal(out[name].shape)
        drawn = base * np.exp(spread * noise) if base else spread * noise
        out[name] = jnp.asarray(drawn.astype(out[name].dtype))
    for name, factor in factors.items():
        out[name] = (out[name] * factor).astype(out[name].dtype)
    return out
```

```python
from contextlib import ExitStack

import concourse.bass as bass
from concourse import mybir

P = 128
F32 = mybir.dt.float32
F32R = mybir.dt.float32r
BF16 = mybir.dt.bfloat16
U32 = mybir.dt.uint32
ACT = mybir.ActivationFunctionType
ALU = mybir.AluOpType
X = mybir.AxisListType.X

EPS = 1e-5
D = 256
DC = D // P
H = 16
HD = D // H
SEQ = 512
TG = SEQ // P
BANK = 512
STACK = 64
ROWS_MAX = 50
ROWS_ALL = 52
VW = 32
NEG = -1e30


class Pool_:

    def __init__(self, nc, ctx, tag):
        self.nc, self.ctx, self.tag = nc, ctx, tag

    def sb(self, name, shape, dt=F32):
        return self.ctx.enter_context(self.nc.sbuf_tensor(f"{self.tag}_{name}", shape, dt))

    def sem(self, name):
        return self.ctx.enter_context(self.nc.semaphore(f"{self.tag}_{name}"))


def product3(pe, out, a_hi, a_lo, b_hi, b_lo, first, last, shared_bank=False):
    pe.matmul(out, a_hi, b_hi, start=first, stop=False, skip_group_check=shared_bank)
    pe.matmul(out, a_hi, b_lo, start=False, stop=False, skip_group_check=shared_bank)
    return pe.matmul(out, a_lo, b_hi, start=False, stop=last, skip_group_check=shared_bank)


def layernorm_vector(dve, x_rows, stats6, mean_var, rstd, xn, var_ready, rstd_ready, xn_ready, n):
    for t in range(TG):
        dve.bn_stats(stats6[:, t, :], x_rows(t))
    dve.drain()
    for t in range(TG):
        dve.bn_aggr(mean_var[:, t, :], stats6[:, t, :])
    dve.drain()
    dve.tensor_scalar(mean_var[:, :, 1], mean_var[:, :, 1], EPS, None, ALU.add).then_inc(var_ready, 1)
    dve.wait_ge(rstd_ready, n + 1)
    for t in range(TG):
        ins = dve.tensor_scalar(xn[:, t, :], x_rows(t), mean_var[:, t, 0:1], rstd[:, t:t + 1],
                                ALU.subtract, ALU.mult)
    ins.then_inc(xn_ready, 1)


def attention_stage(nc, tag, x, psum, const, wqkv, wo, bqkv, bo, alibi, NG, x_in=None):
    with ExitStack() as ctx:
        mem = Pool_(nc, ctx, tag)
        wqkv_hi, wqkv_lo = (mem.sb(f"wqkv_{s}", [P, DC, 3 * D], F32R) for s in ("hi", "lo"))
        wo_hi, wo_lo = (mem.sb(f"wo_{s}", [P, DC, D], F32R) for s in ("hi", "lo"))
        bias_qkv = mem.sb("bias_qkv", [P, 3 * D])
        bias_o = mem.sb("bias_o", [P, D])
        stats6 = mem.sb("stats6", [P, TG, 6])
        mean_var = mem.sb("mean_var", [P, TG, 2])
        rstd = mem.sb("rstd", [P, TG])
        xn = mem.sb("xn", [P, TG, D])
        xT_hi, xT_lo = (mem.sb(f"xT_{s}", [P, DC, SEQ], F32R) for s in ("hi", "lo"))
        qk = mem.sb("qk", [P, TG, 2 * D])
        q_stack = mem.sb("q_stack", [P, TG, H, STACK])
        k_stack = mem.sb("k_stack", [P, TG, H, STACK])
        qT = mem.sb("qT", [P, H // 2, SEQ], F32R)
        kT = mem.sb("kT", [P, H // 2, SEQ], F32R)
        v = mem.sb("v", [P, TG, H, VW])
        probs = mem.sb("probs", [P, 2, 10, BANK])
        neg_max = mem.sb("neg_max", [P, TG, H])
        ctxT_raw = mem.sb("ctxT_raw", [P, H // 4, SEQ])
        inv_sum = mem.sb("inv_sum", [P, TG, H])
        ctx_n = mem.sb("ctx_n", [P, TG, D])

        weights_in = mem.sem("weights_in")
        consts_in = mem.sem("consts_in")
        weights_split = mem.sem("weights_split")
        stack_const = mem.sem("stack_const")
        var_ready, rstd_ready, xn_ready = (mem.sem(s) for s in ("var_ready", "rstd_ready", "xn_ready"))
        xnT_ready = mem.sem("xnT_ready")
        xT_hi_ready = mem.sem("xT_hi_ready")
        xT_lo_ready = mem.sem("xT_lo_ready")
        qkv_ready = mem.sem("qkv_ready")
        qk_ready = mem.sem("qk_ready")
        v_ready = mem.sem("v_ready")
        stack_hi_ready = mem.sem("stack_hi_ready")
        stack_lo_ready = mem.sem("stack_lo_ready")
        stack_dup_ready = mem.sem("stack_dup_ready")
        stackT_ready = mem.sem("stackT_ready")
        qT_ready = mem.sem("qT_ready")
        kT_ready = mem.sem("kT_ready")
        max_scores_ready = mem.sem("max_scores_ready")
        max_scores_used = mem.sem("max_scores_used")
        max_ready = mem.sem("max_ready")
        q2T_ready = mem.sem("q2T_ready")
        q2T_copied = mem.sem("q2T_copied")
        scores_ready = mem.sem("scores_ready")
        probs_ready = mem.sem("probs_ready")
        ctxT_ready = mem.sem("ctxT_ready")
        ctxT_copied = mem.sem("ctxT_copied")
        ctx_ready = mem.sem("ctx_ready")
        ctx_normed = mem.sem("ctx_normed")
        cT_ready = mem.sem("cT_ready")
        cT_hi_ready = mem.sem("cT_hi_ready")
        cT_lo_ready = mem.sem("cT_lo_ready")
        proj_ready = mem.sem("proj_ready")
        x_biased = mem.sem("x_biased")
        x_done = mem.sem("x_done")

        raw_qkv = probs[:, 0, 0:3, :].rearrange("p a b -> p (a b)").rearrange("p (c n) -> p c n", c=DC)
        raw_o = probs[:, 0, 3, :].rearrange("p (c n) -> p c n", c=DC)
        PAIRS = H // 2
        GROUPS = H // 4
        ITEMS = 10
        NI = GROUPS * ITEMS

        def x_rows(g, t):
            return x[:, bass.ds(g * (TG * D) + t * D, D)]

        def max_item(i):
            if i >= 8:
                return [(i - 8, 1, 0, 2 * P), (i - 6, 1, 2 * P, 2 * P)]
            return [(i // 2, 3, 0, 4 * P)] if i % 2 == 0 else [(i // 2, 0, 0, P), (i // 2, 2, P, 3 * P)]

        def prob_item(i):
            if i >= 8:
                return [(i - 8, 2, 0, 2 * P), (i - 6, 2, 2 * P, 2 * P)]
            return [(i // 2, 0, 0, 4 * P)] if i % 2 == 0 else [(i // 2, 1, 0, 3 * P), (i // 2, 3, 3 * P, P)]

        def probs_of(group, j, kt):
            item, col = {0: (2 * j, 0), 1: (2 * j + 1, 0), 3: (2 * j + 1, 3 * P),
                         2: (8 + j % 2, j // 2 * 2 * P)}[kt]
            return probs[:, group % 2, item, col:col + SEQ - kt * P]

        block = ctx.enter_context(nc.Block())

        @block.sync
        def _(sp):
            sp.dma_start(raw_qkv, wqkv.rearrange("(c p) n -> p c n", p=P)).then_inc(weights_in, 16)
            sp.dma_start(raw_o, wo.rearrange("(c p) n -> p c n", p=P)).then_inc(weights_in, 16)
            sp.dma_start(bias_qkv[:], bqkv.partition_broadcast(P)).then_inc(consts_in, 16)
            sp.dma_start(bias_o[:], bo.partition_broadcast(P)).then_inc(consts_in, 16)
            sp.wait_ge(x_done, 1)

        @block.gpsimd
        def _(pool):
            pool.memset(q_stack[:], 0.0)
            pool.memset(k_stack[:], 0.0)
            pool.memset(v[:], 0.0)
            pool.drain()
            pool.memset(q_stack[:, :, :, 48:50], 1.0)
            pool.memset(k_stack[:, :, :, 50:52], 1.0)
            pool.memset(v[:, :, :, HD:HD + 1], 1.0).then_inc(stack_const, 1)
            pool.wait_ge(consts_in, 32)
            with pool.Fori(0, NG) as g:
                pool.wait_ge(var_ready, g + 1)
                pool.tensor_tensor(rstd[:], mean_var[:, :, 1], const.minus_half[:, 0:TG],
                                   ALU.pow).then_inc(rstd_ready, 1)
                pool.wait_ge(xn_ready, g + 1)
                for t in range(TG):
                    ins = pool.tensor_tensor(x_rows(g, t), x_rows(g, t), bias_o[:], ALU.add)
                ins.then_inc(x_biased, 1)
                for t in range(TG):
                    pool.wait_ge(stack_hi_ready, g * TG + t + 1)
                    q_hi = q_stack[:, t, :, 0:16]
                    one = const.ones[:, 0:1].unsqueeze(2).to_broadcast([P, H, HD])
                    pool.tensor_tensor(q_stack[:, t, :, 32:48], q_hi, one, ALU.mult)
                    pool.tensor_copy(k_stack[:, t, :, 16:32], k_stack[:, t, :, 0:16]).then_inc(stack_dup_ready, 1)

        @block.scalar
        def _(act):
            act.wait_ge(weights_in, 32)
            act.activation(wqkv_hi[:], raw_qkv, ACT.Copy)
            act.activation(wo_hi[:], raw_o, ACT.Copy).then_inc(weights_split, 1)
            act.wait_ge(stack_const, 1)
            with act.Fori(0, NG) as g:
                for c in range(DC):
                    act.wait_ge(xnT_ready, g * DC + c + 1)
                    act.activation(xT_hi[:, c, :], psum[:, c, :], ACT.Copy).then_inc(xT_hi_ready, 1)
                for t in range(TG):
                    act.wait_ge(qk_ready, g * TG + t + 1)
                    act.activation(q_stack[:, t, :, 0:16].bitcast(F32R),
                                   qk[:, t, 0:D].rearrange("p (h d) -> p h d", h=H), ACT.Copy)
                    act.activation(k_stack[:, t, :, 0:16].bitcast(F32R),
                                   qk[:, t, D:2 * D].rearrange("p (h d) -> p h d", h=H),
                                   ACT.Copy).then_inc(stack_hi_ready, 1)
                for pr in range(PAIRS):
                    act.wait_ge(stackT_ready, g * (2 * PAIRS) + 2 * pr + 1)
                    act.activation(qT[:, pr, :], psum[:, 3 + (2 * pr) % 4, :], ACT.Copy).then_inc(qT_ready, 1)
                for grp in range(GROUPS):
                    for u in range(2):
                        act.wait_ge(q2T_ready, g * PAIRS + 2 * grp + u + 1)
                        act.activation(qT[:, 2 * grp + u, :], psum[:, 6, :], ACT.Copy).then_inc(q2T_copied, 1)
                    if grp >= 2:
                        act.wait_ge(ctxT_ready, g * GROUPS + grp - 1)
                    for i in range(ITEMS):
                        n = grp * ITEMS + i
                        act.wait_ge(scores_ready, g * NI + n + 1)
                        act.activation(probs[:, grp % 2, i, :], psum[:, 3 + n % 3, :], ACT.Exp,
                                       scale=float(HD) ** -0.5).then_inc(probs_ready, 1)
                for c in range(DC):
                    act.wait_ge(cT_ready, g * DC + c + 1)
                    act.activation(xT_hi[:, c, :], psum[:, 4 + c, :], ACT.Copy).then_inc(cT_hi_ready, 1)

        @block.vector
        def _(dve):
            dve.wait_ge(weights_split, 1)
            dve.tensor_tensor(wqkv_lo[:], raw_qkv, wqkv_hi[:].bitcast(F32), ALU.subtract)
            dve.tensor_tensor(wo_lo[:], raw_o, wo_hi[:].bitcast(F32), ALU.subtract).then_inc(weights_split, 1)
            dve.wait_ge(consts_in, 32)
            dve.wait_ge(stack_const, 1)
            if alibi is not None:
                for col, op in ((48, None), (49, ALU.subtract)):
                    dst = k_stack[:, :, :, col].bitcast(F32R)
                    if op is None:
                        dve.tensor_copy(dst, alibi)
                    else:
                        dve.tensor_tensor(dst, alibi, k_stack[:, :, :, 48], op)
                    dve.drain()
            with dve.Fori(0, NG) as g:
                layernorm_vector(dve, lambda t: x_rows(g, t), stats6, mean_var, rstd, xn,
                                 var_ready, rstd_ready, xn_ready, g)
                for c in range(DC):
                    dve.wait_ge(xT_hi_ready, g * DC + c + 1)
                    dve.tensor_tensor(xT_lo[:, c, :], psum[:, c, :], xT_hi[:, c, :].bitcast(F32),
                                      ALU.subtract).then_inc(xT_lo_ready, 1)
                for t in range(TG):
                    dve.wait_ge(qkv_ready, g * TG + t + 1)
                    dve.tensor_tensor(qk[:, t, :], psum[:, 2 * t, :], bias_qkv[:, 0:2 * D],
                                      ALU.add).then_inc(qk_ready, 1)
                    dve.tensor_tensor(v[:, t, :, 0:HD], psum[:, 2 * t + 1, 0:D].rearrange("p (h d) -> p h d", h=H),
                                      bias_qkv[:, 2 * D:3 * D].rearrange("p (h d) -> p h d", h=H),
                                      ALU.add).then_inc(v_ready, 1)
                for t in range(TG):
                    dve.wait_ge(stack_hi_ready, g * TG + t + 1)
                    dve.tensor_tensor(q_stack[:, t, :, 16:32].bitcast(F32R),
                                      qk[:, t, 0:D].rearrange("p (h d) -> p h d", h=H),
                                      q_stack[:, t, :, 0:16], ALU.subtract)
                    dve.tensor_tensor(k_stack[:, t, :, 32:48].bitcast(F32R),
                                      qk[:, t, D:2 * D].rearrange("p (h d) -> p h d", h=H),
                                      k_stack[:, t, :, 0:16], ALU.subtract).then_inc(stack_lo_ready, 1)
                for pr in range(PAIRS):
                    dve.wait_ge(stackT_ready, g * (2 * PAIRS) + 2 * pr + 2)
                    dve.tensor_copy(kT[:, pr, :], psum[:, 3 + (2 * pr + 1) % 4, :]).then_inc(kT_ready, 1)

                def copy_ctxT(grp):
                    dve.wait_ge(ctxT_ready, g * GROUPS + grp + 1)
                    dve.tensor_copy(ctxT_raw[:, grp, :], psum[:, 7, :]).then_inc(ctxT_copied, 1)

                for grp in range(GROUPS):
                    for i in range(ITEMS):
                        n = grp * ITEMS + i
                        dve.wait_ge(max_scores_ready, g * NI + n + 1)
                        if i >= 8:
                            ins = dve.tensor_reduce(neg_max[:, 1, 4 * grp + i - 8:4 * grp + i - 5:2],
                                                    psum[:, n % 3, :].rearrange("p (a k) -> p a k", a=2),
                                                    X, ALU.max, negate=True)
                        else:
                            for j, t, col, w in max_item(i):
                                head = 4 * grp + j
                                ins = dve.tensor_reduce(neg_max[:, t, head:head + 1], psum[:, n % 3, col:col + w],
                                                        X, ALU.max, negate=True)
                        ins.then_inc(max_scores_used, 1)
                    dve.drain()
                    cols = slice(4 * grp, 4 * grp + 4)
                    dve.tensor_copy(q_stack[:, :, cols, 50].bitcast(F32R), neg_max[:, :, cols])
                    dve.drain()
                    dve.tensor_tensor(q_stack[:, :, cols, 51].bitcast(F32R), neg_max[:, :, cols],
                                      q_stack[:, :, cols, 50], ALU.subtract).then_inc(max_ready, 1)
                    if grp >= 2:
                        copy_ctxT(grp - 2)
                copy_ctxT(GROUPS - 2)
                copy_ctxT(GROUPS - 1)
                for t in range(TG):
                    dve.wait_ge(ctx_ready, g * TG + t + 1)
                    dve.reciprocal(inv_sum[:, t, :], psum[:, t, HD:BANK:VW])
                dve.drain()
                for t in range(TG):
                    dve.tensor_tensor(ctx_n[:, t, :].rearrange("p (h d) -> p h d", h=H),
                                      psum[:, t, :].rearrange("p (h d) -> p h d", h=H)[:, :, 0:HD],
                                      inv_sum[:, t, :].unsqueeze(2).to_broadcast([P, H, HD]),
                                      ALU.mult).then_inc(ctx_normed, 1)
                for c in range(DC):
                    dve.wait_ge(cT_hi_ready, g * DC + c + 1)
                    dve.tensor_tensor(xT_lo[:, c, :], psum[:, 4 + c, :], xT_hi[:, c, :].bitcast(F32),
                                      ALU.subtract).then_inc(cT_lo_ready, 1)
                dve.wait_ge(x_biased, g + 1)
                for u in range(TG // 2):
                    dve.wait_ge(proj_ready, g * (TG // 2) + u + 1)
                    rows = x[:, bass.ds(g * (TG * D) + 2 * u * D, 2 * D)]
                    ins = dve.tensor_tensor(rows, rows, psum[:, 6 + u, :], ALU.add)
                ins.then_inc(x_done, 1)
                dve.drain()

        @block.tensor
        def _(pe):
            pe.wait_ge(weights_split, 2)

            with pe.Fori(0, NG) as g:
                pe.wait_ge(xn_ready, g + 1)
                for c in range(DC):
                    for t in range(TG):
                        ins = pe.transpose(psum[:, c, t * P:(t + 1) * P], xn[:, t, c * P:(c + 1) * P], const.ident[:])
                    ins.then_inc(xnT_ready, 1)
                pe.wait_ge(xT_lo_ready, g * DC + DC)
                for t in range(TG):
                    for bank, c0, c1 in ((2 * t, 0, 2 * D), (2 * t + 1, 2 * D, 3 * D)):
                        for c in range(DC):
                            tok = slice(t * P, (t + 1) * P)
                            ins = product3(pe, psum[:, bank, 0:c1 - c0], xT_hi[:, c, tok], xT_lo[:, c, tok],
                                           wqkv_hi[:, c, c0:c1], wqkv_lo[:, c, c0:c1], c == 0, c == DC - 1)
                    ins.then_inc(qkv_ready, 1)
                pe.wait_ge(stack_lo_ready, g * TG + TG)
                pe.wait_ge(stack_dup_ready, g * TG + TG)
                pe.wait_ge(v_ready, g * TG + TG)

                for pr in range(PAIRS):
                    for side, stack in enumerate((q_stack, k_stack)):
                        m = 2 * pr + side
                        if m >= 4:
                            pe.wait_ge((qT_ready, kT_ready)[side], g * PAIRS + pr - 1)
                        for t in range(TG):
                            ins = pe.transpose(psum[:, 3 + m % 4, t * P:(t + 1) * P],
                                               stack[:, t, 2 * pr:2 * pr + 2, :].rearrange("p a b -> p (a b)"),
                                               const.ident[:])
                        ins.then_inc(stackT_ready, 1)

                def stack_rows(sT, head, rows, c0, c1):
                    row = STACK * (head % 2)
                    return sT[row:row + rows, head // 2, c0:c1]

                def max_scores(n):
                    grp, i = n // ITEMS, n % ITEMS
                    if i % 4 == 0 and i < 8:
                        pe.wait_ge(qT_ready, g * PAIRS + 2 * grp + i // 4 + 1)
                        pe.wait_ge(kT_ready, g * PAIRS + 2 * grp + i // 4 + 1)
                    if n >= 3:
                        pe.wait_ge(max_scores_used, g * NI + n - 2)
                    for j, t, col, w in max_item(i):
                        pe.matmul(psum[:, n % 3, col:col + w],
                                  stack_rows(qT, 4 * grp + j, ROWS_MAX, t * P, (t + 1) * P),
                                  stack_rows(kT, 4 * grp + j, ROWS_MAX, 0, w), start=True, stop=False)
                        ins = pe.matmul(psum[:, n % 3, col + w - P:col + w], const.ident_bf[:], const.mask_q[:],
                                        start=False, stop=True)
                    ins.then_inc(max_scores_ready, 1)

                def prob_scores(n):
                    grp, i = n // ITEMS, n % ITEMS
                    if i % 4 == 0 and i < 8:
                        pe.wait_ge(q2T_copied, g * PAIRS + 2 * grp + i // 4 + 1)
                    if n >= 3:
                        pe.wait_ge(probs_ready, g * NI + n - 2)
                    for j, t, col, w in prob_item(i):
                        pe.matmul(psum[:, 3 + n % 3, col:col + w],
                                  stack_rows(kT, 4 * grp + j, ROWS_ALL, t * P, (t + 1) * P),
                                  stack_rows(qT, 4 * grp + j, ROWS_ALL, t * P, SEQ), start=True, stop=False)
                        ins = pe.matmul(psum[:, 3 + n % 3, col:col + P], const.ident_bf[:], const.mask_k[:],
                                        start=False, stop=True)
                    ins.then_inc(scores_ready, 1)

                def transpose_q2(grp, u):
                    pr = 2 * grp + u
                    if u == 0:
                        pe.wait_ge(max_ready, g * GROUPS + grp + 1)
                    if pr >= 1:
                        pe.wait_ge(q2T_copied, g * PAIRS + pr)
                    for t in range(TG):
                        ins = pe.transpose(psum[:, 6, t * P:(t + 1) * P],
                                           q_stack[:, t, 2 * pr:2 * pr + 2, :].rearrange("p a b -> p (a b)"),
                                           const.ident[:])
                    ins.then_inc(q2T_ready, 1)

                def weigh_values(grp):
                    pe.wait_ge(probs_ready, g * NI + (grp + 1) * ITEMS)
                    if grp >= 1:
                        pe.wait_ge(ctxT_copied, g * GROUPS + grp)
                    for kt in range(TG):
                        for j in range(4):
                            ins = pe.matmul(psum[VW * j:VW * (j + 1), 7, kt * P:SEQ], v[:, kt, 4 * grp + j, :],
                                            probs_of(grp, j, kt), start=(kt == 0), stop=(kt == TG - 1),
                                            tile_position=(0, VW * j))
                    ins.then_inc(ctxT_ready, 1)

                for i in range(ITEMS):
                    max_scores(i)
                pe.wait_ge(qT_ready, g * PAIRS + PAIRS)
                pe.wait_ge(kT_ready, g * PAIRS + PAIRS)
                for grp in range(GROUPS):
                    if grp >= 1:
                        weigh_values(grp - 1)
                    more = grp + 1 < GROUPS
                    transpose_q2(grp, 0)
                    if more:
                        max_scores((grp + 1) * ITEMS)
                        max_scores((grp + 1) * ITEMS + 1)
                    transpose_q2(grp, 1)
                    for i in range(ITEMS):
                        prob_scores(grp * ITEMS + i)
                        if more and i + 2 < ITEMS:
                            max_scores((grp + 1) * ITEMS + i + 2)
                weigh_values(GROUPS - 1)
                pe.wait_ge(max_scores_used, g * NI + NI)
                pe.wait_ge(ctxT_copied, g * GROUPS + GROUPS)
                for t in range(TG):
                    for q in range(GROUPS):
                        ins = pe.transpose(psum[:, t, q * P:(q + 1) * P], ctxT_raw[:, q, t * P:(t + 1) * P],
                                           const.ident[:])
                    ins.then_inc(ctx_ready, 1)
                pe.wait_ge(ctx_normed, g * TG + TG)
                for c in range(DC):
                    for t in range(TG):
                        ins = pe.transpose(psum[:, 4 + c, t * P:(t + 1) * P], ctx_n[:, t, c * P:(c + 1) * P],
                                           const.ident[:])
                    ins.then_inc(cT_ready, 1)
                pe.wait_ge(cT_lo_ready, g * DC + DC)
                for t in range(TG):
                    for c in range(DC):
                        tok = slice(t * P, (t + 1) * P)
                        ins = product3(pe, psum[:, 6 + t // 2, (t % 2) * D:(t % 2 + 1) * D],
                                       xT_hi[:, c, tok], xT_lo[:, c, tok], wo_hi[:, c, :], wo_lo[:, c, :],
                                       c == 0, c == DC - 1)
                    if t % 2:
                        ins.then_inc(proj_ready, 1)


def experts_stage(nc, tag, x, psum, const, w_all, w_router, router_bias, spec, NG, first=0, combine=None,
                  add_in=None, out_acc=None, store=None):
    E, SHARED, I, K, route = spec
    NE = w_all.shape[0]
    GU = 2 * I
    C = DC * GU + D
    with ExitStack() as ctx:
        mem = Pool_(nc, ctx, tag)
        w_hi, w_lo = (mem.sb(f"w_{s}", [P, NE * C], F32R) for s in ("hi", "lo"))
        w_raw = mem.sb("w_raw", [P, 2, C])
        stats6 = mem.sb("stats6", [P, TG, 6])
        mean_var = mem.sb("mean_var", [P, TG, 2])
        rstd = mem.sb("rstd", [P, TG])
        xn = mem.sb("xn", [P, TG, D])
        xT_hi, xT_lo = (mem.sb(f"xT_{s}", [P, DC, SEQ], F32R) for s in ("hi", "lo"))
        gate = mem.sb("gate", [P, 2, TG, I])
        hid = mem.sb("hid", [P, 2, TG, I])
        hT_hi, hT_lo = (mem.sb(f"hT_{s}", [P, 2, SEQ], F32R) for s in ("hi", "lo"))
        if route is not None:
            wr_raw = mem.sb("wr_raw", [P, DC, E])
            wr_hi, wr_lo = (mem.sb(f"wr_{s}", [P, DC, E], F32R) for s in ("hi", "lo"))
            bias_r = mem.sb("bias_r", [P, E])
            logits = mem.sb("logits", [P, TG, E])
            probs = mem.sb("probs", [P, TG, E])
            row = mem.sb("row", [P, TG])
            top = mem.sb("top", [P, TG, 8])
            cum = mem.sb("cum", [P, TG, 8])
            top_w = mem.sb("top_w", [P, TG, 8])
            top_i = mem.sb("top_i", [P, TG, 8], U32)
            top_if = mem.sb("top_if", [P, TG, 8])
            one_hot = mem.sb("one_hot", [P, TG, K, E])

        names = ("even_weights_in", "odd_weights_in", "router_in", "bias_in", "weights_hi", "weights_lo", "router_split", "var_ready",
                 "rstd_ready", "xn_ready", "xnT_ready", "xT_hi_ready", "xT_lo_ready", "logits_ready",
                 "logits_shifted", "exps_ready", "gate_up_ready", "gate_ready", "hid_ready", "hidT_ready",
                 "hT_hi_ready", "hT_lo_ready", "sum_ready", "sum_used", "group_done", "rows_stored")
        sem = {name: mem.sem(name) for name in names}
        weights_in = (sem["even_weights_in"], sem["odd_weights_in"])
        GUB, HB, YB = 0, 4, 6
        C_ALL = E + SHARED

        def x_rows(g, t):
            return x[:, bass.ds(g * (TG * D) + t * D, D)]

        block = ctx.enter_context(nc.Block())

        @block.sync
        def _(sp):
            if route is not None:
                sp.dma_start(wr_raw[:], w_router.rearrange("(c p) e -> p c e", p=P)).then_inc(sem["router_in"], 16)
                if router_bias is not None:
                    sp.dma_start(bias_r[:], router_bias.partition_broadcast(P)).then_inc(sem["bias_in"], 16)
            for e in range(NE):
                if e >= 2:
                    sp.wait_ge(sem["weights_lo"], e - 1)
                sp.dma_start(w_raw[:, e % 2, :], w_all[e]).then_inc(weights_in[e % 2], 16)
            if store is not None:
                with sp.Fori(0, NG) as g:
                    sp.wait_ge(sem["group_done"], g + 1)
                    sp.dma_start(store[bass.ds(g, 1)].rearrange("b (t p) d -> p (b t) d", p=P),
                                 x[:, bass.ds(g * (TG * D), TG * D)].rearrange("p (n d) -> p n d", d=D)
                                 ).then_inc(sem["rows_stored"], 16)
                sp.wait_ge(sem["rows_stored"], 16 * NG)

        @block.gpsimd
        def _(pool):
            with pool.Fori(0, NG) as g:
                pool.wait_ge(sem["var_ready"], g + 1)
                pool.tensor_tensor(rstd[:], mean_var[:, :, 1], const.minus_half[:, 0:TG],
                                   ALU.pow).then_inc(sem["rstd_ready"], 1)

        @block.scalar
        def _(act):
            if route is not None:
                act.wait_ge(sem["router_in"], 16)
                act.activation(wr_hi[:], wr_raw[:], ACT.Copy).then_inc(sem["router_split"], 1)
            for e in range(NE):
                act.wait_ge(weights_in[e % 2], 16 * (e // 2 + 1))
                act.activation(w_hi[:, e * C:(e + 1) * C], w_raw[:, e % 2, :], ACT.Copy).then_inc(sem["weights_hi"], 1)
            with act.Fori(0, NG) as g:
                for c in range(DC):
                    act.wait_ge(sem["xnT_ready"], g * DC + c + 1)
                    act.activation(xT_hi[:, c, :], psum[:, HB + c, :], ACT.Copy).then_inc(sem["xT_hi_ready"], 1)
                if route is not None:
                    act.wait_ge(sem["logits_shifted"], g + 1)
                    act.activation(probs[:], logits[:], ACT.Exp).then_inc(sem["exps_ready"], 1)

                def silu(n, b):
                    act.wait_ge(sem["gate_up_ready"], n + 1)
                    gu = psum[:, GUB + 2 * b:GUB + 2 * b + 2, :].rearrange("p a (u k) -> p (a u) k", u=2)
                    act.activation(gate[:, b], gu[:, :, 0:I], ACT.Silu).then_inc(sem["gate_ready"], 1)

                def hidden_hi(n, b):
                    act.wait_ge(sem["hidT_ready"], n + 1)
                    act.activation(hT_hi[0:I, b, :], psum[0:I, HB + b, :], ACT.Copy).then_inc(sem["hT_hi_ready"], 1)

                expert_loop(act, NE, g, None, lambda e, n, b: silu(n, b), lambda e, n, b: hidden_hi(n, b), None)

        @block.vector
        def _(dve):
            if route is not None:
                dve.wait_ge(sem["router_split"], 1)
                dve.tensor_tensor(wr_lo[:], wr_raw[:], wr_hi[:].bitcast(F32), ALU.subtract).then_inc(
                    sem["router_split"], 1)
                if SHARED:
                    dve.memset(combine[:, :, E:E + SHARED], 1.0)
                if router_bias is not None:
                    dve.wait_ge(sem["bias_in"], 16)
            for e in range(NE):
                dve.wait_ge(sem["weights_hi"], e + 1)
                dve.tensor_tensor(w_lo[:, e * C:(e + 1) * C], w_raw[:, e % 2, :],
                                  w_hi[:, e * C:(e + 1) * C].bitcast(F32), ALU.subtract).then_inc(sem["weights_lo"], 1)
            with dve.Fori(0, NG) as g:
                layernorm_vector(dve, lambda t: x_rows(g, t), stats6, mean_var, rstd, xn,
                                 sem["var_ready"], sem["rstd_ready"], sem["xn_ready"], g)
                for c in range(DC):
                    dve.wait_ge(sem["xT_hi_ready"], g * DC + c + 1)
                    dve.tensor_tensor(xT_lo[:, c, :], psum[:, HB + c, :], xT_hi[:, c, :].bitcast(F32),
                                      ALU.subtract).then_inc(sem["xT_lo_ready"], 1)
                if route is not None:
                    dve.wait_ge(sem["logits_ready"], g + 1)
                    raw = psum[:, GUB, 0:TG * E].rearrange("p (t e) -> p t e", t=TG)
                    if router_bias is not None:
                        dve.tensor_tensor(logits[:], raw, bias_r[:].unsqueeze(1).to_broadcast([P, TG, E]), ALU.add)
                    else:
                        dve.tensor_copy(logits[:], raw)
                    dve.drain()
                    dve.tensor_reduce(row[:], logits[:], X, ALU.max)
                    dve.drain()
                    dve.tensor_tensor(logits[:], logits[:], row[:].unsqueeze(2).to_broadcast([P, TG, E]),
                                      ALU.subtract).then_inc(sem["logits_shifted"], 1)
                    dve.wait_ge(sem["exps_ready"], g + 1)
                    dve.tensor_reduce(row[:], probs[:], X, ALU.add)
                    dve.drain()
                    dve.reciprocal(row[:], row[:])
                    dve.drain()
                    dve.tensor_tensor(probs[:], probs[:], row[:].unsqueeze(2).to_broadcast([P, TG, E]), ALU.mult)
                    dve.drain()
                    for t in range(TG):
                        dve.max(top[:, t, :], probs[:, t, :])
                    dve.drain()
                    for t in range(TG):
                        dve.max_index(top_i[:, t, :], top[:, t, :], probs[:, t, :])
                    route(dve, top, cum, top_w, row, const)
                    dve.drain()
                    dve.tensor_copy(top_if[:], top_i[:])
                    dve.drain()
                    ids = const.iota[:, 0:E].unsqueeze(1).unsqueeze(1).to_broadcast([P, TG, K, E])
                    dve.tensor_tensor(one_hot[:], ids, top_if[:, :, 0:K].unsqueeze(3).to_broadcast([P, TG, K, E]),
                                      ALU.is_equal)
                    dve.drain()
                    dve.tensor_tensor(one_hot[:], one_hot[:],
                                      top_w[:, :, 0:K].unsqueeze(3).to_broadcast([P, TG, K, E]), ALU.mult)
                    dve.drain()
                    dve.tensor_reduce(combine[:, bass.ds(g * TG, TG), 0:E],
                                      one_hot[:].rearrange("p t k e -> p t e k"), X, ALU.add)
                    dve.drain()

                def hidden(e, n, b):
                    dve.wait_ge(sem["gate_ready"], n + 1)
                    gu = psum[:, GUB + 2 * b:GUB + 2 * b + 2, :].rearrange("p a (u k) -> p (a u) k", u=2)
                    for t in range(TG):
                        weight = combine[:, bass.ds(g * TG + t, 1), bass.ds(e + first, 1)].rearrange("p a b -> p (a b)")
                        ins = dve.scalar_tensor_tensor(hid[:, b, t, :], gate[:, b, t, :], weight, gu[:, t, I:2 * I],
                                                       ALU.mult, ALU.mult)
                    ins.then_inc(sem["hid_ready"], 1)

                def hidden_lo(n, b):
                    dve.wait_ge(sem["hT_hi_ready"], n + 1)
                    dve.tensor_tensor(hT_lo[0:I, b, :], psum[0:I, HB + b, :], hT_hi[0:I, b, :].bitcast(F32),
                                      ALU.subtract).then_inc(sem["hT_lo_ready"], 1)

                expert_loop(dve, NE, g, None, hidden, lambda e, n, b: hidden_lo(n, b), None)
                dve.wait_ge(sem["sum_ready"], g + 1)
                rows = x[:, bass.ds(g * (TG * D), TG * D)]
                y = psum[:, YB:YB + 2, :].rearrange("p a b -> p (a b)")
                if out_acc is not None:
                    dve.tensor_copy(out_acc[:, bass.ds(g * (TG * D), TG * D)], y).then_inc(sem["sum_used"], 1)
                else:
                    dve.tensor_tensor(rows, rows, y, ALU.add).then_inc(sem["sum_used"], 1)
                    dve.drain()
                    if add_in is not None:
                        dve.tensor_tensor(rows, rows, add_in[:, bass.ds(g * (TG * D), TG * D)],
                                          ALU.add).then_inc(sem["group_done"], 1)
                        dve.drain()

        @block.tensor
        def _(pe):
            pe.wait_ge(sem["weights_lo"], NE)
            if route is not None:
                pe.wait_ge(sem["router_split"], 2)
            with pe.Fori(0, NG) as g:
                pe.wait_ge(sem["xn_ready"], g + 1)
                for c in range(DC):
                    for t in range(TG):
                        ins = pe.transpose(psum[:, HB + c, t * P:(t + 1) * P], xn[:, t, c * P:(c + 1) * P],
                                           const.ident[:])
                    ins.then_inc(sem["xnT_ready"], 1)
                pe.wait_ge(sem["xT_lo_ready"], g * DC + DC)
                if route is not None:
                    for t in range(TG):
                        for c in range(DC):
                            tok = slice(t * P, (t + 1) * P)
                            ins = product3(pe, psum[:, GUB, t * E:(t + 1) * E], xT_hi[:, c, tok], xT_lo[:, c, tok],
                                           wr_hi[:, c, :], wr_lo[:, c, :], c == 0, c == DC - 1)
                    ins.then_inc(sem["logits_ready"], 1)
                    pe.wait_ge(sem["exps_ready"], g + 1)

                def gate_up(e, n, b):
                    for t in range(TG):
                        for c in range(DC):
                            tok = slice(t * P, (t + 1) * P)
                            cols = bass.ds(e * C + c * GU, GU)
                            out = psum[:, GUB + 2 * b + t // 2, (t % 2) * (BANK // 2):(t % 2) * (BANK // 2) + GU]
                            ins = product3(pe, out, xT_hi[:, c, tok], xT_lo[:, c, tok], w_hi[:, cols], w_lo[:, cols],
                                           c == 0, c == DC - 1)
                    ins.then_inc(sem["gate_up_ready"], 1)

                def transpose_hidden(n, b):
                    pe.wait_ge(sem["hid_ready"], n + 1)
                    for t in range(TG):
                        ins = pe.transpose(psum[0:I, HB + b, t * P:(t + 1) * P], hid[:, b, t, :], const.ident[:])
                    ins.then_inc(sem["hidT_ready"], 1)

                def down(e, n, b, is_first, is_last):
                    pe.wait_ge(sem["hT_lo_ready"], n + 1)
                    cols = bass.ds(e * C + DC * GU, D)
                    for t in range(TG):
                        tok = slice(t * P, (t + 1) * P)
                        ins = product3(pe, psum[:, YB + t // 2, (t % 2) * D:(t % 2 + 1) * D],
                                       hT_hi[0:I, b, tok], hT_lo[0:I, b, tok], w_hi[0:I, cols], w_lo[0:I, cols],
                                       is_first and t % 2 == 0, is_last, shared_bank=True)
                    if is_last:
                        ins.then_inc(sem["sum_ready"], 1)

                expert_loop(pe, NE, g, gate_up, None, lambda e, n, b: transpose_hidden(n, b), down)


def expert_loop(eng, NE, g, ahead, now_a, now_b, behind):
    start = ahead or now_a

    def step(e, n, b, first=False, last=False):
        if not last:
            start(e + 1, n + 1, 1 - b)
        now_b(e, n, b)
        if behind and not first:
            behind(e - 1, n - 1, 1 - b, e_is(e, 1), False)

    def e_is(e, value):
        return isinstance(e, int) and e == value

    base = g * NE
    start(0, base, 0)
    step(0, base, 0, first=True)
    step(1, base + 1, 1)
    pairs = (NE - 3) // 2
    with eng.Fori(0, pairs) as i:
        step(i * 2 + 2, base + i * 2 + 2, 0)
        step(i * 2 + 3, base + i * 2 + 3, 1)
    for e in range(2 + 2 * pairs, NE):
        step(e, base + e, e % 2, last=(e == NE - 1))
    if behind:
        e = NE - 1
        behind(e, base + e, e % 2, False, True)


def top2_weights(dve, top, cum, top_w, row, const):
    dve.tensor_reduce(row[:], top[:, :, 0:2], X, ALU.add)
    dve.drain()
    dve.tensor_scalar(row[:], row[:], 1e-9, None, ALU.add)
    dve.drain()
    dve.reciprocal(row[:], row[:])
    dve.drain()
    dve.tensor_tensor(top_w[:, :, 0:2], top[:, :, 0:2], row[:].unsqueeze(2).to_broadcast([P, TG, 2]), ALU.mult)


def top8_weights(dve, top, cum, top_w, row, const):
    def normalise(dst, src):
        dve.tensor_reduce(row[:], src, X, ALU.add)
        dve.drain()
        dve.tensor_scalar(row[:], row[:], 1e-12, None, ALU.max)
        dve.drain()
        dve.reciprocal(row[:], row[:])
        dve.drain()
        dve.tensor_tensor(dst, src, row[:].unsqueeze(2).to_broadcast([P, TG, 8]), ALU.mult)
        dve.drain()

    normalise(top_w[:], top[:])
    for t in range(TG):
        dve.tensor_tensor_scan(cum[:, t, :], const.ones[:, 0:8], top_w[:, t, :], 0.0, ALU.mult, ALU.add)
    dve.drain()
    dve.scalar_tensor_tensor(top_w[:, :, 1:8], cum[:, :, 0:7], 0.8, top[:, :, 1:8], ALU.is_lt, ALU.mult)
    dve.tensor_copy(top_w[:, :, 0:1], top[:, :, 0:1])
    dve.drain()
    normalise(top_w[:], top_w[:])


class Const:
    pass


def two_layers(nc, x_in, wqkv0, wo0, bqkv0, bo0, w_router0, b_router0, w_experts0, wqkv1, wo1, bqkv1, bo1,
               w_router1, w_experts1, ident, mask_q, mask_k, alibi4, iota, out):
    E0, E1 = w_router0.shape[1], w_router1.shape[1]
    I0 = (w_experts0.shape[2] - D) // (2 * DC)
    I1 = (w_experts1.shape[2] - D) // (2 * DC)
    NG = x_in.shape[0]
    NT = NG * TG
    with ExitStack() as ctx:
        mem = Pool_(nc, ctx, "all")
        x = mem.sb("x", [P, NT * D])
        const = Const()
        const.ident = mem.sb("ident", [P, P])
        const.ident_bf = mem.sb("ident_bf", [P, P], BF16)
        const.mask_q = mem.sb("mask_q", [P, P], BF16)
        const.mask_k = mem.sb("mask_k", [P, P], BF16)
        const.minus_half = mem.sb("minus_half", [P, TG])
        const.ones = mem.sb("ones", [P, 8])
        const.iota = mem.sb("iota", [P, 32])
        alibi = mem.sb("alibi", [P, TG, H])
        psum = ctx.enter_context(nc.psum_tensor("psum", [P, 8, BANK], F32))

        with ExitStack() as first:
            mem0 = Pool_(nc, first, "load")
            masks = mem0.sb("masks", [P, 2, P])
            x_loaded = mem0.sem("x_loaded")
            consts_loaded = mem0.sem("consts_loaded")
            block = first.enter_context(nc.Block())

            @block.sync
            def _(sp):
                sp.dma_start(const.ident[:], ident).then_inc(consts_loaded, 16)
                sp.dma_start(const.iota[:], iota).then_inc(consts_loaded, 16)
                sp.dma_start(masks[:, 0, :], mask_q).then_inc(consts_loaded, 16)
                sp.dma_start(masks[:, 1, :], mask_k).then_inc(consts_loaded, 16)
                sp.dma_start(alibi[:], alibi4.rearrange("t p h -> p t h")).then_inc(consts_loaded, 16)
                sp.dma_start(x[:].rearrange("p (n d) -> p n d", d=D),
                             x_in.rearrange("b (t p) d -> p (b t) d", p=P)).then_inc(x_loaded, 16)
                sp.wait_ge(x_loaded, 16)

            @block.vector
            def _(dve):
                dve.memset(const.minus_half[:], -0.5)
                dve.memset(const.ones[:], 1.0)
                dve.wait_ge(consts_loaded, 80)
                dve.tensor_copy(const.ident_bf[:], const.ident[:])
                dve.tensor_copy(const.mask_q[:], masks[:, 0, :])
                dve.tensor_copy(const.mask_k[:], masks[:, 1, :])

        attention_stage(nc, "attn0", x, psum, const, wqkv0, wo0, bqkv0, bo0, alibi[:], NG)

        with ExitStack() as moe:
            mem2 = Pool_(nc, moe, "route0")
            combine = mem2.sb("combine", [P, NT, E0 + 1])
            experts_stage(nc, "moe0", x, psum, const, w_experts0, w_router0, b_router0,
                          (E0, 1, I0, 2, top2_weights), NG, combine=combine)

        attention_stage(nc, "attn1", x, psum, const, wqkv1, wo1, bqkv1, bo1, None, NG)

        with ExitStack() as moe:
            mem2 = Pool_(nc, moe, "route1")
            combine = mem2.sb("combine", [P, NT, E1])
            half_sum = mem2.sb("half_sum", [P, NT * D])
            experts_stage(nc, "moe1a", x, psum, const, w_experts1[0:E1 // 2], w_router1, None,
                          (E1, 0, I1, 8, top8_weights), NG, combine=combine, out_acc=half_sum)
            experts_stage(nc, "moe1b", x, psum, const, w_experts1[E1 // 2:E1], None, None,
                          (E1, 0, I1, 8, None), NG, first=E1 // 2, combine=combine, add_in=half_sum, store=out)


def laid_out(inputs):
    import numpy as np

    def experts(gate_up, down):
        n, d, gu = gate_up.shape
        out = np.zeros((n, P, DC * gu + d), gate_up.dtype)
        out[:, :, :DC * gu] = gate_up.reshape(n, DC, P, gu).transpose(0, 2, 1, 3).reshape(n, P, DC * gu)
        out[:, :down.shape[1], DC * gu:] = down
        return out

    a = {k: np.asarray(v) for k, v in inputs.items()}
    gu0 = np.concatenate([np.concatenate([a["L0_ffn_Wg"], a["L0_ffn_sWg"][None]], 0),
                          np.concatenate([a["L0_ffn_Wu"], a["L0_ffn_sWu"][None]], 0)], 2)
    dn0 = np.concatenate([a["L0_ffn_Wd"], a["L0_ffn_sWd"][None]], 0)
    i = np.arange(P)
    above = np.where(i[None, :] > i[:, None], np.float32(NEG), np.float32(0))
    slopes = np.float32(2.0 ** (-8.0 / H)) ** np.arange(1, H + 1, dtype=np.float32)
    distances = np.arange(1 - SEQ, 1, dtype=np.float32)
    alibi = (np.float32(HD) ** np.float32(0.5)) * slopes[None, :] * distances[:, None]
    return {
        "x_in": a["L0_attn_x"],
        "wqkv0": np.concatenate([a["L0_attn_Wq"], a["L0_attn_Wk"], a["L0_attn_Wv"]], 1),
        "wo0": a["L0_attn_Wo"],
        "bqkv0": np.concatenate([a["L0_attn_bq"], a["L0_attn_bk"], a["L0_attn_bv"]]),
        "bo0": a["L0_attn_bo"],
        "w_router0": a["L0_ffn_Wr"].T,
        "b_router0": a["L0_ffn_bias"],
        "w_experts0": experts(gu0, dn0),
        "wqkv1": a["L1_attn_W_attn"],
        "wo1": a["L1_attn_W_proj"],
        "bqkv1": a["L1_attn_b_attn"],
        "bo1": a["L1_attn_b_proj"],
        "w_router1": a["L1_ffn_gate_weight"].T,
        "w_experts1": experts(a["L1_ffn_gate_up_proj"].transpose(0, 2, 1), a["L1_ffn_down_proj"].transpose(0, 2, 1)),
        "ident": np.eye(P, dtype=np.float32),
        "mask_q": above,
        "mask_k": above.T,
        "alibi4": alibi.astype(np.float32).reshape(TG, P, H),
        "iota": np.broadcast_to(np.arange(32, dtype=np.float32), (P, 32)),
    }


def kernel(**inputs):
    import numpy as _np
    import concourse.bacc as _bacc
    from concourse.bass_utils import run_bass_kernel_spmd as _run

    nc = _bacc.Bacc("TRN2", target_bir_lowering=False, num_devices=1)
    arrays = {k: _np.ascontiguousarray(v) for k, v in laid_out(inputs).items()}
    args = {k: nc.dram_tensor(k, v.shape, mybir.dt.from_np(v.dtype), kind="ExternalInput").ap()
            for k, v in arrays.items()}
    shape = inputs["L0_attn_x"].shape
    out = nc.dram_tensor("out", shape, F32, kind="ExternalOutput").ap()
    two_layers(nc, **args, out=out)
    r = _run(nc, [arrays], core_ids=[0])
    return r.results[0]["out"]
```

```python
from contextlib import ExitStack

import concourse.bass as bass
from concourse import mybir

P = 128
F32 = mybir.dt.float32
F32R = mybir.dt.float32r
BF16 = mybir.dt.bfloat16
U32 = mybir.dt.uint32
ACT = mybir.ActivationFunctionType
ALU = mybir.AluOpType
X = mybir.AxisListType.X

EPS = 1e-5
D = 256
DC = D // P
H = 16
HD = D // H
SEQ = 512
TG = SEQ // P
BANK = 512
STACK = 64
ROWS_MAX = 50
ROWS_ALL = 52
VW = 32
NEG = -1e30
PACK = 4


class Pool_:

    def __init__(self, nc, ctx, tag):
        self.nc, self.ctx, self.tag, self.sems = nc, ctx, tag, []

    def sb(self, name, shape, dt=F32):
        return self.ctx.enter_context(self.nc.sbuf_tensor(f"{self.tag}_{name}", shape, dt))

    def sem(self, name):
        self.sems.append(self.ctx.enter_context(self.nc.semaphore(f"{self.tag}_{name}")))
        return self.sems[-1]

    def clear_sems(self):
        with self.nc.Block() as block:
            @block.gpsimd
            def _(pool):
                for sem in self.sems:
                    pool.sem_clear(sem)


def hold(pool, const, c=0):
    pool.tensor_tensor(const.tick[:, c + 1:c + 2], const.tick[:, 0:1], const.tick[:, 0:1], ALU.add)


def product3(pe, out, a_hi, a_lo, b_hi, b_lo, first, last, shared_bank=False):
    pe.matmul(out, a_hi, b_hi, start=first, stop=False, skip_group_check=shared_bank)
    pe.matmul(out, a_hi, b_lo, start=False, stop=False, skip_group_check=shared_bank)
    return pe.matmul(out, a_lo, b_hi, start=False, stop=last, skip_group_check=shared_bank)


def layernorm_vector(dve, x_rows, stats6, mean_var, rstd, xn, var_ready, rstd_ready, xn_ready, n):
    for t in range(TG):
        dve.bn_stats(stats6[:, t, :], x_rows(t))
    dve.drain()
    for t in range(TG):
        dve.bn_aggr(mean_var[:, t, :], stats6[:, t, :])
    dve.drain()
    dve.tensor_scalar(mean_var[:, :, 1], mean_var[:, :, 1], EPS, None, ALU.add).then_inc(var_ready, 1)
    dve.wait_ge(rstd_ready, n + 1)
    for t in range(TG):
        ins = dve.tensor_scalar(xn[:, t, :], x_rows(t), mean_var[:, t, 0:1], rstd[:, t:t + 1],
                                ALU.subtract, ALU.mult)
    ins.then_inc(xn_ready, 1)


def batch_jobs(first, last):
    jobs = []
    for grp in range(H // 4):
        if not last or grp < 2:
            jobs += [("stack", (grp + 2) % 4, 0), ("stack", (grp + 2) % 4, 1)]
        jobs += [("max", grp)]
        if grp == 1 and not last:
            jobs += [("rows",)] + [("qkv", t) for t in range(TG)]
        if grp == 1 and not first:
            jobs += [("ctx", 0), ("ctx", 1)]
        if grp == 2 and not first:
            jobs += [("ctxT",), ("proj",)]
    return jobs


AHEAD_JOBS = [("rows",)] + [("qkv", t) for t in range(TG)] + [("stack", grp, u) for grp in (0, 1) for u in (0, 1)]
TAIL_JOBS = [("ctx", 0), ("ctx", 1), ("ctxT",), ("proj",)]


def attention_stage(nc, tag, x, psum, const, wqkv, wo, bqkv, bo, alibi, NG):
    with ExitStack() as ctx:
        mem = Pool_(nc, ctx, tag)
        wqkv_hi, wqkv_lo = (mem.sb(f"wqkv_{s}", [P, DC, 3 * D], F32R) for s in ("hi", "lo"))
        wo_hi, wo_lo = (mem.sb(f"wo_{s}", [P, DC, D], F32R) for s in ("hi", "lo"))
        bias_qkv = mem.sb("bias_qkv", [P, 3 * D])
        bias_o = mem.sb("bias_o", [P, D])
        stats6 = mem.sb("stats6", [P, TG, 6])
        mean_var = mem.sb("mean_var", [P, TG, 2])
        rstd = mem.sb("rstd", [P, TG])
        xn = mem.sb("xn", [P, TG, D])
        xT_hi, xT_lo = (mem.sb(f"xT_{s}", [P, DC, SEQ], F32R) for s in ("hi", "lo"))
        qkv = mem.sb("qkv", [P, TG, 3 * D])
        q_stack = mem.sb("q_stack", [P, TG, H, STACK])
        k_stack = mem.sb("k_stack", [P, TG, H, STACK])
        qT = mem.sb("qT", [P, H // 2, SEQ], F32R)
        kT = mem.sb("kT", [P, H // 2, SEQ], F32R)
        v = mem.sb("v", [P, TG, H, VW])
        probs = mem.sb("probs", [P, 2, 10, BANK])
        neg_max = mem.sb("neg_max", [P, TG, H])
        ctxT_raw = mem.sb("ctxT_raw", [P, H // 4, SEQ])
        inv_sum = mem.sb("inv_sum", [P, TG, H])
        ctx_n = mem.sb("ctx_n", [P, TG, D])

        weights_in = mem.sem("weights_in")
        consts_in = mem.sem("consts_in")
        weights_split = mem.sem("weights_split")
        stack_const = mem.sem("stack_const")
        var_ready, rstd_ready, xn_ready = (mem.sem(s) for s in ("var_ready", "rstd_ready", "xn_ready"))
        work_ready = [mem.sem(f"work_ready{i}") for i in range(2)]
        work_read = [mem.sem(f"work_read{i}") for i in range(2)]
        xT_hi_ready = mem.sem("xT_hi_ready")
        stack_hi_ready = mem.sem("stack_hi_ready")
        stack_ready = mem.sem("stack_ready")
        max_scores_ready = mem.sem("max_scores_ready")
        max_scores_used = mem.sem("max_scores_used")
        max_ready = mem.sem("max_ready")
        scores_ready = mem.sem("scores_ready")
        probs_ready = mem.sem("probs_ready")
        v_copied = mem.sem("v_copied")
        ctxT_ready = mem.sem("ctxT_ready")
        ctxT_copied = mem.sem("ctxT_copied")
        cT_hi_ready = mem.sem("cT_hi_ready")
        x_biased = mem.sem("x_biased")

        raw_qkv = probs[:, 0, 0:3, :].rearrange("p a b -> p (a b)").rearrange("p (c n) -> p c n", c=DC)
        raw_o = probs[:, 0, 3, :].rearrange("p (c n) -> p c n", c=DC)
        GROUPS = H // 4
        ITEMS = 10
        NI = GROUPS * ITEMS
        WORK, MAXB, PROBB, CTXB = 0, 2, 4, 7

        def x_rows(b, t):
            return x[:, bass.ds(b * (TG * D) + t * D, D)]

        def job_number(b, job, first=False, last=False):
            before = len(AHEAD_JOBS)
            if not first:
                before = before + len(batch_jobs(True, False)) + (b - 1) * len(batch_jobs(False, False))
            return before + batch_jobs(first, last).index(job)

        def tail_number(job):
            return job_number(NG - 1, ("max", 3), last=True) + 1 + TAIL_JOBS.index(job)

        def max_item(i):
            if i >= 8:
                return [(i - 8, 1, 0, 2 * P), (i - 6, 1, 2 * P, 2 * P)]
            return [(i // 2, 3, 0, 4 * P)] if i % 2 == 0 else [(i // 2, 0, 0, P), (i // 2, 2, P, 3 * P)]

        def prob_item(i):
            if i >= 8:
                return [(i - 8, 2, 0, 2 * P), (i - 6, 2, 2 * P, 2 * P)]
            return [(i // 2, 0, 0, 4 * P)] if i % 2 == 0 else [(i // 2, 1, 0, 3 * P), (i // 2, 3, 3 * P, P)]

        def probs_of(grp, j, kt):
            item, col = {0: (2 * j, 0), 1: (2 * j + 1, 0), 3: (2 * j + 1, 3 * P),
                         2: (8 + j % 2, j // 2 * 2 * P)}[kt]
            return probs[:, grp % 2, item, col:col + SEQ - kt * P]

        def heads(rows, grp, width=HD):
            return rows[:, :, grp * 4 * width:(grp + 1) * 4 * width].rearrange("p t (h d) -> p t h d", h=4)

        def over_batches(eng, part):
            part(0, True, False)
            with eng.Fori(1, NG - 1) as b:
                part(b, False, False)
            part(NG - 1, False, True)

        ctx.callback(mem.clear_sems)
        block = ctx.enter_context(nc.Block())

        @block.sync
        def _(sp):
            sp.dma_start(raw_qkv, wqkv.rearrange("(c p) n -> p c n", p=P)).then_inc(weights_in, 16)
            sp.dma_start(raw_o, wo.rearrange("(c p) n -> p c n", p=P)).then_inc(weights_in, 16)
            sp.dma_start(bias_qkv[:], bqkv.partition_broadcast(P)).then_inc(consts_in, 16)
            sp.dma_start(bias_o[:], bo.partition_broadcast(P)).then_inc(consts_in, 16)

        @block.gpsimd
        def _(pool):
            pool.memset(q_stack[:], 0.0)
            pool.memset(k_stack[:], 0.0)
            pool.memset(v[:], 0.0)
            pool.drain()
            pool.memset(q_stack[:, :, :, 48:50], 1.0)
            pool.memset(k_stack[:, :, :, 50:52], 1.0)
            pool.memset(v[:, :, :, HD:HD + 1], 1.0).then_inc(stack_const, 1)
            pool.wait_ge(consts_in, 32)

            def power(b):
                pool.wait_ge(var_ready, b + 1)
                pool.tensor_tensor(rstd[:], mean_var[:, :, 1], const.minus_half[:, 0:TG],
                                   ALU.pow).then_inc(rstd_ready, 1)

            def add_bias(b):
                pool.wait_ge(xn_ready, b + 1)
                for t in range(TG):
                    ins = pool.tensor_tensor(x_rows(b, t), x_rows(b, t), bias_o[:], ALU.add)
                ins.then_inc(x_biased, 1)

            def complete_stacks(G, grp):
                pool.wait_ge(stack_hi_ready, G + 1)
                for t in range(TG):
                    hs = slice(4 * grp, 4 * grp + 4)
                    one = const.ones[:, 0:1].unsqueeze(2).to_broadcast([P, 4, HD])
                    q_rows, k_rows = (heads(qkv[:, :, c:c + D], grp)[:, t] for c in (0, D))
                    pool.tensor_tensor(q_stack[:, t, hs, 32:48], q_stack[:, t, hs, 0:16], one, ALU.mult)
                    pool.tensor_tensor(k_stack[:, t, hs, 16:32], k_stack[:, t, hs, 0:16], one, ALU.mult)
                    pool.tensor_tensor(q_stack[:, t, hs, 16:32].bitcast(F32R), q_rows, q_stack[:, t, hs, 0:16],
                                       ALU.subtract)
                    ins = pool.tensor_tensor(k_stack[:, t, hs, 32:48].bitcast(F32R), k_rows,
                                             k_stack[:, t, hs, 0:16], ALU.subtract)
                ins.then_inc(stack_ready, 1)

            power(0)
            add_bias(0)
            for grp in range(3):
                complete_stacks(grp, grp)

            def batch(b, first, last):
                for grp in range(GROUPS):
                    G = b * GROUPS + grp
                    if grp == 0 and not last:
                        power(b + 1)
                    if grp == 1 and not last:
                        add_bias(b + 1)
                    if not (last and grp >= 1):
                        complete_stacks(G + 3, (grp + 3) % GROUPS)

            over_batches(pool, batch)

        @block.scalar
        def _(act):
            act.wait_ge(weights_in, 32)
            act.activation(wqkv_hi[:], raw_qkv, ACT.Copy)
            act.activation(wo_hi[:], raw_o, ACT.Copy).then_inc(weights_split, 1)
            act.wait_ge(stack_const, 1)

            def transposed_hi(n, count, done):
                for c in range(DC):
                    act.wait_ge(work_ready[c], n + 1)
                    act.activation(xT_hi[:, c, :], psum[:, WORK + c, :], ACT.Copy).then_inc(done, 1)

            def split_hi(G, grp, n_qkv=None):
                if n_qkv is not None:
                    act.wait_ge(work_read[1], n_qkv + 1)
                hs = slice(4 * grp, 4 * grp + 4)
                act.activation(q_stack[:, :, hs, 0:16].bitcast(F32R), heads(qkv[:, :, 0:D], grp), ACT.Copy)
                act.activation(k_stack[:, :, hs, 0:16].bitcast(F32R), heads(qkv[:, :, D:2 * D], grp),
                               ACT.Copy).then_inc(stack_hi_ready, 1)

            def copy_stacks(n, pair):
                for u, stackT in enumerate((qT, kT)):
                    act.wait_ge(work_ready[u], n + 1)
                    act.activation(stackT[:, pair, :], psum[:, WORK + u, :], ACT.Copy).then_inc(work_read[u], 1)

            def copy_ctxT(G, grp):
                act.wait_ge(ctxT_ready, G + 1)
                act.activation(ctxT_raw[:, grp, :], psum[:, CTXB, :], ACT.Copy).then_inc(ctxT_copied, 1)

            def copy_values(b):
                act.activation(v[:, :, :, 0:HD], qkv[:, :, 2 * D:3 * D].rearrange("p t (h d) -> p t h d", h=H),
                               ACT.Copy).then_inc(v_copied, 1)

            transposed_hi(0, 0, xT_hi_ready)
            for grp in range(3):
                split_hi(grp, grp, AHEAD_JOBS.index(("qkv", 3)))
            for grp in range(2):
                for u in range(2):
                    copy_stacks(AHEAD_JOBS.index(("stack", grp, u)), 2 * grp + u)

            def batch(b, first, last):
                def number(*job):
                    return job_number(b, job, first, last)

                for grp in range(GROUPS):
                    G = b * GROUPS + grp
                    if not last or grp < 2:
                        for u in range(2):
                            copy_stacks(number("stack", (grp + 2) % 4, u), 2 * ((grp + 2) % 4) + u)
                    if not (first and grp < 2):
                        copy_ctxT(G - 2, (grp - 2) % GROUPS)
                    for u in range(2):
                        act.wait_ge(work_ready[u], number("max", grp) + 1)
                        act.activation(qT[:, 2 * grp + u, :], psum[:, WORK + u, :], ACT.Copy).then_inc(work_read[u], 1)
                    for i in range(ITEMS):
                        n = grp * ITEMS + i
                        act.wait_ge(scores_ready, b * NI + n + 1)
                        act.activation(probs[:, grp % 2, i, :], psum[:, PROBB + n % 3, :], ACT.Exp,
                                       scale=float(HD) ** -0.5).then_inc(probs_ready, 1)
                        if grp == 1 and i == 0:
                            if not last:
                                transposed_hi(number("rows"), 0, xT_hi_ready)
                            copy_values(b)
                        if grp == 2 and i == 3 and not first:
                            transposed_hi(number("ctxT"), 0, cT_hi_ready)
                        if i == (7 if grp == 1 else 0) and not (last and grp >= 1):
                            split_hi(G + 3, (grp + 3) % GROUPS, number("qkv", 3) if grp == 1 else None)

            over_batches(act, batch)
            for k in (2, 1):
                copy_ctxT(NG * GROUPS - k, GROUPS - k)
            transposed_hi(tail_number(("ctxT",)), 0, cT_hi_ready)

        @block.vector
        def _(dve):
            dve.wait_ge(weights_split, 1)
            dve.tensor_tensor(wqkv_lo[:], raw_qkv, wqkv_hi[:].bitcast(F32), ALU.subtract)
            dve.tensor_tensor(wo_lo[:], raw_o, wo_hi[:].bitcast(F32), ALU.subtract).then_inc(weights_split, 1)
            dve.wait_ge(consts_in, 32)
            dve.wait_ge(stack_const, 1)
            if alibi is not None:
                dve.tensor_copy(k_stack[:, :, :, 48].bitcast(F32R), alibi)
                dve.drain()
                dve.tensor_tensor(k_stack[:, :, :, 49].bitcast(F32R), alibi, k_stack[:, :, :, 48], ALU.subtract)

            def row_stats(b):
                for t in range(TG):
                    dve.bn_stats(stats6[:, t, :], x_rows(b, t))
                dve.drain()
                for t in range(TG):
                    dve.bn_aggr(mean_var[:, t, :], stats6[:, t, :])
                dve.drain()
                dve.tensor_scalar(mean_var[:, :, 1], mean_var[:, :, 1], EPS, None, ALU.add).then_inc(var_ready, 1)

            def normalise(b):
                dve.wait_ge(rstd_ready, b + 1)
                for t in range(TG):
                    ins = dve.tensor_scalar(xn[:, t, :], x_rows(b, t), mean_var[:, t, 0:1], rstd[:, t:t + 1],
                                            ALU.subtract, ALU.mult)
                ins.then_inc(xn_ready, 1)

            def transposed_lo(hi_ready, n_hi):
                for c in range(DC):
                    dve.wait_ge(hi_ready, n_hi + c + 1)
                    dve.tensor_tensor(xT_lo[:, c, :], psum[:, WORK + c, :], xT_hi[:, c, :].bitcast(F32),
                                      ALU.subtract).then_inc(work_read[c], 1)

            def copy_qkv(n, t):
                dve.wait_ge(work_ready[0], n + 1)
                dve.tensor_tensor(qkv[:, t, 0:2 * D], psum[:, WORK, :], bias_qkv[:, 0:2 * D],
                                  ALU.add).then_inc(work_read[0], 1)
                dve.wait_ge(work_ready[1], n + 1)
                dve.tensor_tensor(qkv[:, t, 2 * D:3 * D], psum[:, WORK + 1, 0:D], bias_qkv[:, 2 * D:3 * D],
                                  ALU.add).then_inc(work_read[1], 1)

            def row_maxima(b, G, grp, i):
                dve.wait_ge(max_scores_ready, G * ITEMS + i + 1)
                bank = psum[:, MAXB + i % 2, :]
                if i >= 8:
                    ins = dve.tensor_reduce(neg_max[:, 1, 4 * grp + i - 8:4 * grp + i - 5:2],
                                            bank.rearrange("p (a k) -> p a k", a=2), X, ALU.max, negate=True)
                else:
                    for j, t, col, w in max_item(i):
                        head = 4 * grp + j
                        ins = dve.tensor_reduce(neg_max[:, t, head:head + 1], bank[:, col:col + w], X, ALU.max,
                                                negate=True)
                ins.then_inc(max_scores_used, 1)

            def stack_maxima(grp):
                dve.drain()
                cols = slice(4 * grp, 4 * grp + 4)
                dve.tensor_copy(q_stack[:, :, cols, 50].bitcast(F32R), neg_max[:, :, cols])
                dve.drain()
                dve.tensor_tensor(q_stack[:, :, cols, 51].bitcast(F32R), neg_max[:, :, cols],
                                  q_stack[:, :, cols, 50], ALU.subtract).then_inc(max_ready, 1)

            def norm_contexts(n, half):
                for u in range(2):
                    dve.wait_ge(work_ready[u], n + 1)
                    dve.reciprocal(inv_sum[:, 2 * half + u, :], psum[:, WORK + u, HD:BANK:VW])
                dve.drain()
                for u in range(2):
                    t = 2 * half + u
                    dve.tensor_tensor(ctx_n[:, t, :].rearrange("p (h d) -> p h d", h=H),
                                      psum[:, WORK + u, :].rearrange("p (h d) -> p h d", h=H)[:, :, 0:HD],
                                      inv_sum[:, t, :].unsqueeze(2).to_broadcast([P, H, HD]),
                                      ALU.mult).then_inc(work_read[u], 1)

            def add_projection(b, n):
                dve.wait_ge(x_biased, b + 1)
                for u in range(2):
                    dve.wait_ge(work_ready[u], n + 1)
                    rows = x[:, bass.ds(b * (TG * D) + 2 * u * D, 2 * D)]
                    dve.tensor_tensor(rows, rows, psum[:, WORK + u, :], ALU.add).then_inc(work_read[u], 1)

            row_stats(0)
            normalise(0)
            transposed_lo(xT_hi_ready, 0)
            for t in range(TG):
                copy_qkv(AHEAD_JOBS.index(("qkv", t)), t)
            for i in range(ITEMS):
                row_maxima(0, 0, 0, i)
            stack_maxima(0)

            def batch(b, first, last):
                def number(*job):
                    return job_number(b, job, first, last)

                for grp in range(GROUPS):
                    G = b * GROUPS + grp
                    nxt = (grp + 1) % GROUPS
                    if grp == 0 and not last:
                        row_stats(b + 1)
                    for i in range(ITEMS):
                        if not (last and grp == 3):
                            row_maxima(b, G + 1, nxt, i)
                        if grp == 1 and not last:
                            if i == 1:
                                transposed_lo(xT_hi_ready, (b + 1) * DC)
                                dve.wait_ge(v_copied, b + 1)
                            if i in (2, 3, 4, 5):
                                copy_qkv(number("qkv", i - 2), i - 2)
                        if grp == 2 and not first:
                            if i == 4:
                                transposed_lo(cT_hi_ready, (b - 1) * DC)
                            if i == 7:
                                add_projection(b - 1, number("proj"))
                    if not (last and grp == 3):
                        stack_maxima(nxt)
                    if grp == 1 and not first:
                        norm_contexts(number("ctx", 0), 0)
                        norm_contexts(number("ctx", 1), 1)
                    if grp == 0 and not last:
                        normalise(b + 1)

            over_batches(dve, batch)
            for half in range(2):
                norm_contexts(tail_number(("ctx", half)), half)
            transposed_lo(cT_hi_ready, (NG - 1) * DC)
            add_projection(NG - 1, tail_number(("proj",)))

        @block.tensor
        def _(pe):
            pe.wait_ge(weights_split, 2)

            def bank_free(c, n):
                pe.wait_ge(work_read[c], n)

            def transpose_rows(rows, n):
                if not isinstance(n, int) or n > 0:
                    bank_free(0, n)
                    bank_free(1, n)
                for c in range(DC):
                    for t in range(TG):
                        ins = pe.transpose(psum[:, WORK + c, t * P:(t + 1) * P], rows[:, t, c * P:(c + 1) * P],
                                           const.ident[:])
                    ins.then_inc(work_ready[c], 1)

            def make_qkv(n, t):
                for u, c0, c1 in ((0, 0, 2 * D), (1, 2 * D, 3 * D)):
                    bank_free(u, n)
                    for c in range(DC):
                        if t == 0 and u == 0 and c == 1:
                            bank_free(1, n)
                        tok = slice(t * P, (t + 1) * P)
                        ins = product3(pe, psum[:, WORK + u, 0:c1 - c0], xT_hi[:, c, tok], xT_lo[:, c, tok],
                                       wqkv_hi[:, c, c0:c1], wqkv_lo[:, c, c0:c1], c == 0, c == DC - 1)
                    ins.then_inc(work_ready[u], 1)

            def transpose_pair(stack, bank, pair, n):
                bank_free(bank, n)
                for t in range(TG):
                    ins = pe.transpose(psum[:, WORK + bank, t * P:(t + 1) * P],
                                       stack[:, t, 2 * pair:2 * pair + 2, :].rearrange("p a b -> p (a b)"),
                                       const.ident[:])
                ins.then_inc(work_ready[bank], 1)

            def transpose_stacks(G, grp, u, n):
                if u == 0:
                    pe.wait_ge(stack_ready, G + 1)
                transpose_pair(q_stack, 0, 2 * grp + u, n)
                transpose_pair(k_stack, 1, 2 * grp + u, n)

            def transpose_maxima(G, grp, n):
                pe.wait_ge(max_ready, G + 1)
                for u in range(2):
                    transpose_pair(q_stack, u, 2 * grp + u, n)

            def stack_rows(sT, head, rows, c0, c1):
                row = STACK * (head % 2)
                return sT[row:row + rows, head // 2, c0:c1]

            def add_mask(bank, blocks, half_of_rows, rows, part, whole):
                at = slice(half_of_rows * (P // 2), (half_of_rows + 1) * (P // 2))
                step = blocks[-1] - blocks[0] if len(blocks) > 1 else P
                some, full = (1, 0) if part[0] else (0, 1)
                for n, (h, (c0, c1)) in enumerate(((some, part), (full, whole))):
                    src = rows[at, h, c0:c1].unsqueeze(1).to_broadcast([P // 2, len(blocks), c1 - c0])
                    out = bank[:, blocks[0]:blocks[0] + (len(blocks) - 1) * step + P]
                    if len(blocks) > 1:
                        out = bass_blocks(bank, blocks, c0, c1)
                    else:
                        src, out = rows[at, h, c0:c1], bank[:, blocks[0] + c0:blocks[0] + c1]
                    pe.matmul(out, const.mask_sel[at, h, :], src, start=(n == 0), stop=False,
                              skip_group_check=True)

            def bass_blocks(bank, blocks, c0, c1):
                first, second = (c // P for c in blocks)
                return bank.rearrange("p (n c) -> p n c", c=P)[:, first:second + 1:second - first, c0:c1]

            def max_scores(G, grp, i):
                if not isinstance(G, int) or G > 0 or i >= 2:
                    pe.wait_ge(max_scores_used, G * ITEMS + i - 1)
                pieces = max_item(i)
                bank = psum[:, MAXB + i % 2, :]
                add_mask(bank, [col + w - P for _, _, col, w in pieces], pieces[0][0] % 2, const.mask_rows,
                         (P // 2, P), (0, P))
                for j, t, col, w in pieces:
                    head = 4 * grp + j
                    ins = pe.matmul(bank[:, col:col + w], stack_rows(qT, head, ROWS_MAX, t * P, (t + 1) * P),
                                    stack_rows(kT, head, ROWS_MAX, 0, w), start=False, stop=True,
                                    skip_group_check=True)
                ins.then_inc(max_scores_ready, 1)

            def prob_scores(b, grp, i, first):
                n = grp * ITEMS + i
                if n >= 3:
                    pe.wait_ge(probs_ready, b * NI + n - 2)
                elif not first:
                    pe.wait_ge(probs_ready, b * NI - (0, 2, 1)[n])
                pieces = prob_item(i)
                bank = psum[:, PROBB + n % 3, :]
                add_mask(bank, [col for _, _, col, _ in pieces], pieces[0][0] % 2, const.mask_rowsT,
                         (0, P // 2), (0, P))
                for j, t, col, w in pieces:
                    head = 4 * grp + j
                    ins = pe.matmul(bank[:, col:col + w], stack_rows(kT, head, ROWS_ALL, t * P, (t + 1) * P),
                                    stack_rows(qT, head, ROWS_ALL, t * P, SEQ), start=False, stop=True,
                                    skip_group_check=True)
                ins.then_inc(scores_ready, 1)

            def weigh_values(b, G, grp, key_tiles):
                if key_tiles[0] == 0:
                    values_free(b, G)
                for kt in key_tiles:
                    for j in range(4):
                        ins = pe.matmul(psum[VW * j:VW * (j + 1), CTXB, kt * P:SEQ], v[:, kt, 4 * grp + j, :],
                                        probs_of(grp, j, kt), start=(kt == 0), stop=(kt == TG - 1),
                                        tile_position=(0, VW * j))
                if key_tiles[-1] == TG - 1:
                    ins.then_inc(ctxT_ready, 1)

            def values_free(b, G):
                pe.wait_ge(probs_ready, (G + 1) * ITEMS)
                pe.wait_ge(v_copied, b + 1)
                if not isinstance(G, int) or G > 0:
                    pe.wait_ge(ctxT_copied, G)

            def transpose_contexts(n, half, G_last):
                pe.wait_ge(ctxT_copied, G_last + 1)
                for u in range(2):
                    bank_free(u, n)
                    t = 2 * half + u
                    for q in range(GROUPS):
                        ins = pe.transpose(psum[:, WORK + u, q * P:(q + 1) * P], ctxT_raw[:, q, t * P:(t + 1) * P],
                                           const.ident[:])
                    ins.then_inc(work_ready[u], 1)

            def project(n):
                for u in range(2):
                    bank_free(0, n)
                    bank_free(1, n)
                    for t in (2 * u, 2 * u + 1):
                        for c in range(DC):
                            tok = slice(t * P, (t + 1) * P)
                            ins = product3(pe, psum[:, WORK + u, (t % 2) * D:(t % 2 + 1) * D],
                                           xT_hi[:, c, tok], xT_lo[:, c, tok], wo_hi[:, c, :], wo_lo[:, c, :],
                                           c == 0, c == DC - 1)
                    ins.then_inc(work_ready[u], 1)

            pe.wait_ge(xn_ready, 1)
            transpose_rows(xn, 0)
            for t in range(TG):
                make_qkv(AHEAD_JOBS.index(("qkv", t)), t)
            for grp in range(2):
                for u in range(2):
                    transpose_stacks(grp, grp, u, AHEAD_JOBS.index(("stack", grp, u)))
            for c in range(2):
                bank_free(c, AHEAD_JOBS.index(("stack", 0, 1)) + 1)
            for i in range(ITEMS):
                max_scores(0, 0, i)

            def batch(b, first, last):
                def number(*job):
                    return job_number(b, job, first, last)

                for grp in range(GROUPS):
                    G = b * GROUPS + grp
                    nxt = (grp + 1) % GROUPS
                    weigh = not (first and grp < 2)
                    values = (b if grp >= 2 else b - 1, G - 2, (grp - 2) % GROUPS)
                    ahead = not last or grp < 2
                    if ahead:
                        transpose_stacks(G + 2, (grp + 2) % 4, 0, number("stack", (grp + 2) % 4, 0))
                    if weigh:
                        weigh_values(*values, (0,))
                    if ahead:
                        transpose_stacks(G + 2, (grp + 2) % 4, 1, number("stack", (grp + 2) % 4, 1))
                    if weigh:
                        weigh_values(*values, (1, 2, 3))
                    transpose_maxima(G, grp, number("max", grp))
                    if not (last and grp == 3):
                        max_scores(G + 1, nxt, 0)
                    for i in range(ITEMS):
                        if i + 1 < ITEMS and not (last and grp == 3):
                            max_scores(G + 1, nxt, i + 1)
                        if i == 0:
                            for c in range(2):
                                bank_free(c, number("max", grp) + 1)
                        prob_scores(b, grp, i, first)
                        if grp == 1 and not last:
                            if i == 0:
                                pe.wait_ge(xn_ready, b + 2)
                                transpose_rows(xn, number("rows"))
                            if i in (1, 2, 3, 4):
                                make_qkv(number("qkv", i - 1), i - 1)
                        if grp == 1 and not first and i in (8, 9):
                            transpose_contexts(number("ctx", i - 8), i - 8, b * GROUPS - 1)
                        if grp == 2 and not first:
                            if i == 3:
                                transpose_rows(ctx_n, number("ctxT"))
                            if i == 6:
                                project(number("proj"))

            over_batches(pe, batch)
            for k in (2, 1):
                weigh_values(NG - 1, NG * GROUPS - k, GROUPS - k, (0, 1, 2, 3))
            for half in range(2):
                transpose_contexts(tail_number(("ctx", half)), half, NG * GROUPS - 1)
            transpose_rows(ctx_n, tail_number(("ctxT",)))
            project(tail_number(("proj",)))


def slot_tiles(tokens, experts, k, step):
    need = tokens * k // P + experts - 1
    return -(-need // step) * step


def round_tiles(k):
    return 8 if k <= 4 else 4


def route_stage(nc, tag, x, psum, const, w_all, w_router, router_bias, spec, NG, keep):
    E, SHARED, I, K, weights_of = spec
    NT = NG * TG
    NS = keep.NS
    NC = -(-NS // P)
    GU = 2 * I
    C = DC * GU + D
    NE = E + SHARED
    TB = round_tiles(K)
    split = keep.w_hi is not None
    with ExitStack() as ctx:
        mem = Pool_(nc, ctx, tag)
        w_raw = mem.sb("w_raw", [P, 2, C]) if split else None
        stats6 = mem.sb("stats6", [P, TG, 6])
        mean_var = mem.sb("mean_var", [P, TG, 2])
        rstd = mem.sb("rstd", [P, TG])
        xn = mem.sb("xn", [P, TG, D])
        xT_hi, xT_lo = (mem.sb(f"xT_{s}", [P, DC, SEQ], F32R) for s in ("hi", "lo"))
        if SHARED:
            gate = mem.sb("gate", [P, TG, I])
            hid = mem.sb("hid", [P, TG, I])
            hT_hi, hT_lo = (mem.sb(f"hT_{s}", [P, SEQ], F32R) for s in ("hi", "lo"))
        wr_raw = mem.sb("wr_raw", [P, DC, E])
        wr_hi, wr_lo = (mem.sb(f"wr_{s}", [P, DC, E], F32R) for s in ("hi", "lo"))
        bias_r = mem.sb("bias_r", [P, E])
        logits = mem.sb("logits", [P, NT, E])
        probs = mem.sb("probs", [P, NT, E])
        row = mem.sb("row", [P, NT])
        top = mem.sb("top", [P, NT, 8])
        cum = mem.sb("cum", [P, NT, 8])
        probs_g = mem.sb("probs_g", [P, TG, E])
        top_g = mem.sb("top_g", [P, TG, 8])
        top_ig = mem.sb("top_ig", [P, TG, 8], U32)
        top_if = mem.sb("top_if", [P, NT, 8])
        one_hot = mem.sb("one_hot", [P, max(NT * K * E, NS * E)])
        chosen = mem.sb("chosen", [P, NT, E], BF16)
        totals = mem.sb("totals", [P, E, NT])
        running = mem.sb("running", [P, E, NT])
        slots = mem.sb("slots", [P, NT, E])
        ones = mem.sb("ones", [P, E * NT])
        counts = mem.sb("counts", [P, E])
        over = mem.sb("over", [P, E, NT])
        n_tiles = mem.sb("n_tiles", [P, E])
        tile_end = mem.sb("tile_end", [P, E])
        shift = mem.sb("shift", [P, E])
        expert_f, packed_f = (mem.sb(name, [P, NS]) for name in ("expert_f", "packed_f"))
        slot_f = mem.sb("slot_f", [P, NT, K])
        zeros = mem.sb("zeros", [P, P])
        slot_cols = mem.sb("slot_cols", [P, 2, TB * K], U32)
        id_cols = mem.sb("id_cols", [P, 2, TB])
        tokens_of = mem.sb("tokens_of", [P, NC, P])

        names = ("even_weights_in", "odd_weights_in", "router_in", "bias_in", "weights_hi", "weights_lo", "router_split",
                 "var_ready", "rstd_ready", "xn_ready", "rows_kept", "xnT_ready", "xT_hi_ready", "xT_lo_ready",
                 "logits_ready", "logits_taken", "logits_shifted", "exps_ready", "gate_up_ready", "gate_ready",
                 "hid_ready", "hidT_ready", "hT_hi_ready", "hT_lo_ready", "y_ready", "y_added", "chosen_ready",
                 "counts_ready", "slots_ready", "zeros_ready", "list_cleared", "list_in", "listT_ready")
        sem = {name: mem.sem(name) for name in names}
        scattered = keep.dma_sems.scattered
        weights_in = (sem["even_weights_in"], sem["odd_weights_in"])
        LB, GUB, HB, YB, RB = 0, 1, 4, 6, 2
        last_first = [NE - 1] + list(range(NE - 1)) if SHARED else list(range(NE))
        NR = -(-NT * E // BANK)

        def x_rows(g, t):
            return x[:, bass.ds(g * (TG * D) + t * D, D)]

        def split_weights(eng, lo, numbers):
            for n in numbers:
                e = last_first[n]
                cols = slice(e * C, (e + 1) * C)
                if lo:
                    eng.wait_ge(sem["weights_hi"], n + 1)
                    eng.tensor_tensor(keep.w_lo[:, cols], w_raw[:, n % 2, :], keep.w_hi[:, cols].bitcast(F32),
                                      ALU.subtract).then_inc(sem["weights_lo"], 1)
                else:
                    eng.wait_ge(weights_in[n % 2], 16 * (n // 2 + 1))
                    eng.activation(keep.w_hi[:, cols], w_raw[:, n % 2, :], ACT.Copy).then_inc(sem["weights_hi"], 1)

        ctx.callback(mem.clear_sems)
        block = ctx.enter_context(nc.Block())

        @block.sync
        def _(sp):
            sp.dma_start(wr_raw[:], w_router.rearrange("(c p) e -> p c e", p=P)).then_inc(sem["router_in"], 16)
            if router_bias is not None:
                sp.dma_start(bias_r[:], router_bias.partition_broadcast(P)).then_inc(sem["bias_in"], 16)
            if split:
                sp.dma_start(w_raw[:, 0, :], w_all[last_first[0]]).then_inc(weights_in[0], 16)
                sp.dma_start(w_raw[:, 1, :], w_all[last_first[1]]).then_inc(weights_in[1], 16)
            sp.wait_ge(sem["zeros_ready"], 1)
            for c in range(NC):
                n = min(P, NS - c * P)
                sp.dma_start(keep.slot_list[c * P * P:(c * P + n) * P].rearrange("(n s) o -> n (s o)", s=P),
                             zeros[0:n, :]).then_inc(sem["list_cleared"], 16)
            with sp.Fori(0, NG) as g:
                sp.wait_ge(sem["xn_ready"], g + 1)
                sp.dma_start(keep.xn_rows[bass.ds(g, 1)].rearrange("b (t p) d -> p (b t) d", p=P),
                             xn[:]).then_inc(sem["rows_kept"], 16)
            if split:
                for n in range(2, NE):
                    sp.wait_ge(sem["weights_lo"], n - 1)
                    sp.dma_start(w_raw[:, n % 2, :], w_all[last_first[n]]).then_inc(weights_in[n % 2], 16)
            else:
                sp.dma_start(keep.w_raw[:].rearrange("p (e c) -> p e c", c=C),
                             w_all.rearrange("e p c -> p e c")).then_inc(weights_in[0], 16)
            for b in range(2):
                sp.wait_ge(scattered[b], 8 * NT * K)
            for c in range(NC):
                n = min(P, NS - c * P)
                sp.dma_start(tokens_of[0:n, c, :],
                             keep.slot_list[c * P * P:(c * P + n) * P].rearrange("(n s) o -> n (s o)", s=P)
                             ).then_inc(sem["list_in"], 16)
            sp.wait_ge(sem["rows_kept"], 16 * NG)
            if not split:
                sp.wait_ge(weights_in[0], 16)

        @block.gpsimd
        def _(pool):
            with pool.Fori(0, NG) as g:
                pool.wait_ge(sem["var_ready"], g + 1)
                pool.tensor_tensor(rstd[:], mean_var[:, :, 1], const.minus_half[:, 0:TG],
                                   ALU.pow).then_inc(sem["rstd_ready"], 1)
            pool.wait_ge(sem["slots_ready"], 1)
            pool.wait_ge(sem["list_cleared"], 16 * NC)

            def one_round(i, b):
                pool.tensor_copy(slot_cols[:, b, :], keep.slot_u[:, bass.ds(i * (TB * K), TB * K)])
                pool.tensor_copy(id_cols[:, b, :], const.token_id[:, bass.ds(i * TB, TB)])
                pool.drain()
                for t in range(TB):
                    for k in range(K):
                        c = t * K + k
                        pool.indirect_dma_start(keep.slot_list, bass.IndirectOffsetOnAxis(slot_cols[:, b, c:c + 1], 0),
                                                id_cols[:, b, t:t + 1], None).then_inc(scattered[b], 16)

            one_round(0, 0)
            one_round(1, 1)
            with pool.Fori(1, NT // TB // 2) as i:
                for b in range(2):
                    pool.wait_ge(scattered[b], i * (16 * TB * K))
                    hold(pool, const)
                    one_round(i * 2 + b, b)

        @block.scalar
        def _(act):
            act.wait_ge(sem["router_in"], 16)
            act.activation(wr_hi[:], wr_raw[:], ACT.Copy).then_inc(sem["router_split"], 1)
            if split:
                split_weights(act, False, range(2))
            with act.Fori(0, NG) as g:
                for c in range(DC):
                    act.wait_ge(sem["xnT_ready"], g * DC + c + 1)
                    act.activation(xT_hi[:, c, :], psum[:, HB + c, :], ACT.Copy).then_inc(sem["xT_hi_ready"], 1)
                if SHARED:
                    act.wait_ge(sem["gate_up_ready"], g + 1)
                    gu = psum[:, GUB:GUB + 2, :].rearrange("p a (u k) -> p (a u) k", u=2)
                    act.activation(gate[:], gu[:, :, 0:I], ACT.Silu).then_inc(sem["gate_ready"], 1)
                    act.wait_ge(sem["hidT_ready"], g + 1)
                    act.activation(hT_hi[0:I, :], psum[0:I, HB, :], ACT.Copy).then_inc(sem["hT_hi_ready"], 1)
            act.wait_ge(sem["logits_shifted"], 1)
            act.activation(probs[:], logits[:], ACT.Exp).then_inc(sem["exps_ready"], 1)
            if split:
                split_weights(act, False, range(2, NE))

        @block.vector
        def _(dve):
            dve.memset(zeros[:], 0.0).then_inc(sem["zeros_ready"], 1)
            dve.memset(ones[:], 1.0)
            dve.wait_ge(sem["router_split"], 1)
            dve.tensor_tensor(wr_lo[:], wr_raw[:], wr_hi[:].bitcast(F32), ALU.subtract).then_inc(sem["router_split"], 1)
            if router_bias is not None:
                dve.wait_ge(sem["bias_in"], 16)

            def normalise(g):
                if not (isinstance(g, int) and g == 0):
                    dve.wait_ge(sem["rows_kept"], g * 16)
                layernorm_vector(dve, lambda t: x_rows(g, t), stats6, mean_var, rstd, xn,
                                 sem["var_ready"], sem["rstd_ready"], sem["xn_ready"], g)

            def group(g, last):
                for c in range(DC):
                    dve.wait_ge(sem["xT_hi_ready"], g * DC + c + 1)
                    dve.tensor_tensor(xT_lo[:, c, :], psum[:, HB + c, :], xT_hi[:, c, :].bitcast(F32),
                                      ALU.subtract).then_inc(sem["xT_lo_ready"], 1)
                if not last:
                    normalise(g + 1)
                dve.wait_ge(sem["logits_ready"], g + 1)
                raw = psum[:, LB, 0:TG * E].rearrange("p (t e) -> p t e", t=TG)
                mine = logits[:, bass.ds(g * TG, TG), :]
                if router_bias is not None:
                    dve.tensor_tensor(mine, raw, bias_r[:].unsqueeze(1).to_broadcast([P, TG, E]),
                                      ALU.add).then_inc(sem["logits_taken"], 1)
                else:
                    dve.tensor_copy(mine, raw).then_inc(sem["logits_taken"], 1)
                if SHARED:
                    dve.wait_ge(sem["gate_ready"], g + 1)
                    gu = psum[:, GUB:GUB + 2, :].rearrange("p a (u k) -> p (a u) k", u=2)
                    dve.tensor_tensor(hid[:], gate[:], gu[:, :, I:2 * I], ALU.mult).then_inc(sem["hid_ready"], 1)
                    dve.wait_ge(sem["hT_hi_ready"], g + 1)
                    dve.tensor_tensor(hT_lo[0:I, :], psum[0:I, HB, :], hT_hi[0:I, :].bitcast(F32),
                                      ALU.subtract).then_inc(sem["hT_lo_ready"], 1)
                    dve.wait_ge(sem["y_ready"], g + 1)
                    rows = x[:, bass.ds(g * (TG * D), TG * D)]
                    dve.tensor_tensor(rows, rows, psum[:, YB:YB + 2, :].rearrange("p a b -> p (a b)"),
                                      ALU.add).then_inc(sem["y_added"], 1)

            if split:
                split_weights(dve, True, range(2))
            normalise(0)
            with dve.Fori(0, NG - 1) as g:
                group(g, False)
            group(NG - 1, True)

            dve.drain()
            dve.tensor_reduce(row[:], logits[:], X, ALU.max)
            dve.drain()
            dve.tensor_tensor(logits[:], logits[:], row[:].unsqueeze(2).to_broadcast([P, NT, E]),
                              ALU.subtract).then_inc(sem["logits_shifted"], 1)
            dve.wait_ge(sem["exps_ready"], 1)
            dve.tensor_reduce(row[:], probs[:], X, ALU.add)
            dve.drain()
            dve.reciprocal(row[:], row[:])
            dve.drain()
            dve.tensor_tensor(probs[:], probs[:], row[:].unsqueeze(2).to_broadcast([P, NT, E]), ALU.mult)
            dve.drain()
            with dve.Fori(0, NG) as g:
                tiles = bass.ds(g * TG, TG)
                dve.tensor_copy(probs_g[:], probs[:, tiles, :])
                dve.drain()
                for t in range(TG):
                    dve.max(top_g[:, t, :], probs_g[:, t, :])
                dve.drain()
                for t in range(TG):
                    dve.max_index(top_ig[:, t, :], top_g[:, t, :], probs_g[:, t, :])
                dve.tensor_copy(top[:, tiles, :], top_g[:])
                dve.drain()
                dve.tensor_copy(top_if[:, tiles, :], top_ig[:])
                dve.drain()
            choices = one_hot[:, 0:NT * K * E].rearrange("p (t k e) -> p t k e", t=NT, k=K)
            dve.tensor_tensor(choices, const.iota[:, 0:E].unsqueeze(1).unsqueeze(1).to_broadcast([P, NT, K, E]),
                              top_if[:, :, 0:K].unsqueeze(3).to_broadcast([P, NT, K, E]), ALU.is_equal)
            dve.drain()
            dve.tensor_reduce(slots[:], choices.rearrange("p t k e -> p t e k"), X, ALU.add)
            dve.drain()
            dve.tensor_copy(chosen[:], slots[:]).then_inc(sem["chosen_ready"], 1)
            weights_of(dve, top, cum, keep.top_w, row, ones, NT)

            dve.wait_ge(sem["counts_ready"], 1)
            dve.tensor_copy(totals[:], psum[:, RB + NR:RB + 2 * NR, :].rearrange("p a b -> p (a b)")[:, 0:NT * E]
                            .rearrange("p (t e) -> p e t", e=E))
            dve.drain()
            dve.tensor_tensor_scan(running[:].rearrange("p e t -> p (e t)"), ones[:],
                                   totals[:].rearrange("p e t -> p (e t)"), 0.0, ALU.mult, ALU.add)
            dve.tensor_reduce(counts[:], totals[:], X, ALU.add)
            dve.drain()
            dve.tensor_tensor(running[:], running[:], totals[:], ALU.subtract)
            dve.tensor_tensor(over[:], counts[:].unsqueeze(2).to_broadcast([P, E, NT]),
                              const.slot_steps[:, 0:NT].unsqueeze(1).to_broadcast([P, E, NT]), ALU.is_gt)
            dve.drain()
            dve.tensor_reduce(n_tiles[:], over[:], X, ALU.add)
            dve.drain()
            dve.tensor_tensor_scan(tile_end[:], ones[:, 0:E], n_tiles[:], 0.0, ALU.mult, ALU.add)
            dve.drain()
            dve.tensor_tensor(shift[:], tile_end[:], n_tiles[:], ALU.subtract)
            dve.drain()
            dve.scalar_tensor_tensor(shift[:], shift[:], float(P), running[:, :, 0], ALU.mult, ALU.subtract)
            dve.drain()
            dve.tensor_tensor(running[:], running[:], shift[:].unsqueeze(2).to_broadcast([P, E, NT]), ALU.add)
            dve.drain()
            dve.tensor_tensor(slots[:], psum[:, RB:RB + NR, :].rearrange("p a b -> p (a b)")[:, 0:NT * E]
                              .rearrange("p (t e) -> p t e", e=E), running[:].rearrange("p e t -> p t e"), ALU.add)
            dve.drain()
            for k in range(K):
                dve.tensor_tensor(choices[:, :, k, :], choices[:, :, k, :], slots[:], ALU.mult)
            dve.drain()
            dve.tensor_reduce(slot_f[:], choices, X, ALU.add)
            dve.drain()
            dve.tensor_copy(keep.slot_u[:], slot_f[:].rearrange("p t k -> p (t k)")).then_inc(sem["slots_ready"], 1)
            ends = one_hot[:, 0:NS * E].rearrange("p (n e) -> p n e", e=E)
            dve.tensor_tensor(ends, const.tile_no[:, 0:NS].unsqueeze(2).to_broadcast([P, NS, E]),
                              tile_end[:].unsqueeze(1).to_broadcast([P, NS, E]), ALU.is_ge)
            dve.drain()
            dve.tensor_reduce(expert_f[:], ends, X, ALU.add)
            dve.drain()
            dve.tensor_scalar(expert_f[:], expert_f[:], float(E - 1), None, ALU.min)
            dve.drain()
            dve.tensor_copy(packed_f[:], expert_f[:])
            for m in range(1, PACK):
                dve.drain()
                dve.scalar_tensor_tensor(packed_f[:, 0:NS - m], expert_f[:, m:NS], float(E ** m),
                                         packed_f[:, 0:NS - m], ALU.mult, ALU.add)
            dve.drain()
            dve.tensor_copy(keep.experts_u[:], packed_f[:])
            if split:
                split_weights(dve, True, range(2, NE))
            dve.wait_ge(sem["listT_ready"], NC)
            dve.tensor_copy(keep.token_u[:], psum[:, GUB, 0:NS])

        @block.tensor
        def _(pe):
            pe.wait_ge(sem["router_split"], 2)
            if SHARED:
                pe.wait_ge(sem["weights_lo"], 1)

            def group(g, first):
                pe.wait_ge(sem["xn_ready"], g + 1)
                for c in range(DC):
                    for t in range(TG):
                        ins = pe.transpose(psum[:, HB + c, t * P:(t + 1) * P], xn[:, t, c * P:(c + 1) * P],
                                           const.ident[:])
                    ins.then_inc(sem["xnT_ready"], 1)
                pe.wait_ge(sem["xT_lo_ready"], g * DC + DC)
                if not first:
                    pe.wait_ge(sem["logits_taken"], g)
                for t in range(TG):
                    tok = slice(t * P, (t + 1) * P)
                    for c in range(DC):
                        ins = product3(pe, psum[:, LB, t * E:(t + 1) * E], xT_hi[:, c, tok], xT_lo[:, c, tok],
                                       wr_hi[:, c, :], wr_lo[:, c, :], c == 0, c == DC - 1)
                ins.then_inc(sem["logits_ready"], 1)
                if not SHARED:
                    return
                base = E * C
                for t in range(TG):
                    tok = slice(t * P, (t + 1) * P)
                    for c in range(DC):
                        cols = slice(base + c * GU, base + (c + 1) * GU)
                        ins = product3(pe, psum[:, GUB + t // 2, (t % 2) * (BANK // 2):(t % 2) * (BANK // 2) + GU],
                                       xT_hi[:, c, tok], xT_lo[:, c, tok], keep.w_hi[:, cols], keep.w_lo[:, cols],
                                       c == 0, c == DC - 1)
                ins.then_inc(sem["gate_up_ready"], 1)
                pe.wait_ge(sem["hid_ready"], g + 1)
                for t in range(TG):
                    ins = pe.transpose(psum[0:I, HB, t * P:(t + 1) * P], hid[:, t, :], const.ident[:])
                ins.then_inc(sem["hidT_ready"], 1)
                pe.wait_ge(sem["hT_lo_ready"], g + 1)
                if not first:
                    pe.wait_ge(sem["y_added"], g)
                cols = slice(base + DC * GU, base + C)
                for t in range(TG):
                    tok = slice(t * P, (t + 1) * P)
                    ins = product3(pe, psum[:, YB + t // 2, (t % 2) * D:(t % 2 + 1) * D], hT_hi[0:I, tok],
                                   hT_lo[0:I, tok], keep.w_hi[0:I, cols], keep.w_lo[0:I, cols], True, True)
                ins.then_inc(sem["y_ready"], 1)

            group(0, True)
            with pe.Fori(1, NG) as g:
                group(g, False)
            pe.wait_ge(sem["chosen_ready"], 1)
            for r in range(NR):
                n = min(BANK, NT * E - r * BANK)
                marks = chosen[:].rearrange("p t e -> p (t e)")[:, r * BANK:r * BANK + n]
                pe.matmul(psum[:, RB + r, 0:n], const.before[:], marks, start=True, stop=True)
                ins = pe.matmul(psum[:, RB + NR + r, 0:n], const.all_ones[:], marks, start=True, stop=True)
            ins.then_inc(sem["counts_ready"], 1)
            pe.wait_ge(sem["list_in"], 16 * NC)
            for c in range(NC):
                n = min(P, NS - c * P)
                pe.transpose(psum[:, GUB, c * P:c * P + n], tokens_of[0:n, c, :],
                             const.ident[0:n, 0:n]).then_inc(sem["listT_ready"], 1)


def slot_stage(nc, tag, psum, const, spec, keep):
    E, SHARED, I, K, _ = spec
    NS = keep.NS
    GU = 2 * I
    C = DC * GU + D
    ROUND = 8
    RING = 4
    split = keep.w_hi is None
    with ExitStack() as ctx:
        mem = Pool_(nc, ctx, tag)
        xg = mem.sb("xg", [P, ROUND, D])
        xT_hi, xT_lo = (mem.sb(f"xT_{s}", [P, RING, D], F32R) for s in ("hi", "lo"))
        gate = mem.sb("gate", [P, RING, I])
        hid = mem.sb("hid", [P, RING, I])
        hT_hi, hT_lo = (mem.sb(f"hT_{s}", [P, RING, P], F32R) for s in ("hi", "lo"))
        y = mem.sb("y", [P, RING, D])
        token_cols = mem.sb("token_cols", [P, 2 * ROUND], U32)
        if split:
            wt_hi, wt_lo = (mem.sb(f"wt_{s}", [P, ROUND, C], F32R) for s in ("hi", "lo"))
        names = ("rows_transposed", "xT_hi_ready", "xT_lo_ready", "gate_up_ready", "gate_ready", "hid_ready",
                 "hidT_ready", "hT_hi_ready", "hT_lo_ready", "y_ready", "y_copied", "wt_hi_ready", "wt_lo_ready")
        sem = {name: mem.sem(name) for name in names}
        gathered = keep.dma_sems.rows_gathered
        stored = [mem.sem(f"stored{j}") for j in range(RING)]

        def ring_of_psum(first_bank, width):
            return lambda n: psum[:, first_bank + n % 2, 0:width]

        rowsT_ps, gate_up_ps = ring_of_psum(0, D), ring_of_psum(2, GU)
        hidT_ps, y_ps = ring_of_psum(4, P), ring_of_psum(6, D)

        def steps(eng, before, step, load):
            before()
            for r in (0, ROUND):
                load(r)
                for j in range(ROUND):
                    step(r + j, j)
            with eng.Fori(2, NS // ROUND - 1) as i:
                load(i * ROUND)
                for j in range(ROUND):
                    step(i * ROUND + j, j)
            load(NS - ROUND)
            for j in range(ROUND):
                step(NS - ROUND + j, j)

        def experts_from(eng, n):
            word = eng.value_load(keep.experts_u[0:1, bass.ds(n, 1)])
            return [eng.snap((word // E ** m) % E) for m in range(PACK)]

        def at_least(n, value):
            return not isinstance(n, int) or n >= value

        def at_most(n, value):
            return not isinstance(n, int) or n <= value

        def weight_experts(eng, expert, r):
            expert.update(zip(range(5, 9), experts_from(eng, r + 5)))
            if at_most(r, NS - 2 * ROUND):
                expert.update(zip(range(9, 13), experts_from(eng, r + 9)))

        ctx.callback(mem.clear_sems)
        block = ctx.enter_context(nc.Block())

        @block.sync
        def _(sp):
            with sp.Fori(0, NS // RING) as i:
                for j in range(RING):
                    sp.wait_ge(sem["y_copied"], i * RING + j + 1)
                    sp.dma_start(keep.y_rows[bass.ds(i * RING + j, 1)].rearrange("o p d -> p (o d)"),
                                 y[:, j, :]).then_inc(stored[j], 16)
            for j in range(RING):
                sp.wait_ge(stored[j], 16 * (NS // RING))

        @block.gpsimd
        def _(pool):
            def two_rounds(i, first):
                for half in range(2):
                    base = i * (2 * ROUND) + half * ROUND
                    if not first:
                        pool.wait_ge(sem["rows_transposed"], base - ROUND)
                        hold(pool, const, half * (ROUND + 1))
                    pool.tensor_copy(token_cols[:, half * ROUND:(half + 1) * ROUND],
                                     keep.token_u[:, bass.ds(base, ROUND)])
                    pool.drain()
                    for j in range(ROUND):
                        if not (first and half == 0):
                            pool.wait_ge(sem["rows_transposed"], base + j - ROUND + 1)
                            hold(pool, const, half * (ROUND + 1) + 1 + j)
                        c = half * ROUND + j
                        pool.indirect_dma_start(xg[:, j, :], None, keep.xn_flat,
                                                bass.IndirectOffsetOnAxis(token_cols[:, c:c + 1], 0)
                                                ).then_inc(gathered[j], 16)

            two_rounds(0, True)
            with pool.Fori(1, NS // (2 * ROUND)) as i:
                two_rounds(i, False)

        @block.scalar
        def _(act):
            def rows_hi(n, j):
                act.wait_ge(sem["rows_transposed"], n + 1)
                act.activation(xT_hi[:, j % RING, :], rowsT_ps(j), ACT.Copy).then_inc(sem["xT_hi_ready"], 1)

            expert = {}

            def load(r):
                if split:
                    weight_experts(act, expert, r)

            def weights_hi(n, j, e):
                act.activation(wt_hi[:, j, :], keep.w_raw[:, bass.ds(e * C, C)],
                               ACT.Copy).then_inc(sem["wt_hi_ready"], 1)

            def silu(n, j):
                act.wait_ge(sem["gate_up_ready"], n + 1)
                act.activation(gate[:, j % RING, :], gate_up_ps(j)[:, 0:I], ACT.Silu).then_inc(sem["gate_ready"], 1)

            def hidden_hi(n, j):
                act.wait_ge(sem["hidT_ready"], n + 1)
                act.activation(hT_hi[0:I, j % RING, :], hidT_ps(j)[0:I], ACT.Copy).then_inc(sem["hT_hi_ready"], 1)

            def copy_y(n, j):
                act.wait_ge(sem["y_ready"], n + 1)
                if at_least(n, RING):
                    act.wait_ge(stored[j % RING], (n - j % RING) * (16 // RING))
                act.activation(y[:, j % RING, :], y_ps(j), ACT.Copy).then_inc(sem["y_copied"], 1)

            def before():
                if split:
                    for j, e in enumerate(experts_from(act, 0) + experts_from(act, 4)[0:1]):
                        weights_hi(j, j, e)
                for n in range(4):
                    rows_hi(n, n)
                silu(0, 0)
                silu(1, 1)

            def step(n, j):
                if at_most(n, NS - 5):
                    rows_hi(n + 4, (j + 4) % ROUND)
                if at_most(n, NS - 3):
                    silu(n + 2, (j + 2) % ROUND)
                hidden_hi(n, j)
                if at_least(n, 3):
                    copy_y(n - 3, (j - 3) % ROUND)
                if split and at_most(n, NS - 6):
                    weights_hi(n + 5, (j + 5) % ROUND, expert[j + 5])

            steps(act, before, step, load)
            for n in range(NS - 3, NS):
                copy_y(n, n % ROUND)

        @block.vector
        def _(dve):
            def rows_lo(n, j):
                dve.wait_ge(sem["xT_hi_ready"], n + 1)
                dve.tensor_tensor(xT_lo[:, j % RING, :], rowsT_ps(j), xT_hi[:, j % RING, :].bitcast(F32),
                                  ALU.subtract).then_inc(sem["xT_lo_ready"], 1)

            expert = {}

            def load(r):
                if split:
                    weight_experts(dve, expert, r)

            def weights_lo(n, j, e):
                dve.wait_ge(sem["wt_hi_ready"], n + 1)
                dve.tensor_tensor(wt_lo[:, j, :], keep.w_raw[:, bass.ds(e * C, C)], wt_hi[:, j, :].bitcast(F32),
                                  ALU.subtract).then_inc(sem["wt_lo_ready"], 1)

            def hidden(n, j):
                dve.wait_ge(sem["gate_ready"], n + 1)
                dve.tensor_tensor(hid[:, j % RING, :], gate[:, j % RING, :], gate_up_ps(j)[:, I:2 * I],
                                  ALU.mult).then_inc(sem["hid_ready"], 1)

            def hidden_lo(n, j):
                dve.wait_ge(sem["hT_hi_ready"], n + 1)
                dve.tensor_tensor(hT_lo[0:I, j % RING, :], hidT_ps(j)[0:I], hT_hi[0:I, j % RING, :].bitcast(F32),
                                  ALU.subtract).then_inc(sem["hT_lo_ready"], 1)

            def before():
                if split:
                    for j, e in enumerate(experts_from(dve, 0) + experts_from(dve, 4)[0:1]):
                        weights_lo(j, j, e)
                for n in range(4):
                    rows_lo(n, n)
                hidden(0, 0)
                hidden(1, 1)

            def step(n, j):
                if at_most(n, NS - 5):
                    rows_lo(n + 4, (j + 4) % ROUND)
                if at_most(n, NS - 3):
                    hidden(n + 2, (j + 2) % ROUND)
                hidden_lo(n, j)
                if split and at_most(n, NS - 6):
                    weights_lo(n + 5, (j + 5) % ROUND, expert[j + 5])

            steps(dve, before, step, load)

        @block.tensor
        def _(pe):
            expert = {}

            def load(r):
                if split:
                    return
                if at_least(r, 1):
                    expert.update(zip(range(-2, 2), experts_from(pe, r - 2)))
                else:
                    expert.update(zip(range(0, 4), experts_from(pe, 0)))
                expert.update(zip(range(2, 6), experts_from(pe, r + 2)))
                expert.update(zip(range(6, 10), experts_from(pe, r + 6)))

            def weights(e, j, first, last):
                if split:
                    return wt_hi[:, j, first:last], wt_lo[:, j, first:last]
                cols = bass.ds(e * C + first, last - first)
                return keep.w_hi[:, cols], keep.w_lo[:, cols]

            def transpose_rows(n, j):
                pe.wait_ge(gathered[j], (n - j) * (16 // ROUND) + 16)
                if at_least(n, 2):
                    pe.wait_ge(sem["xT_lo_ready"], n - 1)
                for c in range(DC):
                    ins = pe.transpose(rowsT_ps(j)[:, c * P:(c + 1) * P], xg[:, j, c * P:(c + 1) * P],
                                       const.ident[:])
                ins.then_inc(sem["rows_transposed"], 1)

            def gate_up(n, j, e):
                pe.wait_ge(sem["xT_lo_ready"], n + 1)
                if split:
                    pe.wait_ge(sem["wt_lo_ready"], n + 1)
                if at_least(n, 2):
                    pe.wait_ge(sem["hid_ready"], n - 1)
                hi, lo = weights(e, j, 0, DC * GU)
                for c in range(DC):
                    part = slice(c * P, (c + 1) * P)
                    cols = slice(c * GU, (c + 1) * GU)
                    ins = product3(pe, gate_up_ps(j), xT_hi[:, j % RING, part], xT_lo[:, j % RING, part],
                                   hi[:, cols], lo[:, cols], c == 0, c == DC - 1)
                ins.then_inc(sem["gate_up_ready"], 1)

            def transpose_hidden(n, j):
                pe.wait_ge(sem["hid_ready"], n + 1)
                if at_least(n, 2):
                    pe.wait_ge(sem["hT_lo_ready"], n - 1)
                pe.transpose(hidT_ps(j)[0:I], hid[:, j % RING, :], const.ident[:]).then_inc(sem["hidT_ready"], 1)

            def down(n, j, e):
                pe.wait_ge(sem["hT_lo_ready"], n + 1)
                if at_least(n, 2):
                    pe.wait_ge(sem["y_copied"], n - 1)
                hi, lo = weights(e, j, DC * GU, C)
                product3(pe, y_ps(j), hT_hi[0:I, j % RING, :], hT_lo[0:I, j % RING, :],
                         hi[0:I], lo[0:I], True, True).then_inc(sem["y_ready"], 1)

            def before():
                for n in range(4):
                    transpose_rows(n, n)
                first = [None] * 2 if split else experts_from(pe, 0)
                for n in range(2):
                    gate_up(n, n, first[n])

            def step(n, j):
                if at_most(n, NS - 5):
                    transpose_rows(n + 4, (j + 4) % ROUND)
                if at_most(n, NS - 3):
                    gate_up(n + 2, (j + 2) % ROUND, expert.get(j + 2))
                transpose_hidden(n, j)
                if at_least(n, 2):
                    down(n - 2, (j - 2) % ROUND, expert.get(j - 2))

            steps(pe, before, step, load)
            for j in (ROUND - 2, ROUND - 1):
                down(NS - ROUND + j, j, expert.get(j))


def gather_stage(nc, tag, x, const, spec, NG, keep, store=None):
    K = spec[3]
    NT = NG * TG
    TB = round_tiles(K)
    COLS = TB * K
    with ExitStack() as ctx:
        mem = Pool_(nc, ctx, tag)
        yg = mem.sb("yg", [P, 2, COLS, D])
        slot_cols = mem.sb("slot_cols", [P, 2, COLS], U32)
        gathered = keep.dma_sems.y_gathered
        added, rows_stored = mem.sem("added"), mem.sem("rows_stored")
        ctx.callback(mem.clear_sems)
        block = ctx.enter_context(nc.Block())

        @block.gpsimd
        def _(pool):
            def one_round(i, b):
                pool.tensor_copy(slot_cols[:, b, :], keep.slot_u[:, bass.ds(i * COLS, COLS)])
                pool.drain()
                for c in range(COLS):
                    pool.indirect_dma_start(yg[:, b, c, :], None, keep.y_flat,
                                            bass.IndirectOffsetOnAxis(slot_cols[:, b, c:c + 1], 0)
                                            ).then_inc(gathered[c], 16)

            one_round(0, 0)
            one_round(1, 1)
            with pool.Fori(1, NT // TB // 2) as i:
                for b in range(2):
                    pool.wait_ge(added, i * 2 + b - 1)
                    hold(pool, const)
                    one_round(i * 2 + b, b)

        @block.vector
        def _(dve):
            with dve.Fori(0, NT // TB // 2) as i:
                for b in range(2):
                    for k in range(K):
                        for t in range(TB):
                            dve.wait_ge(gathered[t * K + k], i * 32 + 16 * (b + 1))
                            tile = i * (2 * TB) + (b * TB + t)
                            rows = x[:, bass.ds(tile * D, D)]
                            weight = keep.top_w[:, bass.ds(tile, 1), k:k + 1].rearrange("p a b -> p (a b)")
                            ins = dve.scalar_tensor_tensor(rows, yg[:, b, t * K + k, :], weight, rows,
                                                           ALU.mult, ALU.add)
                        if k < K - 1:
                            dve.drain()
                    ins.then_inc(added, 1)

        if store is not None:
            out_rounds = store.rearrange("b (r s) d -> (b r) s d", s=TB * P)

            @block.sync
            def _(sp):
                with sp.Fori(0, NT // TB) as i:
                    sp.wait_ge(added, i + 1)
                    sp.dma_start(out_rounds[bass.ds(i, 1)].rearrange("b (t p) d -> p (b t) d", p=P),
                                 x[:, bass.ds(i * (TB * D), TB * D)].rearrange("p (n d) -> p n d", d=D)
                                 ).then_inc(rows_stored, 16)
                sp.wait_ge(rows_stored, 16 * (NT // TB))


class GatherSems:

    def __init__(self, nc, ctx, tag, K):
        mem = Pool_(nc, ctx, tag)
        self.scattered = [mem.sem(f"{s}_rounds_scattered") for s in ("even", "odd")]
        self.rows_gathered = [mem.sem(f"rows_gathered{j}") for j in range(8)]
        self.y_gathered = [mem.sem(f"y_gathered{c}") for c in range(round_tiles(K) * K)]


class Kept:

    def __init__(self, nc, ctx, tag, spec, NG, resident, dma_sems):
        self.dma_sems = dma_sems
        E, SHARED, I, K, _ = spec
        mem = Pool_(nc, ctx, tag)
        NT, C = NG * TG, DC * 2 * I + D
        self.NS = NS = slot_tiles(NT * P, E, K, 16)
        self.w_hi = self.w_lo = self.w_raw = None
        if resident:
            self.w_hi, self.w_lo = (mem.sb(f"w_{s}", [P, (E + SHARED) * C], F32R) for s in ("hi", "lo"))
        else:
            self.w_raw = mem.sb("w_raw", [P, E * C])
        self.top_w = mem.sb("top_w", [P, NT, 8])
        self.slot_u = mem.sb("slot_u", [P, NT * K], U32)
        self.token_u = mem.sb("token_u", [P, NS], U32)
        self.experts_u = mem.sb("experts_u", [P, NS], U32)
        self.slot_list = nc.dram_tensor(f"{tag}_slot_list", (NS * P, 1), F32).ap()
        self.xn_rows = nc.dram_tensor(f"{tag}_xn_rows", (NG, SEQ, D), F32).ap()
        self.xn_flat = self.xn_rows.rearrange("b s d -> (b s) d")
        self.y_rows = nc.dram_tensor(f"{tag}_y_rows", (NS, P, D), F32).ap()
        self.y_flat = self.y_rows.rearrange("n p d -> (n p) d")


def top2_weights(dve, top, cum, top_w, row, ones, NT):
    dve.tensor_reduce(row[:], top[:, :, 0:2], X, ALU.add)
    dve.drain()
    dve.tensor_scalar(row[:], row[:], 1e-9, None, ALU.add)
    dve.drain()
    dve.reciprocal(row[:], row[:])
    dve.drain()
    dve.tensor_tensor(top_w[:, :, 0:2], top[:, :, 0:2], row[:].unsqueeze(2).to_broadcast([P, NT, 2]), ALU.mult)


def top8_weights(dve, top, cum, top_w, row, ones, NT):
    def normalise(dst, src):
        dve.tensor_reduce(row[:], src, X, ALU.add)
        dve.drain()
        dve.tensor_scalar(row[:], row[:], 1e-12, None, ALU.max)
        dve.drain()
        dve.reciprocal(row[:], row[:])
        dve.drain()
        dve.tensor_tensor(dst, src, row[:].unsqueeze(2).to_broadcast([P, NT, 8]), ALU.mult)
        dve.drain()

    normalise(top_w[:], top[:])
    dve.tensor_copy(cum[:, :, 0], top_w[:, :, 0])
    for k in range(1, 7):
        dve.drain()
        dve.tensor_tensor(cum[:, :, k], cum[:, :, k - 1], top_w[:, :, k], ALU.add)
    dve.drain()
    dve.scalar_tensor_tensor(top_w[:, :, 1:8], cum[:, :, 0:7], 0.8, top[:, :, 1:8], ALU.is_lt, ALU.mult)
    dve.tensor_copy(top_w[:, :, 0:1], top[:, :, 0:1])
    dve.drain()
    normalise(top_w[:], top_w[:])


def routed_layer(nc, tag, x, psum, const, w_all, w_router, router_bias, spec, NG, resident, dma_sems, store=None):
    with ExitStack() as ctx:
        keep = Kept(nc, ctx, f"{tag}_keep", spec, NG, resident, dma_sems)
        route_stage(nc, f"{tag}_route", x, psum, const, w_all, w_router, router_bias, spec, NG, keep)
        slot_stage(nc, f"{tag}_slots", psum, const, spec, keep)
        gather_stage(nc, f"{tag}_gather", x, const, spec, NG, keep, store)


class Const:
    pass


def two_layers(nc, x_in, wqkv0, wo0, bqkv0, bo0, w_router0, b_router0, w_experts0, wqkv1, wo1, bqkv1, bo1,
               w_router1, w_experts1, ident, mask_sel, mask_rows, mask_rowsT, alibi4, iota, slot_steps, token_id, before, out):
    E0, E1 = w_router0.shape[1], w_router1.shape[1]
    I0 = (w_experts0.shape[2] - D) // (2 * DC)
    I1 = (w_experts1.shape[2] - D) // (2 * DC)
    NG = x_in.shape[0]
    NT = NG * TG
    with ExitStack() as ctx:
        mem = Pool_(nc, ctx, "all")
        x = mem.sb("x", [P, NT * D])
        gather_sems = [GatherSems(nc, ctx, f"moe{layer}", K) for layer, K in enumerate((2, 7))]
        const = Const()
        const.ident = mem.sb("ident", [P, P])
        const.mask_sel = mem.sb("mask_sel", [P, 2, P], BF16)
        const.mask_rows = mem.sb("mask_rows", [P, 2, P], BF16)
        const.mask_rowsT = mem.sb("mask_rowsT", [P, 2, P], BF16)
        const.minus_half = mem.sb("minus_half", [P, TG])
        const.ones = mem.sb("ones", [P, 8])
        const.tick = mem.sb("tick", [P, 19])
        const.iota = mem.sb("iota", [P, iota.shape[1]])
        const.tile_no = const.iota
        const.slot_steps = mem.sb("slot_steps", [P, NT])
        const.token_id = mem.sb("token_id", [P, NT])
        const.before = mem.sb("before", [P, P], BF16)
        const.all_ones = mem.sb("all_ones", [P, P], BF16)
        alibi = mem.sb("alibi", [P, TG, H])
        psum = ctx.enter_context(nc.psum_tensor("psum", [P, 8, BANK], F32))

        with ExitStack() as first:
            mem0 = Pool_(nc, first, "load")
            masks = mem0.sb("masks", [P, 3, 2, P])
            before_raw = mem0.sb("before_raw", [P, P])
            x_loaded = mem0.sem("x_loaded")
            consts_loaded = mem0.sem("consts_loaded")
            first.callback(mem0.clear_sems)
            block = first.enter_context(nc.Block())

            @block.sync
            def _(sp):
                sp.dma_start(const.ident[:], ident).then_inc(consts_loaded, 16)
                sp.dma_start(const.iota[:], iota).then_inc(consts_loaded, 16)
                sp.dma_start(const.slot_steps[:], slot_steps[:, 0:NT]).then_inc(consts_loaded, 16)
                sp.dma_start(const.token_id[:], token_id[:, 0:NT]).then_inc(consts_loaded, 16)
                sp.dma_start(before_raw[:], before).then_inc(consts_loaded, 16)
                sp.dma_start(masks[:, 0], mask_sel).then_inc(consts_loaded, 16)
                sp.dma_start(masks[:, 1], mask_rows).then_inc(consts_loaded, 16)
                sp.dma_start(masks[:, 2], mask_rowsT).then_inc(consts_loaded, 16)
                sp.dma_start(alibi[:], alibi4.rearrange("t p h -> p t h")).then_inc(consts_loaded, 16)
                sp.dma_start(x[:].rearrange("p (n d) -> p n d", d=D),
                             x_in.rearrange("b (t p) d -> p (b t) d", p=P)).then_inc(x_loaded, 16)
                sp.wait_ge(x_loaded, 16)

            @block.vector
            def _(dve):
                dve.memset(const.minus_half[:], -0.5)
                dve.memset(const.ones[:], 1.0)
                dve.memset(const.tick[:], 0.0)
                dve.memset(const.all_ones[:], 1.0)
                dve.wait_ge(consts_loaded, 16 * 9)
                dve.tensor_copy(const.before[:], before_raw[:])
                dve.tensor_copy(const.mask_sel[:], masks[:, 0])
                dve.tensor_copy(const.mask_rows[:], masks[:, 1])
                dve.tensor_copy(const.mask_rowsT[:], masks[:, 2])

        attention_stage(nc, "attn0", x, psum, const, wqkv0, wo0, bqkv0, bo0, alibi[:], NG)

        routed_layer(nc, "moe0", x, psum, const, w_experts0, w_router0, b_router0, (E0, 1, I0, 2, top2_weights),
                     NG, True, gather_sems[0])

        attention_stage(nc, "attn1", x, psum, const, wqkv1, wo1, bqkv1, bo1, None, NG)

        routed_layer(nc, "moe1", x, psum, const, w_experts1, w_router1, None, (E1, 0, I1, 7, top8_weights),
                     NG, False, gather_sems[1], store=out)


def laid_out(inputs):
    import numpy as np

    def experts(gate_up, down):
        n, d, gu = gate_up.shape
        out = np.zeros((n, P, DC * gu + d), gate_up.dtype)
        out[:, :, :DC * gu] = gate_up.reshape(n, DC, P, gu).transpose(0, 2, 1, 3).reshape(n, P, DC * gu)
        out[:, :down.shape[1], DC * gu:] = down
        return out

    a = {k: np.asarray(v) for k, v in inputs.items()}
    gu0 = np.concatenate([np.concatenate([a["L0_ffn_Wg"], a["L0_ffn_sWg"][None]], 0),
                          np.concatenate([a["L0_ffn_Wu"], a["L0_ffn_sWu"][None]], 0)], 2)
    dn0 = np.concatenate([a["L0_ffn_Wd"], a["L0_ffn_sWd"][None]], 0)
    i = np.arange(P)
    above = np.where(i[None, :] > i[:, None], np.float32(NEG), np.float32(0))
    slopes = np.float32(2.0 ** (-8.0 / H)) ** np.arange(1, H + 1, dtype=np.float32)
    distances = np.arange(1 - SEQ, 1, dtype=np.float32)
    alibi = (np.float32(HD) ** np.float32(0.5)) * slopes[None, :] * distances[:, None]
    return {
        "x_in": a["L0_attn_x"],
        "wqkv0": np.concatenate([a["L0_attn_Wq"], a["L0_attn_Wk"], a["L0_attn_Wv"]], 1),
        "wo0": a["L0_attn_Wo"],
        "bqkv0": np.concatenate([a["L0_attn_bq"], a["L0_attn_bk"], a["L0_attn_bv"]]),
        "bo0": a["L0_attn_bo"],
        "w_router0": a["L0_ffn_Wr"].T,
        "b_router0": a["L0_ffn_bias"],
        "w_experts0": experts(gu0, dn0),
        "wqkv1": a["L1_attn_W_attn"],
        "wo1": a["L1_attn_W_proj"],
        "bqkv1": a["L1_attn_b_attn"],
        "bo1": a["L1_attn_b_proj"],
        "w_router1": a["L1_ffn_gate_weight"].T,
        "w_experts1": experts(a["L1_ffn_gate_up_proj"].transpose(0, 2, 1), a["L1_ffn_down_proj"].transpose(0, 2, 1)),
        "ident": np.eye(P, dtype=np.float32),
        "mask_sel": np.tile(np.eye(P, dtype=np.float32).reshape(2, P // 2, P), (1, 2, 1)).transpose(1, 0, 2),
        "mask_rows": np.tile(above.reshape(2, P // 2, P), (1, 2, 1)).transpose(1, 0, 2),
        "mask_rowsT": np.tile(above.T.reshape(2, P // 2, P), (1, 2, 1)).transpose(1, 0, 2),
        "alibi4": alibi.astype(np.float32).reshape(TG, P, H),
        "iota": np.broadcast_to(np.arange(256, dtype=np.float32), (P, 256)),
        "slot_steps": np.broadcast_to(P * np.arange(a["L0_attn_x"].shape[0] * TG, dtype=np.float32),
                                      (P, a["L0_attn_x"].shape[0] * TG)),
        "token_id": (P * np.arange(a["L0_attn_x"].shape[0] * TG)[None, :] + i[:, None]).astype(np.float32),
        "before": (i[:, None] < i[None, :]).astype(np.float32),
    }


def kernel(**inputs):
    import numpy as _np
    import concourse.bacc as _bacc
    from concourse.bass_utils import run_bass_kernel_spmd as _run

    nc = _bacc.Bacc("TRN2", target_bir_lowering=False, num_devices=1)
    arrays = {k: _np.ascontiguousarray(v) for k, v in laid_out(inputs).items()}
    args = {k: nc.dram_tensor(k, v.shape, mybir.dt.from_np(v.dtype), kind="ExternalInput").ap()
            for k, v in arrays.items()}
    shape = inputs["L0_attn_x"].shape
    out = nc.dram_tensor("out", shape, F32, kind="ExternalOutput").ap()
    two_layers(nc, **args, out=out)
    r = _run(nc, [arrays], core_ids=[0])
    return r.results[0]["out"]
```

```python
from contextlib import ExitStack

import concourse.bass as bass
from concourse import mybir

P = 128
F32 = mybir.dt.float32
F32R = mybir.dt.float32r
BF16 = mybir.dt.bfloat16
U32 = mybir.dt.uint32
ACT = mybir.ActivationFunctionType
ALU = mybir.AluOpType
X = mybir.AxisListType.X

EPS = 1e-5
D = 256
DC = D // P
H = 16
HD = D // H
SEQ = 512
TG = SEQ // P
BANK = 512
STACK = 64
ROWS_MAX = 50
ROWS_ALL = 52
VW = 32
NEG = -1e30
PACK = 4


class Pool_:

    def __init__(self, nc, ctx, tag):
        self.nc, self.ctx, self.tag, self.sems = nc, ctx, tag, []

    def sb(self, name, shape, dt=F32):
        return self.ctx.enter_context(self.nc.sbuf_tensor(f"{self.tag}_{name}", shape, dt))

    def sem(self, name):
        self.sems.append(self.ctx.enter_context(self.nc.semaphore(f"{self.tag}_{name}")))
        return self.sems[-1]

    def clear_sems(self):
        with self.nc.Block() as block:
            @block.gpsimd
            def _(pool):
                for sem in self.sems:
                    pool.sem_clear(sem)


def hold(pool, const, c=0):
    return pool.tensor_tensor(const.tick[:, c + 1:c + 2], const.tick[:, 0:1], const.tick[:, 0:1], ALU.add)


def product3(pe, out, a_hi, a_lo, b_hi, b_lo, first, last, shared_bank=False):
    pe.matmul(out, a_hi, b_hi, start=first, stop=False, skip_group_check=shared_bank)
    pe.matmul(out, a_hi, b_lo, start=False, stop=False, skip_group_check=shared_bank)
    return pe.matmul(out, a_lo, b_hi, start=False, stop=last, skip_group_check=shared_bank)


def batch_jobs(first, last):
    jobs = []
    for grp in range(H // 4):
        if not last or grp < 2:
            jobs += [("stack", (grp + 2) % 4, 0), ("stack", (grp + 2) % 4, 1)]
        jobs += [("max", grp)]
        if grp == 1 and not last:
            jobs += [("rows",)] + [("qkv", t) for t in range(TG)]
        if grp == 1 and not first:
            jobs += [("ctx", 0), ("ctx", 1)]
        if grp == 2 and not first:
            jobs += [("ctxT",), ("proj",)]
    return jobs


AHEAD_JOBS = [("rows",)] + [("qkv", t) for t in range(TG)] + [("stack", grp, u) for grp in (0, 1) for u in (0, 1)]
TAIL_JOBS = [("ctx", 0), ("ctx", 1), ("ctxT",), ("proj",)]


def attention_stage(nc, tag, x, psum, const, wqkv, wo, bqkv, bo, alibi, NG, x_in=None):
    with ExitStack() as ctx:
        mem = Pool_(nc, ctx, tag)
        wqkv_hi, wqkv_lo = (mem.sb(f"wqkv_{s}", [P, DC, 3 * D], F32R) for s in ("hi", "lo"))
        wo_hi, wo_lo = (mem.sb(f"wo_{s}", [P, DC, D], F32R) for s in ("hi", "lo"))
        bias_qkv = mem.sb("bias_qkv", [P, 3 * D])
        bias_o = mem.sb("bias_o", [P, D])
        stats6 = mem.sb("stats6", [P, TG, 6])
        mean_var = mem.sb("mean_var", [P, TG, 2])
        rstd = mem.sb("rstd", [P, TG])
        xn = mem.sb("xn", [P, TG, D])
        xT_hi, xT_lo = (mem.sb(f"xT_{s}", [P, DC, SEQ], F32R) for s in ("hi", "lo"))
        qkv = mem.sb("qkv", [P, TG, 3 * D])
        q_stack = mem.sb("q_stack", [P, TG, H, STACK])
        k_stack = mem.sb("k_stack", [P, TG, H, STACK])
        qT = mem.sb("qT", [P, H // 2, SEQ], F32R)
        kT = mem.sb("kT", [P, H // 2, SEQ], F32R)
        v = mem.sb("v", [P, TG, H, VW])
        probs = mem.sb("probs", [P, 2, 10, BANK])
        neg_max = mem.sb("neg_max", [P, TG, H])
        ctxT_raw = mem.sb("ctxT_raw", [P, H // 4, SEQ])
        inv_sum = mem.sb("inv_sum", [P, TG, H])
        ctx_n = mem.sb("ctx_n", [P, TG, D])

        weights_in = mem.sem("weights_in")
        consts_in = mem.sem("consts_in")
        x_rest_in = mem.sem("x_rest_in")
        weights_split = mem.sem("weights_split")
        stack_const = mem.sem("stack_const")
        var_ready, rstd_ready, xn_ready = (mem.sem(s) for s in ("var_ready", "rstd_ready", "xn_ready"))
        work_ready = [mem.sem(f"work_ready{i}") for i in range(2)]
        work_read = [mem.sem(f"work_read{i}") for i in range(2)]
        xT_hi_ready = mem.sem("xT_hi_ready")
        stack_hi_ready = mem.sem("stack_hi_ready")
        stack_ready = mem.sem("stack_ready")
        max_scores_ready = mem.sem("max_scores_ready")
        max_scores_used = mem.sem("max_scores_used")
        max_ready = mem.sem("max_ready")
        scores_ready = mem.sem("scores_ready")
        probs_ready = mem.sem("probs_ready")
        v_copied = mem.sem("v_copied")
        ctxT_ready = mem.sem("ctxT_ready")
        ctxT_copied = mem.sem("ctxT_copied")
        cT_hi_ready = mem.sem("cT_hi_ready")
        x_biased = mem.sem("x_biased")

        raw_qkv = probs[:, 0, 0:3, :].rearrange("p a b -> p (a b)").rearrange("p (c n) -> p c n", c=DC)
        raw_o = probs[:, 0, 3, :].rearrange("p (c n) -> p c n", c=DC)
        GROUPS = H // 4
        ITEMS = 10
        NI = GROUPS * ITEMS
        WORK, MAXB, PROBB, CTXB = 0, 2, 4, 7

        def x_rows(b, t):
            return x[:, bass.ds(b * (TG * D) + t * D, D)]

        def job_number(b, job, first=False, last=False):
            before = len(AHEAD_JOBS)
            if not first:
                before = before + len(batch_jobs(True, False)) + (b - 1) * len(batch_jobs(False, False))
            return before + batch_jobs(first, last).index(job)

        def tail_number(job):
            return job_number(NG - 1, ("max", 3), last=True) + 1 + TAIL_JOBS.index(job)

        def max_item(i):
            if i >= 8:
                return [(i - 8, 1, 0, 2 * P), (i - 6, 1, 2 * P, 2 * P)]
            return [(i // 2, 3, 0, 4 * P)] if i % 2 == 0 else [(i // 2, 0, 0, P), (i // 2, 2, P, 3 * P)]

        def prob_item(i):
            if i >= 8:
                return [(i - 8, 2, 0, 2 * P), (i - 6, 2, 2 * P, 2 * P)]
            return [(i // 2, 0, 0, 4 * P)] if i % 2 == 0 else [(i // 2, 1, 0, 3 * P), (i // 2, 3, 3 * P, P)]

        def probs_of(grp, j, kt):
            item, col = {0: (2 * j, 0), 1: (2 * j + 1, 0), 3: (2 * j + 1, 3 * P),
                         2: (8 + j % 2, j // 2 * 2 * P)}[kt]
            return probs[:, grp % 2, item, col:col + SEQ - kt * P]

        def heads(rows, grp, width=HD):
            return rows[:, :, grp * 4 * width:(grp + 1) * 4 * width].rearrange("p t (h d) -> p t h d", h=4)

        def over_batches(eng, part):
            part(0, True, False)
            with eng.Fori(1, NG - 1) as b:
                part(b, False, False)
            part(NG - 1, False, True)

        ctx.callback(mem.clear_sems)
        block = ctx.enter_context(nc.Block())

        @block.sync
        def _(sp):
            sp.dma_start(raw_qkv, wqkv.rearrange("(c p) n -> p c n", p=P)).then_inc(weights_in, 16)
            sp.dma_start(raw_o, wo.rearrange("(c p) n -> p c n", p=P)).then_inc(weights_in, 16)
            sp.dma_start(bias_qkv[:], bqkv.partition_broadcast(P)).then_inc(consts_in, 16)
            sp.dma_start(bias_o[:], bo.partition_broadcast(P)).then_inc(consts_in, 16)
            if x_in is not None:
                sp.dma_start(x[:, TG * D:].rearrange("p (n d) -> p n d", d=D),
                             x_in[1:].rearrange("b (t p) d -> p (b t) d", p=P)).then_inc(x_rest_in, 16)

        @block.gpsimd
        def _(pool):
            pool.memset(q_stack[:], 0.0)
            pool.memset(k_stack[:], 0.0)
            pool.memset(v[:], 0.0)
            pool.drain()
            pool.memset(q_stack[:, :, :, 48:50], 1.0)
            pool.memset(k_stack[:, :, :, 50:52], 1.0)
            pool.memset(v[:, :, :, HD:HD + 1], 1.0).then_inc(stack_const, 1)
            pool.wait_ge(consts_in, 32)

            def power(b):
                pool.wait_ge(var_ready, b + 1)
                pool.tensor_tensor(rstd[:], mean_var[:, :, 1], const.minus_half[:, 0:TG],
                                   ALU.pow).then_inc(rstd_ready, 1)

            def add_bias(b):
                pool.wait_ge(xn_ready, b + 1)
                for t in range(TG):
                    ins = pool.tensor_tensor(x_rows(b, t), x_rows(b, t), bias_o[:], ALU.add)
                ins.then_inc(x_biased, 1)

            def complete_stacks(G, grp):
                pool.wait_ge(stack_hi_ready, G + 1)
                for t in range(TG):
                    hs = slice(4 * grp, 4 * grp + 4)
                    one = const.ones[:, 0:1].unsqueeze(2).to_broadcast([P, 4, HD])
                    q_rows, k_rows = (heads(qkv[:, :, c:c + D], grp)[:, t] for c in (0, D))
                    pool.tensor_tensor(q_stack[:, t, hs, 32:48], q_stack[:, t, hs, 0:16], one, ALU.mult)
                    pool.tensor_tensor(k_stack[:, t, hs, 16:32], k_stack[:, t, hs, 0:16], one, ALU.mult)
                    pool.tensor_tensor(q_stack[:, t, hs, 16:32].bitcast(F32R), q_rows, q_stack[:, t, hs, 0:16],
                                       ALU.subtract)
                    ins = pool.tensor_tensor(k_stack[:, t, hs, 32:48].bitcast(F32R), k_rows,
                                             k_stack[:, t, hs, 0:16], ALU.subtract)
                ins.then_inc(stack_ready, 1)

            power(0)
            add_bias(0)
            for grp in range(3):
                complete_stacks(grp, grp)

            def batch(b, first, last):
                for grp in range(GROUPS):
                    G = b * GROUPS + grp
                    if grp == 0 and not last:
                        power(b + 1)
                    if grp == 1 and not last:
                        add_bias(b + 1)
                    if not (last and grp >= 1):
                        complete_stacks(G + 3, (grp + 3) % GROUPS)

            over_batches(pool, batch)

        @block.scalar
        def _(act):
            act.wait_ge(weights_in, 32)
            act.activation(wqkv_hi[:], raw_qkv, ACT.Copy)
            act.activation(wo_hi[:], raw_o, ACT.Copy).then_inc(weights_split, 1)
            act.wait_ge(stack_const, 1)

            def transposed_hi(n, count, done):
                for c in range(DC):
                    act.wait_ge(work_ready[c], n + 1)
                    act.activation(xT_hi[:, c, :], psum[:, WORK + c, :], ACT.Copy).then_inc(done, 1)

            def split_hi(G, grp, n_qkv=None):
                if n_qkv is not None:
                    act.wait_ge(work_read[1], n_qkv + 1)
                hs = slice(4 * grp, 4 * grp + 4)
                act.activation(q_stack[:, :, hs, 0:16].bitcast(F32R), heads(qkv[:, :, 0:D], grp), ACT.Copy)
                act.activation(k_stack[:, :, hs, 0:16].bitcast(F32R), heads(qkv[:, :, D:2 * D], grp),
                               ACT.Copy).then_inc(stack_hi_ready, 1)

            def copy_stacks(n, pair):
                for u, stackT in enumerate((qT, kT)):
                    act.wait_ge(work_ready[u], n + 1)
                    act.activation(stackT[:, pair, :], psum[:, WORK + u, :], ACT.Copy).then_inc(work_read[u], 1)

            def copy_ctxT(G, grp):
                act.wait_ge(ctxT_ready, G + 1)
                act.activation(ctxT_raw[:, grp, :], psum[:, CTXB, :], ACT.Copy).then_inc(ctxT_copied, 1)

            def copy_values(b):
                act.activation(v[:, :, :, 0:HD], qkv[:, :, 2 * D:3 * D].rearrange("p t (h d) -> p t h d", h=H),
                               ACT.Copy).then_inc(v_copied, 1)

            transposed_hi(0, 0, xT_hi_ready)
            for grp in range(3):
                split_hi(grp, grp, AHEAD_JOBS.index(("qkv", 3)))
            for grp in range(2):
                for u in range(2):
                    copy_stacks(AHEAD_JOBS.index(("stack", grp, u)), 2 * grp + u)

            def batch(b, first, last):
                def number(*job):
                    return job_number(b, job, first, last)

                for grp in range(GROUPS):
                    G = b * GROUPS + grp
                    if not last or grp < 2:
                        for u in range(2):
                            copy_stacks(number("stack", (grp + 2) % 4, u), 2 * ((grp + 2) % 4) + u)
                    if not (first and grp < 2):
                        copy_ctxT(G - 2, (grp - 2) % GROUPS)
                    for u in range(2):
                        act.wait_ge(work_ready[u], number("max", grp) + 1)
                        act.activation(qT[:, 2 * grp + u, :], psum[:, WORK + u, :], ACT.Copy).then_inc(work_read[u], 1)
                    for i in range(ITEMS):
                        n = grp * ITEMS + i
                        act.wait_ge(scores_ready, b * NI + n + 1)
                        act.activation(probs[:, grp % 2, i, :], psum[:, PROBB + n % 3, :], ACT.Exp,
                                       scale=float(HD) ** -0.5).then_inc(probs_ready, 1)
                        if grp == 1 and i == 0:
                            if not last:
                                transposed_hi(number("rows"), 0, xT_hi_ready)
                            copy_values(b)
                        if grp == 2 and i == 3 and not first:
                            transposed_hi(number("ctxT"), 0, cT_hi_ready)
                        if i == (6 if grp == 1 else 0) and not (last and grp >= 1):
                            split_hi(G + 3, (grp + 3) % GROUPS, number("qkv", 3) if grp == 1 else None)

            over_batches(act, batch)
            for k in (2, 1):
                copy_ctxT(NG * GROUPS - k, GROUPS - k)
            transposed_hi(tail_number(("ctxT",)), 0, cT_hi_ready)

        @block.vector
        def _(dve):
            dve.wait_ge(weights_split, 1)
            dve.tensor_tensor(wqkv_lo[:], raw_qkv, wqkv_hi[:].bitcast(F32), ALU.subtract)
            dve.tensor_tensor(wo_lo[:], raw_o, wo_hi[:].bitcast(F32), ALU.subtract).then_inc(weights_split, 1)
            dve.wait_ge(consts_in, 32)
            dve.wait_ge(stack_const, 1)
            if alibi is not None:
                dve.tensor_copy(k_stack[:, :, :, 48].bitcast(F32R), alibi)
                dve.drain()
                dve.tensor_tensor(k_stack[:, :, :, 49].bitcast(F32R), alibi, k_stack[:, :, :, 48], ALU.subtract)

            def row_stats(b):
                for t in range(TG):
                    dve.bn_stats(stats6[:, t, :], x_rows(b, t))
                dve.drain()
                for t in range(TG):
                    dve.bn_aggr(mean_var[:, t, :], stats6[:, t, :])
                dve.drain()
                dve.tensor_scalar(mean_var[:, :, 1], mean_var[:, :, 1], EPS, None, ALU.add).then_inc(var_ready, 1)

            def normalise(b):
                dve.wait_ge(rstd_ready, b + 1)
                for t in range(TG):
                    ins = dve.tensor_scalar(xn[:, t, :], x_rows(b, t), mean_var[:, t, 0:1], rstd[:, t:t + 1],
                                            ALU.subtract, ALU.mult)
                ins.then_inc(xn_ready, 1)

            def transposed_lo(hi_ready, n_hi):
                for c in range(DC):
                    dve.wait_ge(hi_ready, n_hi + c + 1)
                    dve.tensor_tensor(xT_lo[:, c, :], psum[:, WORK + c, :], xT_hi[:, c, :].bitcast(F32),
                                      ALU.subtract).then_inc(work_read[c], 1)

            def copy_qkv(n, t):
                dve.wait_ge(work_ready[0], n + 1)
                dve.tensor_tensor(qkv[:, t, 0:2 * D], psum[:, WORK, :], bias_qkv[:, 0:2 * D],
                                  ALU.add).then_inc(work_read[0], 1)
                dve.wait_ge(work_ready[1], n + 1)
                dve.tensor_tensor(qkv[:, t, 2 * D:3 * D], psum[:, WORK + 1, 0:D], bias_qkv[:, 2 * D:3 * D],
                                  ALU.add).then_inc(work_read[1], 1)

            def row_maxima(b, G, grp, i):
                dve.wait_ge(max_scores_ready, G * ITEMS + i + 1)
                bank = psum[:, MAXB + i % 2, :]
                if i >= 8:
                    ins = dve.tensor_reduce(neg_max[:, 1, 4 * grp + i - 8:4 * grp + i - 5:2],
                                            bank.rearrange("p (a k) -> p a k", a=2), X, ALU.max, negate=True)
                else:
                    for j, t, col, w in max_item(i):
                        head = 4 * grp + j
                        ins = dve.tensor_reduce(neg_max[:, t, head:head + 1], bank[:, col:col + w], X, ALU.max,
                                                negate=True)
                ins.then_inc(max_scores_used, 1)

            def stack_maxima(grp):
                dve.drain()
                cols = slice(4 * grp, 4 * grp + 4)
                dve.tensor_copy(q_stack[:, :, cols, 50].bitcast(F32R), neg_max[:, :, cols])
                dve.drain()
                dve.tensor_tensor(q_stack[:, :, cols, 51].bitcast(F32R), neg_max[:, :, cols],
                                  q_stack[:, :, cols, 50], ALU.subtract).then_inc(max_ready, 1)

            def norm_contexts(n, half):
                for u in range(2):
                    dve.wait_ge(work_ready[u], n + 1)
                    dve.reciprocal(inv_sum[:, 2 * half + u, :], psum[:, WORK + u, HD:BANK:VW])
                dve.drain()
                for u in range(2):
                    t = 2 * half + u
                    dve.tensor_tensor(ctx_n[:, t, :].rearrange("p (h d) -> p h d", h=H),
                                      psum[:, WORK + u, :].rearrange("p (h d) -> p h d", h=H)[:, :, 0:HD],
                                      inv_sum[:, t, :].unsqueeze(2).to_broadcast([P, H, HD]),
                                      ALU.mult).then_inc(work_read[u], 1)

            def add_projection(b, n):
                dve.wait_ge(x_biased, b + 1)
                for u in range(2):
                    dve.wait_ge(work_ready[u], n + 1)
                    rows = x[:, bass.ds(b * (TG * D) + 2 * u * D, 2 * D)]
                    dve.tensor_tensor(rows, rows, psum[:, WORK + u, :], ALU.add).then_inc(work_read[u], 1)

            row_stats(0)
            normalise(0)
            transposed_lo(xT_hi_ready, 0)
            for t in range(TG):
                copy_qkv(AHEAD_JOBS.index(("qkv", t)), t)
            for i in range(ITEMS):
                row_maxima(0, 0, 0, i)
            stack_maxima(0)

            def batch(b, first, last):
                def number(*job):
                    return job_number(b, job, first, last)

                for grp in range(GROUPS):
                    G = b * GROUPS + grp
                    nxt = (grp + 1) % GROUPS
                    if grp == 0 and first and x_in is not None:
                        dve.wait_ge(x_rest_in, 16)
                    if grp == 0 and not last:
                        row_stats(b + 1)
                    for i in range(ITEMS):
                        if not (last and grp == 3):
                            row_maxima(b, G + 1, nxt, i)
                        if grp == 1 and not last:
                            if i == 1:
                                transposed_lo(xT_hi_ready, (b + 1) * DC)
                                dve.wait_ge(v_copied, b + 1)
                            if i in (2, 3, 4, 5):
                                copy_qkv(number("qkv", i - 2), i - 2)
                        if grp == 2 and not first:
                            if i == 4:
                                transposed_lo(cT_hi_ready, (b - 1) * DC)
                            if i == 7:
                                add_projection(b - 1, number("proj"))
                    if not (last and grp == 3):
                        stack_maxima(nxt)
                    if grp == 1 and not first:
                        norm_contexts(number("ctx", 0), 0)
                        norm_contexts(number("ctx", 1), 1)
                    if grp == 0 and not last:
                        normalise(b + 1)

            over_batches(dve, batch)
            for half in range(2):
                norm_contexts(tail_number(("ctx", half)), half)
            transposed_lo(cT_hi_ready, (NG - 1) * DC)
            add_projection(NG - 1, tail_number(("proj",)))

        @block.tensor
        def _(pe):
            pe.wait_ge(weights_split, 2)

            def bank_free(c, n):
                pe.wait_ge(work_read[c], n)

            def transpose_rows(rows, n):
                if not isinstance(n, int) or n > 0:
                    bank_free(0, n)
                    bank_free(1, n)
                for c in range(DC):
                    for t in range(TG):
                        ins = pe.transpose(psum[:, WORK + c, t * P:(t + 1) * P], rows[:, t, c * P:(c + 1) * P],
                                           const.ident[:])
                    ins.then_inc(work_ready[c], 1)

            def make_qkv(n, t):
                for u, c0, c1 in ((0, 0, 2 * D), (1, 2 * D, 3 * D)):
                    bank_free(u, n)
                    for c in range(DC):
                        if t == 0 and u == 0 and c == 1:
                            bank_free(1, n)
                        tok = slice(t * P, (t + 1) * P)
                        ins = product3(pe, psum[:, WORK + u, 0:c1 - c0], xT_hi[:, c, tok], xT_lo[:, c, tok],
                                       wqkv_hi[:, c, c0:c1], wqkv_lo[:, c, c0:c1], c == 0, c == DC - 1)
                    ins.then_inc(work_ready[u], 1)

            def transpose_pair(stack, bank, pair, n):
                bank_free(bank, n)
                for t in range(TG):
                    ins = pe.transpose(psum[:, WORK + bank, t * P:(t + 1) * P],
                                       stack[:, t, 2 * pair:2 * pair + 2, :].rearrange("p a b -> p (a b)"),
                                       const.ident[:])
                ins.then_inc(work_ready[bank], 1)

            def transpose_stacks(G, grp, u, n):
                if u == 0:
                    pe.wait_ge(stack_ready, G + 1)
                transpose_pair(q_stack, 0, 2 * grp + u, n)
                transpose_pair(k_stack, 1, 2 * grp + u, n)

            def transpose_maxima(G, grp, n):
                pe.wait_ge(max_ready, G + 1)
                for u in range(2):
                    transpose_pair(q_stack, u, 2 * grp + u, n)

            def stack_rows(sT, head, rows, c0, c1):
                row = STACK * (head % 2)
                return sT[row:row + rows, head // 2, c0:c1]

            def add_mask(bank, blocks, half_of_rows, rows, part, whole):
                at = slice(half_of_rows * (P // 2), (half_of_rows + 1) * (P // 2))
                step = blocks[-1] - blocks[0] if len(blocks) > 1 else P
                some, full = (1, 0) if part[0] else (0, 1)
                for n, (h, (c0, c1)) in enumerate(((some, part), (full, whole))):
                    src = rows[at, h, c0:c1].unsqueeze(1).to_broadcast([P // 2, len(blocks), c1 - c0])
                    out = bank[:, blocks[0]:blocks[0] + (len(blocks) - 1) * step + P]
                    if len(blocks) > 1:
                        out = bass_blocks(bank, blocks, c0, c1)
                    else:
                        src, out = rows[at, h, c0:c1], bank[:, blocks[0] + c0:blocks[0] + c1]
                    pe.matmul(out, const.mask_sel[at, h, :], src, start=(n == 0), stop=False,
                              skip_group_check=True)

            def bass_blocks(bank, blocks, c0, c1):
                first, second = (c // P for c in blocks)
                return bank.rearrange("p (n c) -> p n c", c=P)[:, first:second + 1:second - first, c0:c1]

            def max_scores(G, grp, i):
                if not isinstance(G, int) or G > 0 or i >= 2:
                    pe.wait_ge(max_scores_used, G * ITEMS + i - 1)
                pieces = max_item(i)
                bank = psum[:, MAXB + i % 2, :]
                add_mask(bank, [col + w - P for _, _, col, w in pieces], pieces[0][0] % 2, const.mask_rows,
                         (P // 2, P), (0, P))
                for j, t, col, w in pieces:
                    head = 4 * grp + j
                    ins = pe.matmul(bank[:, col:col + w], stack_rows(qT, head, ROWS_MAX, t * P, (t + 1) * P),
                                    stack_rows(kT, head, ROWS_MAX, 0, w), start=False, stop=True,
                                    skip_group_check=True)
                ins.then_inc(max_scores_ready, 1)

            def prob_scores(b, grp, i, first):
                n = grp * ITEMS + i
                if n >= 3:
                    pe.wait_ge(probs_ready, b * NI + n - 2)
                elif not first:
                    pe.wait_ge(probs_ready, b * NI - (0, 2, 1)[n])
                pieces = prob_item(i)
                bank = psum[:, PROBB + n % 3, :]
                add_mask(bank, [col for _, _, col, _ in pieces], pieces[0][0] % 2, const.mask_rowsT,
                         (0, P // 2), (0, P))
                for j, t, col, w in pieces:
                    head = 4 * grp + j
                    ins = pe.matmul(bank[:, col:col + w], stack_rows(kT, head, ROWS_ALL, t * P, (t + 1) * P),
                                    stack_rows(qT, head, ROWS_ALL, t * P, SEQ), start=False, stop=True,
                                    skip_group_check=True)
                ins.then_inc(scores_ready, 1)

            def weigh_values(b, G, grp, key_tiles):
                if key_tiles[0] == 0:
                    values_free(b, G)
                for kt in key_tiles:
                    for j in range(4):
                        ins = pe.matmul(psum[VW * j:VW * (j + 1), CTXB, kt * P:SEQ], v[:, kt, 4 * grp + j, :],
                                        probs_of(grp, j, kt), start=(kt == 0), stop=(kt == TG - 1),
                                        tile_position=(0, VW * j))
                if key_tiles[-1] == TG - 1:
                    ins.then_inc(ctxT_ready, 1)

            def values_free(b, G):
                pe.wait_ge(probs_ready, (G + 1) * ITEMS)
                pe.wait_ge(v_copied, b + 1)
                if not isinstance(G, int) or G > 0:
                    pe.wait_ge(ctxT_copied, G)

            def transpose_contexts(n, half, G_last):
                pe.wait_ge(ctxT_copied, G_last + 1)
                for u in range(2):
                    bank_free(u, n)
                    t = 2 * half + u
                    for q in range(GROUPS):
                        ins = pe.transpose(psum[:, WORK + u, q * P:(q + 1) * P], ctxT_raw[:, q, t * P:(t + 1) * P],
                                           const.ident[:])
                    ins.then_inc(work_ready[u], 1)

            def project(n):
                for u in range(2):
                    bank_free(0, n)
                    bank_free(1, n)
                    for t in (2 * u, 2 * u + 1):
                        for c in range(DC):
                            tok = slice(t * P, (t + 1) * P)
                            ins = product3(pe, psum[:, WORK + u, (t % 2) * D:(t % 2 + 1) * D],
                                           xT_hi[:, c, tok], xT_lo[:, c, tok], wo_hi[:, c, :], wo_lo[:, c, :],
                                           c == 0, c == DC - 1)
                    ins.then_inc(work_ready[u], 1)

            pe.wait_ge(xn_ready, 1)
            transpose_rows(xn, 0)
            for t in range(TG):
                make_qkv(AHEAD_JOBS.index(("qkv", t)), t)
            for grp in range(2):
                for u in range(2):
                    transpose_stacks(grp, grp, u, AHEAD_JOBS.index(("stack", grp, u)))
            for c in range(2):
                bank_free(c, AHEAD_JOBS.index(("stack", 0, 1)) + 1)
            for i in range(ITEMS):
                max_scores(0, 0, i)

            def batch(b, first, last):
                def number(*job):
                    return job_number(b, job, first, last)

                for grp in range(GROUPS):
                    G = b * GROUPS + grp
                    nxt = (grp + 1) % GROUPS
                    weigh = not (first and grp < 2)
                    values = (b if grp >= 2 else b - 1, G - 2, (grp - 2) % GROUPS)
                    ahead = not last or grp < 2
                    if ahead:
                        transpose_stacks(G + 2, (grp + 2) % 4, 0, number("stack", (grp + 2) % 4, 0))
                    if weigh:
                        weigh_values(*values, (0,))
                    if ahead:
                        transpose_stacks(G + 2, (grp + 2) % 4, 1, number("stack", (grp + 2) % 4, 1))
                    if weigh:
                        weigh_values(*values, (1, 2, 3))
                    transpose_maxima(G, grp, number("max", grp))
                    if not (last and grp == 3):
                        max_scores(G + 1, nxt, 0)
                    for i in range(ITEMS):
                        if i + 1 < ITEMS and not (last and grp == 3):
                            max_scores(G + 1, nxt, i + 1)
                        if i == 0:
                            for c in range(2):
                                bank_free(c, number("max", grp) + 1)
                        prob_scores(b, grp, i, first)
                        if grp == 1 and not last:
                            if i == 0:
                                pe.wait_ge(xn_ready, b + 2)
                                transpose_rows(xn, number("rows"))
                            if i in (1, 2, 3, 4):
                                make_qkv(number("qkv", i - 1), i - 1)
                        if grp == 1 and not first and i in (8, 9):
                            transpose_contexts(number("ctx", i - 8), i - 8, b * GROUPS - 1)
                        if grp == 2 and not first:
                            if i == 3:
                                transpose_rows(ctx_n, number("ctxT"))
                            if i == 6:
                                project(number("proj"))

            over_batches(pe, batch)
            for k in (2, 1):
                weigh_values(NG - 1, NG * GROUPS - k, GROUPS - k, (0, 1, 2, 3))
            for half in range(2):
                transpose_contexts(tail_number(("ctx", half)), half, NG * GROUPS - 1)
            transpose_rows(ctx_n, tail_number(("ctxT",)))
            project(tail_number(("proj",)))


def slot_tiles(tokens, experts, k, step):
    need = tokens * k // P + experts - 1
    return -(-need // step) * step


def route_stage(nc, tag, x, psum, const, w_all, w_router, router_bias, spec, NG, keep):
    E, SHARED, I, K, weights_of = spec
    NT = NG * TG
    NS = keep.NS
    NC = -(-NS // P)
    CAP = NT * P
    GU = 2 * I
    C = DC * GU + D
    EPG = E // NG
    COLS = TG * K
    split = keep.w_hi is not None
    LATER = SHARED > 0
    with ExitStack() as ctx:
        mem = Pool_(nc, ctx, tag)
        w_raw = mem.sb("w_raw", [P, EPG, C]) if split else None
        stats6 = mem.sb("stats6", [P, TG, 6])
        mean_var = mem.sb("mean_var", [P, TG, 2])
        mean, var, rstd = (mem.sb(name, [P, NT]) for name in ("mean", "var", "rstd"))
        xn = mem.sb("xn", [P, TG, D])
        xT_hi, xT_lo = (mem.sb(f"xT_{s}", [P, DC, SEQ], F32R) for s in ("hi", "lo"))
        if SHARED:
            gate = mem.sb("gate", [P, TG, I])
            hid = mem.sb("hid", [P, TG, I])
            hT_hi, hT_lo = (mem.sb(f"hT_{s}", [P, SEQ], F32R) for s in ("hi", "lo"))
        wr_raw = mem.sb("wr_raw", [P, DC, E])
        wr_hi, wr_lo = (mem.sb(f"wr_{s}", [P, DC, E], F32R) for s in ("hi", "lo"))
        bias_r = mem.sb("bias_r", [P, E])
        logits = mem.sb("logits", [P, TG, E])
        probs = mem.sb("probs", [P, TG, E])
        row = mem.sb("row", [P, NT])
        top_g = mem.sb("top_g", [P, TG, 8])
        top_i = mem.sb("top_i", [P, TG, 8], U32)
        top_if = mem.sb("top_if", [P, TG, 8])
        top = mem.sb("top", [P, NT, 8])
        cum = mem.sb("cum", [P, NT, 8])
        choices = mem.sb("choices", [P, TG, K, E])
        counts_g = mem.sb("counts_g", [P, TG, E])
        chosen = mem.sb("chosen", [P, TG, E], BF16)
        list_start = mem.sb("list_start", [P, E])
        list_end = mem.sb("list_end", [P, E])
        places = mem.sb("places", [P, TG, E])
        place_f = mem.sb("place_f", [P, TG, K])
        place_all = mem.sb("place_all", [P, NT * K])
        place_u = mem.sb("place_u", [P, NT * K], U32)
        wide = mem.sb("wide", [P, max(NT * K, NS) * E])
        over = mem.sb("over", [P, E, NT])
        ones = mem.sb("ones", [P, E])
        counts, n_tiles, tile_end, step_back = (mem.sb(name, [P, E]) for name in
                                                ("counts", "n_tiles", "tile_end", "step_back"))
        moved = mem.sb("moved", [P, NT * K])
        ends = mem.sb("ends", [P, NC, E])
        list_row_f, tiles_before = (mem.sb(name, [P, NC]) for name in ("list_row_f", "tiles_before"))
        list_row = mem.sb("list_row", [P, NC], U32)
        expert_f, packed_f = (mem.sb(name, [P, NS]) for name in ("expert_f", "packed_f"))
        zeros = mem.sb("zeros", [P, P])
        place_cols = mem.sb("place_cols", [P, 2, COLS], U32)
        id_cols = mem.sb("id_cols", [P, 2, TG])
        tokens_of = mem.sb("tokens_of", [P, NC, P])

        names = ("even_weights_in", "odd_weights_in", "router_in", "bias_in", "weights_hi", "weights_lo",
                 "router_split", "var_ready", "rstd_ready", "xn_ready", "rows_kept", "xnT_ready", "xT_hi_ready",
                 "xT_lo_ready", "logits_ready", "logits_shifted", "exps_ready", "gate_up_ready", "gate_ready",
                 "hid_ready", "hidT_ready", "hT_hi_ready", "hT_lo_ready", "y_ready", "chosen_ready",
                 "counts_ready", "places_ready", "zeros_ready", "lists_cleared", "list_rows_ready", "listT_ready")
        sem = {name: mem.sem(name) for name in names}
        scattered = keep.dma_sems.scattered
        weights_in = (sem["even_weights_in"], sem["odd_weights_in"])
        LB, GUB, RB, HB, YB = 0, 1, 3, 4, 6

        def x_rows(g, t):
            return x[:, bass.ds(g * (TG * D) + t * D, D)]

        def one_column(rows, g, t):
            return rows[:, bass.ds(g * TG + t, 1)]

        def expert_columns(e):
            return bass.ds(e * C, C) if not isinstance(e, int) else slice(e * C, (e + 1) * C)

        ctx.callback(mem.clear_sems)
        block = ctx.enter_context(nc.Block())

        @block.sync
        def _(sp):
            sp.dma_start(wr_raw[:], w_router.rearrange("(c p) e -> p c e", p=P)).then_inc(sem["router_in"], 16)
            if router_bias is not None:
                sp.dma_start(bias_r[:], router_bias.partition_broadcast(P)).then_inc(sem["bias_in"], 16)
            if SHARED:
                sp.dma_start(w_raw[:, 0, :], w_all[E]).then_inc(weights_in[0], 16)
            sp.wait_ge(sem["zeros_ready"], 1)
            for c in range(E * NT // P):
                sp.dma_start(keep.list_tiles[c * P:(c + 1) * P, :], zeros[:]).then_inc(sem["lists_cleared"], 16)
            with sp.Fori(0, NG) as g:
                sp.wait_ge(sem["xn_ready"], g + 1)
                sp.dma_start(keep.xn_rows[bass.ds(g, 1)].rearrange("b (t p) d -> p (b t) d", p=P),
                             xn[:]).then_inc(sem["rows_kept"], 16)
                if split:
                    sp.wait_ge(sem["weights_lo"], g * EPG + 1)
                    for k in range(EPG):
                        sp.dma_start(w_raw[:, k, :], w_all[bass.ds(g * EPG + k, 1)].rearrange("e p c -> p (e c)")
                                     ).then_inc(weights_in[k], 16)
                else:
                    sp.dma_start(keep.w_raw[:, bass.ds(g * (EPG * C), EPG * C)].rearrange("p (e c) -> p e c", c=C),
                                 w_all[bass.ds(g * EPG, EPG)].rearrange("e p c -> p e c")).then_inc(weights_in[0], 16)
            sp.wait_ge(sem["rows_kept"], 16 * NG)
            if not split:
                sp.wait_ge(weights_in[0], 16 * NG)

        @block.gpsimd
        def _(pool):
            def power(g):
                tiles = bass.ds(g * TG, TG)
                pool.wait_ge(sem["var_ready"], g + 1)
                pool.tensor_tensor(rstd[:, tiles], var[:, tiles], const.minus_half[:, 0:TG],
                                   ALU.pow).then_inc(sem["rstd_ready"], 1)

            for g in range(3):
                power(g)
            pool.wait_ge(sem["lists_cleared"], 16 * (E * NT // P))

            def write_group(g, b):
                pool.tensor_copy(place_cols[:, b, :], place_u[:, bass.ds(g * COLS, COLS)])
                pool.tensor_copy(id_cols[:, b, :], const.token_id[:, bass.ds(g * TG, TG)])
                pool.drain()
                for t in range(TG):
                    for k in range(K):
                        c = t * K + k
                        pool.indirect_dma_start(keep.lists, bass.IndirectOffsetOnAxis(place_cols[:, b, c:c + 1], 0),
                                                id_cols[:, b, t:t + 1], None).then_inc(scattered[b], 16)

            for g in range(2):
                power(g + 3)
                pool.wait_ge(sem["places_ready"], g + 1)
                write_group(g, g)

            def two_groups(i):
                for b in range(2):
                    if not isinstance(i, int) or i * 2 + b + 3 < NG:
                        power(i * 2 + b + 3)
                    pool.wait_ge(sem["places_ready"], i * 2 + b + 1)
                    hold(pool, const, 0)
                    pool.wait_ge(scattered[b], i * (16 * COLS))
                    hold(pool, const, 1)
                    write_group(i * 2 + b, b)

            with pool.Fori(1, NG // 2 - 2) as i:
                two_groups(i)
            two_groups(NG // 2 - 2)
            two_groups(NG // 2 - 1)
            for b in range(2):
                pool.wait_ge(scattered[b], 16 * COLS * NG // 2)
            pool.wait_ge(sem["list_rows_ready"], 1)
            for c in range(NC):
                pool.indirect_dma_start(tokens_of[:, c, :], None, keep.list_tiles,
                                        bass.IndirectOffsetOnAxis(list_row[:, c:c + 1], 0)
                                        ).then_inc(keep.dma_sems.tokens_in, 16)

        @block.scalar
        def _(act):
            act.wait_ge(sem["router_in"], 16)
            act.activation(wr_hi[:], wr_raw[:], ACT.Copy).then_inc(sem["router_split"], 1)
            if SHARED:
                act.wait_ge(weights_in[0], 16)
                act.activation(keep.w_hi[:, expert_columns(E)], w_raw[:, 0, :],
                               ACT.Copy).then_inc(sem["weights_hi"], 1)
            with act.Fori(0, NG) as g:
                for c in range(DC):
                    act.wait_ge(sem["xnT_ready"], g * DC + c + 1)
                    act.activation(xT_hi[:, c, :], psum[:, HB + c, :], ACT.Copy).then_inc(sem["xT_hi_ready"], 1)
                act.wait_ge(sem["logits_shifted"], g + 1)
                act.activation(probs[:], logits[:], ACT.Exp).then_inc(sem["exps_ready"], 1)
                if SHARED:
                    act.wait_ge(sem["gate_up_ready"], g + 1)
                    gu = psum[:, GUB:GUB + 2, :].rearrange("p a (u k) -> p (a u) k", u=2)
                    act.activation(gate[:], gu[:, :, 0:I], ACT.Silu).then_inc(sem["gate_ready"], 1)
                    act.wait_ge(sem["hidT_ready"], g + 1)
                    act.activation(hT_hi[0:I, :], psum[0:I, HB, :], ACT.Copy).then_inc(sem["hT_hi_ready"], 1)
                if split:
                    for k in range(EPG):
                        act.wait_ge(weights_in[k], g * 16 + (32 if k == 0 and SHARED else 16))
                        act.activation(keep.w_hi[:, expert_columns(g * EPG + k)], w_raw[:, k, :],
                                       ACT.Copy).then_inc(sem["weights_hi"], 1)

        @block.vector
        def _(dve):
            dve.memset(zeros[:], 0.0).then_inc(sem["zeros_ready"], 1)
            dve.memset(ones[:], 1.0)

            def row_stats(g):
                for t in range(TG):
                    dve.bn_stats(stats6[:, t, :], x_rows(g, t))
                dve.drain()
                for t in range(TG):
                    dve.bn_aggr(mean_var[:, t, :], stats6[:, t, :])
                dve.drain()
                tiles = bass.ds(g * TG, TG)
                dve.tensor_copy(mean[:, tiles], mean_var[:, :, 0])
                dve.tensor_scalar(var[:, tiles], mean_var[:, :, 1], EPS, None,
                                  ALU.add).then_inc(sem["var_ready"], 1)

            for g in range(3):
                row_stats(g)
                dve.drain()
            dve.tensor_scalar(list_start[:], const.iota[:, 0:E], float(CAP), None, ALU.mult)
            dve.drain()
            dve.tensor_copy(list_end[:], list_start[:])
            dve.wait_ge(sem["router_split"], 1)
            dve.tensor_tensor(wr_lo[:], wr_raw[:], wr_hi[:].bitcast(F32), ALU.subtract).then_inc(sem["router_split"], 1)
            if SHARED:
                dve.wait_ge(sem["weights_hi"], 1)
                dve.tensor_tensor(keep.w_lo[:, expert_columns(E)], w_raw[:, 0, :],
                                  keep.w_hi[:, expert_columns(E)].bitcast(F32),
                                  ALU.subtract).then_inc(sem["weights_lo"], 1)
            if router_bias is not None:
                dve.wait_ge(sem["bias_in"], 16)

            def normalise(g):
                dve.wait_ge(sem["rstd_ready"], g + 1)
                if not (isinstance(g, int) and g == 0):
                    dve.wait_ge(sem["rows_kept"], g * 16)
                for t in range(TG):
                    ins = dve.tensor_scalar(xn[:, t, :], x_rows(g, t), one_column(mean, g, t), one_column(rstd, g, t),
                                            ALU.subtract, ALU.mult)
                ins.then_inc(sem["xn_ready"], 1)

            def per_row(g_row):
                return g_row.unsqueeze(2).to_broadcast([P, TG, E])

            def group(g, first, last):
                for c in range(DC):
                    dve.wait_ge(sem["xT_hi_ready"], g * DC + c + 1)
                    dve.tensor_tensor(xT_lo[:, c, :], psum[:, HB + c, :], xT_hi[:, c, :].bitcast(F32),
                                      ALU.subtract).then_inc(sem["xT_lo_ready"], 1)
                if not last:
                    normalise(g + 1)
                if LATER and not first:
                    dve.drain()
                    mark_choices(g - 1)
                    split_lo(g - 1)
                if not isinstance(g, int) or g + 3 < NG:
                    row_stats(g + 3)
                dve.wait_ge(sem["logits_ready"], g + 1)
                raw = psum[:, LB, 0:TG * E].rearrange("p (t e) -> p t e", t=TG)
                if router_bias is not None:
                    dve.tensor_tensor(logits[:], raw, bias_r[:].unsqueeze(1).to_broadcast([P, TG, E]), ALU.add)
                else:
                    dve.tensor_copy(logits[:], raw)
                dve.drain()
                dve.tensor_reduce(row[:, 0:TG], logits[:], X, ALU.max)
                dve.drain()
                dve.tensor_tensor(logits[:], logits[:], per_row(row[:, 0:TG]),
                                  ALU.subtract).then_inc(sem["logits_shifted"], 1)
                dve.wait_ge(sem["exps_ready"], g + 1)
                dve.tensor_reduce(row[:, 0:TG], probs[:], X, ALU.add)
                dve.drain()
                dve.reciprocal(row[:, 0:TG], row[:, 0:TG])
                dve.drain()
                dve.tensor_tensor(probs[:], probs[:], per_row(row[:, 0:TG]), ALU.mult)
                if SHARED:
                    dve.wait_ge(sem["gate_ready"], g + 1)
                    gu = psum[:, GUB:GUB + 2, :].rearrange("p a (u k) -> p (a u) k", u=2)
                    dve.tensor_tensor(hid[:], gate[:], gu[:, :, I:2 * I], ALU.mult).then_inc(sem["hid_ready"], 1)
                if LATER and not first:
                    find_places(g - 1)
                dve.drain()
                for t in range(TG):
                    dve.max(top_g[:, t, :], probs[:, t, :])
                dve.drain()
                for t in range(TG):
                    dve.max_index(top_i[:, t, :], top_g[:, t, :], probs[:, t, :])
                dve.tensor_copy(top[:, bass.ds(g * TG, TG), :], top_g[:])
                dve.drain()
                dve.tensor_copy(top_if[:], top_i[:])
                if SHARED:
                    dve.wait_ge(sem["hT_hi_ready"], g + 1)
                    dve.tensor_tensor(hT_lo[0:I, :], psum[0:I, HB, :], hT_hi[0:I, :].bitcast(F32),
                                      ALU.subtract).then_inc(sem["hT_lo_ready"], 1)
                if SHARED:
                    dve.wait_ge(sem["y_ready"], g + 1)
                    rows = x[:, bass.ds(g * (TG * D), TG * D)]
                    dve.tensor_tensor(rows, rows, psum[:, YB:YB + 2, :].rearrange("p a b -> p (a b)"), ALU.add)
                if not LATER:
                    dve.drain()
                    mark_choices(g)
                    split_lo(g)
                    find_places(g)

            def mark_choices(g):
                dve.tensor_tensor(choices[:], const.iota[:, 0:E].unsqueeze(1).unsqueeze(1).to_broadcast([P, TG, K, E]),
                                  top_if[:, :, 0:K].unsqueeze(3).to_broadcast([P, TG, K, E]), ALU.is_equal)
                dve.drain()
                dve.tensor_reduce(counts_g[:], choices[:].rearrange("p t k e -> p t e k"), X, ALU.add)
                dve.drain()
                dve.tensor_copy(chosen[:], counts_g[:]).then_inc(sem["chosen_ready"], 1)

            def find_places(g):
                dve.wait_ge(sem["counts_ready"], g + 1)
                dve.tensor_tensor(places[:], psum[:, RB, 0:TG * E].rearrange("p (t e) -> p t e", t=TG),
                                  list_end[:].unsqueeze(1).to_broadcast([P, TG, E]), ALU.add)
                dve.drain()
                dve.tensor_tensor(list_end[:], list_end[:], psum[:, RB, TG * E:(TG + 1) * E], ALU.add)
                dve.tensor_tensor(choices[:], choices[:], places[:].unsqueeze(2).to_broadcast([P, TG, K, E]), ALU.mult)
                dve.drain()
                dve.tensor_reduce(place_f[:], choices[:], X, ALU.add)
                dve.drain()
                mine = bass.ds(g * COLS, COLS)
                flat = place_f[:].rearrange("p t k -> p (t k)")
                dve.tensor_copy(place_all[:, mine], flat)
                dve.tensor_copy(place_u[:, mine], flat).then_inc(sem["places_ready"], 1)

            def split_lo(g):
                if split:
                    for k in range(EPG):
                        cols = expert_columns(g * EPG + k)
                        dve.wait_ge(sem["weights_hi"], g * EPG + k + 1 + SHARED)
                        dve.tensor_tensor(keep.w_lo[:, cols], w_raw[:, k, :], keep.w_hi[:, cols].bitcast(F32),
                                          ALU.subtract).then_inc(sem["weights_lo"], 1)

            dve.memset(step_back[:, 0:1], 0.0)
            normalise(0)
            group(0, True, False)
            with dve.Fori(1, NG - 3) as g:
                group(g, False, False)
            group(NG - 3, False, False)
            group(NG - 2, False, False)
            group(NG - 1, False, True)
            dve.drain()
            if LATER:
                mark_choices(NG - 1)
                split_lo(NG - 1)
                find_places(NG - 1)
                dve.drain()

            dve.tensor_tensor(counts[:], list_end[:], list_start[:], ALU.subtract)
            dve.drain()
            dve.tensor_tensor(over[:], counts[:].unsqueeze(2).to_broadcast([P, E, NT]),
                              const.slot_steps[:, 0:NT].unsqueeze(1).to_broadcast([P, E, NT]), ALU.is_gt)
            dve.drain()
            dve.tensor_reduce(n_tiles[:], over[:], X, ALU.add)
            dve.drain()
            dve.tensor_tensor_scan(tile_end[:], ones[:], n_tiles[:], 0.0, ALU.mult, ALU.add)
            dve.drain()
            slot_tile = const.token_id[:, 0:NC]
            dve.tensor_tensor(ends[:], slot_tile.unsqueeze(2).to_broadcast([P, NC, E]),
                              tile_end[:].unsqueeze(1).to_broadcast([P, NC, E]), ALU.is_ge)
            dve.drain()
            dve.tensor_reduce(list_row_f[:], ends[:], X, ALU.add)
            dve.drain()
            dve.tensor_tensor(ends[:], ends[:], n_tiles[:].unsqueeze(1).to_broadcast([P, NC, E]), ALU.mult)
            dve.drain()
            dve.tensor_reduce(tiles_before[:], ends[:], X, ALU.add)
            dve.scalar_tensor_tensor(list_row_f[:], list_row_f[:], float(NT), slot_tile, ALU.mult, ALU.add)
            dve.drain()
            dve.tensor_tensor(list_row_f[:], list_row_f[:], tiles_before[:], ALU.subtract)
            dve.drain()
            dve.tensor_scalar(list_row_f[:], list_row_f[:], float(E * NT - 1), None, ALU.min)
            dve.drain()
            dve.tensor_copy(list_row[:], list_row_f[:]).then_inc(sem["list_rows_ready"], 1)
            before = wide[:, 0:NS * E].rearrange("p (n e) -> p n e", e=E)
            dve.tensor_tensor(before, const.tile_no[:, 0:NS].unsqueeze(2).to_broadcast([P, NS, E]),
                              tile_end[:].unsqueeze(1).to_broadcast([P, NS, E]), ALU.is_ge)
            dve.drain()
            dve.tensor_reduce(expert_f[:], before, X, ALU.add)
            dve.drain()
            dve.tensor_scalar(expert_f[:], expert_f[:], float(E - 1), None, ALU.min)
            dve.drain()
            dve.tensor_copy(packed_f[:], expert_f[:])
            for m in range(1, PACK):
                dve.drain()
                dve.scalar_tensor_tensor(packed_f[:, 0:NS - m], expert_f[:, m:NS], float(E ** m),
                                         packed_f[:, 0:NS - m], ALU.mult, ALU.add)
            dve.drain()
            dve.tensor_copy(keep.experts_u[:], packed_f[:])
            dve.tensor_scalar(step_back[:, 1:E], n_tiles[:, 0:E - 1], -float(P), float(CAP), ALU.mult, ALU.add)
            started = wide[:, 0:NT * K * E].rearrange("p (n e) -> p n e", e=E)
            dve.tensor_tensor(started, place_all[:].unsqueeze(2).to_broadcast([P, NT * K, E]),
                              list_start[:].unsqueeze(1).to_broadcast([P, NT * K, E]), ALU.is_ge)
            dve.drain()
            dve.tensor_tensor(started, started, step_back[:].unsqueeze(1).to_broadcast([P, NT * K, E]), ALU.mult)
            dve.drain()
            dve.tensor_reduce(moved[:], started, X, ALU.add)
            dve.drain()
            dve.tensor_tensor(moved[:], place_all[:], moved[:], ALU.subtract)
            dve.drain()
            dve.tensor_copy(keep.slot_u[:], moved[:])
            weights_of(dve, top, cum, keep.top_w, row, NT)
            dve.wait_ge(sem["listT_ready"], NC)
            dve.tensor_copy(keep.token_u[:], psum[:, GUB, 0:NS])

        @block.tensor
        def _(pe):
            pe.wait_ge(sem["router_split"], 2)
            if SHARED:
                pe.wait_ge(sem["weights_lo"], 1)

            def transpose_rows(g):
                pe.wait_ge(sem["xn_ready"], g + 1)
                for c in range(DC):
                    for t in range(TG):
                        ins = pe.transpose(psum[:, HB + c, t * P:(t + 1) * P], xn[:, t, c * P:(c + 1) * P],
                                           const.ident[:])
                    ins.then_inc(sem["xnT_ready"], 1)

            def count_choices(g):
                pe.wait_ge(sem["chosen_ready"], g + 1)
                for t in range(TG):
                    for before in range(t):
                        pe.matmul(psum[:, RB, t * E:(t + 1) * E], const.all_ones[:], chosen[:, before, :],
                                  start=(before == 0), stop=False)
                    pe.matmul(psum[:, RB, t * E:(t + 1) * E], const.before[:], chosen[:, t, :],
                              start=(t == 0), stop=True)
                for t in range(TG):
                    ins = pe.matmul(psum[:, RB, TG * E:(TG + 1) * E], const.all_ones[:], chosen[:, t, :],
                                    start=(t == 0), stop=(t == TG - 1))
                ins.then_inc(sem["counts_ready"], 1)

            def group(g, first, last):
                pe.wait_ge(sem["xT_lo_ready"], g * DC + DC)
                for t in range(TG):
                    tok = slice(t * P, (t + 1) * P)
                    for c in range(DC):
                        ins = product3(pe, psum[:, LB, t * E:(t + 1) * E], xT_hi[:, c, tok], xT_lo[:, c, tok],
                                       wr_hi[:, c, :], wr_lo[:, c, :], c == 0, c == DC - 1)
                ins.then_inc(sem["logits_ready"], 1)
                if SHARED:
                    base = E * C
                    for t in range(TG):
                        tok = slice(t * P, (t + 1) * P)
                        for c in range(DC):
                            cols = slice(base + c * GU, base + (c + 1) * GU)
                            ins = product3(pe, psum[:, GUB + t // 2, (t % 2) * (BANK // 2):(t % 2) * (BANK // 2) + GU],
                                           xT_hi[:, c, tok], xT_lo[:, c, tok], keep.w_hi[:, cols], keep.w_lo[:, cols],
                                           c == 0, c == DC - 1)
                    ins.then_inc(sem["gate_up_ready"], 1)
                if LATER and not first:
                    count_choices(g - 1)
                if SHARED:
                    pe.wait_ge(sem["hid_ready"], g + 1)
                    for t in range(TG):
                        ins = pe.transpose(psum[0:I, HB, t * P:(t + 1) * P], hid[:, t, :], const.ident[:])
                    ins.then_inc(sem["hidT_ready"], 1)
                    pe.wait_ge(sem["hT_lo_ready"], g + 1)
                    cols = slice(base + DC * GU, base + C)
                    for t in range(TG):
                        tok = slice(t * P, (t + 1) * P)
                        ins = product3(pe, psum[:, YB + t // 2, (t % 2) * D:(t % 2 + 1) * D], hT_hi[0:I, tok],
                                       hT_lo[0:I, tok], keep.w_hi[0:I, cols], keep.w_lo[0:I, cols], True, True)
                    ins.then_inc(sem["y_ready"], 1)
                if not last:
                    transpose_rows(g + 1)
                if not LATER:
                    count_choices(g)

            transpose_rows(0)
            group(0, True, False)
            with pe.Fori(1, NG - 1) as g:
                group(g, False, False)
            group(NG - 1, False, True)
            if LATER:
                count_choices(NG - 1)
            pe.wait_ge(keep.dma_sems.tokens_in, 16 * NC)
            for c in range(NC):
                pe.transpose(psum[:, GUB, c * P:(c + 1) * P], tokens_of[:, c, :],
                             const.ident[:]).then_inc(sem["listT_ready"], 1)


def slot_stage(nc, tag, psum, const, spec, keep):
    E, SHARED, I, K, _ = spec
    NS = keep.NS
    GU = 2 * I
    C = DC * GU + D
    ROUND = 8
    RING = 4
    split = keep.w_hi is None
    with ExitStack() as ctx:
        mem = Pool_(nc, ctx, tag)
        xg = mem.sb("xg", [P, ROUND, D])
        xT_hi, xT_lo = (mem.sb(f"xT_{s}", [P, RING, D], F32R) for s in ("hi", "lo"))
        gate = mem.sb("gate", [P, RING, I])
        hid = mem.sb("hid", [P, RING, I])
        hT_hi, hT_lo = (mem.sb(f"hT_{s}", [P, RING, P], F32R) for s in ("hi", "lo"))
        y = mem.sb("y", [P, RING, D])
        token_cols = mem.sb("token_cols", [P, 2 * ROUND], U32)
        if split:
            wt_hi, wt_lo = (mem.sb(f"wt_{s}", [P, ROUND, C], F32R) for s in ("hi", "lo"))
        names = ("rows_transposed", "xT_hi_ready", "xT_lo_ready", "gate_up_ready", "gate_ready", "hid_ready",
                 "hidT_ready", "hT_hi_ready", "hT_lo_ready", "y_ready", "y_copied", "wt_hi_ready", "wt_lo_ready")
        sem = {name: mem.sem(name) for name in names}
        gathered = keep.dma_sems.rows_gathered
        stored = [mem.sem(f"stored{j}") for j in range(RING)]

        def ring_of_psum(first_bank, width):
            return lambda n: psum[:, first_bank + n % 2, 0:width]

        rowsT_ps, gate_up_ps = ring_of_psum(0, D), ring_of_psum(2, GU)
        hidT_ps, y_ps = ring_of_psum(4, P), ring_of_psum(6, D)

        def steps(eng, before, step, load):
            before()
            for r in (0, ROUND):
                load(r)
                for j in range(ROUND):
                    step(r + j, j)
            with eng.Fori(2, NS // ROUND - 1) as i:
                load(i * ROUND)
                for j in range(ROUND):
                    step(i * ROUND + j, j)
            load(NS - ROUND)
            for j in range(ROUND):
                step(NS - ROUND + j, j)

        def experts_from(eng, n):
            word = eng.value_load(keep.experts_u[0:1, bass.ds(n, 1)])
            return [eng.snap((word // E ** m) % E) for m in range(PACK)]

        def at_least(n, value):
            return not isinstance(n, int) or n >= value

        def at_most(n, value):
            return not isinstance(n, int) or n <= value

        def weight_experts(eng, expert, r):
            expert.update(zip(range(5, 9), experts_from(eng, r + 5)))
            if at_most(r, NS - 2 * ROUND):
                expert.update(zip(range(9, 13), experts_from(eng, r + 9)))

        ctx.callback(mem.clear_sems)
        block = ctx.enter_context(nc.Block())

        @block.sync
        def _(sp):
            with sp.Fori(0, NS // RING) as i:
                for j in range(RING):
                    sp.wait_ge(sem["y_copied"], i * RING + j + 1)
                    sp.dma_start(keep.y_rows[bass.ds(i * RING + j, 1)].rearrange("o p d -> p (o d)"),
                                 y[:, j, :]).then_inc(stored[j], 16)
            for j in range(RING):
                sp.wait_ge(stored[j], 16 * (NS // RING))

        @block.gpsimd
        def _(pool):
            def two_rounds(i, first):
                for half in range(2):
                    base = i * (2 * ROUND) + half * ROUND
                    if not first:
                        pool.wait_ge(sem["rows_transposed"], base - ROUND)
                        hold(pool, const, half * (ROUND + 1))
                    pool.tensor_copy(token_cols[:, half * ROUND:(half + 1) * ROUND],
                                     keep.token_u[:, bass.ds(base, ROUND)])
                    pool.drain()
                    for j in range(ROUND):
                        if not (first and half == 0):
                            pool.wait_ge(sem["rows_transposed"], base + j - ROUND + 1)
                            hold(pool, const, half * (ROUND + 1) + 1 + j)
                        c = half * ROUND + j
                        pool.indirect_dma_start(xg[:, j, :], None, keep.xn_flat,
                                                bass.IndirectOffsetOnAxis(token_cols[:, c:c + 1], 0)
                                                ).then_inc(gathered[j], 16)

            two_rounds(0, True)
            with pool.Fori(1, NS // (2 * ROUND)) as i:
                two_rounds(i, False)

        @block.scalar
        def _(act):
            def rows_hi(n, j):
                act.wait_ge(sem["rows_transposed"], n + 1)
                act.activation(xT_hi[:, j % RING, :], rowsT_ps(j), ACT.Copy).then_inc(sem["xT_hi_ready"], 1)

            expert = {}

            def load(r):
                if split:
                    weight_experts(act, expert, r)

            def weights_hi(n, j, e):
                act.activation(wt_hi[:, j, :], keep.w_raw[:, bass.ds(e * C, C)],
                               ACT.Copy).then_inc(sem["wt_hi_ready"], 1)

            def silu(n, j):
                act.wait_ge(sem["gate_up_ready"], n + 1)
                act.activation(gate[:, j % RING, :], gate_up_ps(j)[:, 0:I], ACT.Silu).then_inc(sem["gate_ready"], 1)

            def hidden_hi(n, j):
                act.wait_ge(sem["hidT_ready"], n + 1)
                act.activation(hT_hi[0:I, j % RING, :], hidT_ps(j)[0:I], ACT.Copy).then_inc(sem["hT_hi_ready"], 1)

            def copy_y(n, j):
                act.wait_ge(sem["y_ready"], n + 1)
                if at_least(n, RING):
                    act.wait_ge(stored[j % RING], (n - j % RING) * (16 // RING))
                act.activation(y[:, j % RING, :], y_ps(j), ACT.Copy).then_inc(sem["y_copied"], 1)

            def before():
                if split:
                    for j, e in enumerate(experts_from(act, 0) + experts_from(act, 4)[0:1]):
                        weights_hi(j, j, e)
                for n in range(4):
                    rows_hi(n, n)
                silu(0, 0)
                silu(1, 1)

            def step(n, j):
                if at_most(n, NS - 5):
                    rows_hi(n + 4, (j + 4) % ROUND)
                if at_most(n, NS - 3):
                    silu(n + 2, (j + 2) % ROUND)
                hidden_hi(n, j)
                if at_least(n, 3):
                    copy_y(n - 3, (j - 3) % ROUND)
                if split and at_most(n, NS - 6):
                    weights_hi(n + 5, (j + 5) % ROUND, expert[j + 5])

            steps(act, before, step, load)
            for n in range(NS - 3, NS):
                copy_y(n, n % ROUND)

        @block.vector
        def _(dve):
            def rows_lo(n, j):
                dve.wait_ge(sem["xT_hi_ready"], n + 1)
                dve.tensor_tensor(xT_lo[:, j % RING, :], rowsT_ps(j), xT_hi[:, j % RING, :].bitcast(F32),
                                  ALU.subtract).then_inc(sem["xT_lo_ready"], 1)

            expert = {}

            def load(r):
                if split:
                    weight_experts(dve, expert, r)

            def weights_lo(n, j, e):
                dve.wait_ge(sem["wt_hi_ready"], n + 1)
                dve.tensor_tensor(wt_lo[:, j, :], keep.w_raw[:, bass.ds(e * C, C)], wt_hi[:, j, :].bitcast(F32),
                                  ALU.subtract).then_inc(sem["wt_lo_ready"], 1)

            def hidden(n, j):
                dve.wait_ge(sem["gate_ready"], n + 1)
                dve.tensor_tensor(hid[:, j % RING, :], gate[:, j % RING, :], gate_up_ps(j)[:, I:2 * I],
                                  ALU.mult).then_inc(sem["hid_ready"], 1)

            def hidden_lo(n, j):
                dve.wait_ge(sem["hT_hi_ready"], n + 1)
                dve.tensor_tensor(hT_lo[0:I, j % RING, :], hidT_ps(j)[0:I], hT_hi[0:I, j % RING, :].bitcast(F32),
                                  ALU.subtract).then_inc(sem["hT_lo_ready"], 1)

            def before():
                if split:
                    for j, e in enumerate(experts_from(dve, 0) + experts_from(dve, 4)[0:1]):
                        weights_lo(j, j, e)
                for n in range(4):
                    rows_lo(n, n)
                hidden(0, 0)
                hidden(1, 1)

            def step(n, j):
                if at_most(n, NS - 5):
                    rows_lo(n + 4, (j + 4) % ROUND)
                if at_most(n, NS - 3):
                    hidden(n + 2, (j + 2) % ROUND)
                hidden_lo(n, j)
                if split and at_most(n, NS - 6):
                    weights_lo(n + 5, (j + 5) % ROUND, expert[j + 5])

            steps(dve, before, step, load)

        @block.tensor
        def _(pe):
            expert = {}

            def load(r):
                if split:
                    return
                if at_least(r, 1):
                    expert.update(zip(range(-2, 2), experts_from(pe, r - 2)))
                else:
                    expert.update(zip(range(0, 4), experts_from(pe, 0)))
                expert.update(zip(range(2, 6), experts_from(pe, r + 2)))
                expert.update(zip(range(6, 10), experts_from(pe, r + 6)))

            def weights(e, j, first, last):
                if split:
                    return wt_hi[:, j, first:last], wt_lo[:, j, first:last]
                cols = bass.ds(e * C + first, last - first)
                return keep.w_hi[:, cols], keep.w_lo[:, cols]

            def transpose_rows(n, j):
                pe.wait_ge(gathered[j], (n - j) * (16 // ROUND) + 16)
                if at_least(n, 2):
                    pe.wait_ge(sem["xT_lo_ready"], n - 1)
                for c in range(DC):
                    ins = pe.transpose(rowsT_ps(j)[:, c * P:(c + 1) * P], xg[:, j, c * P:(c + 1) * P],
                                       const.ident[:])
                ins.then_inc(sem["rows_transposed"], 1)

            def gate_up(n, j, e):
                pe.wait_ge(sem["xT_lo_ready"], n + 1)
                if split:
                    pe.wait_ge(sem["wt_lo_ready"], n + 1)
                if at_least(n, 2):
                    pe.wait_ge(sem["hid_ready"], n - 1)
                hi, lo = weights(e, j, 0, DC * GU)
                for c in range(DC):
                    part = slice(c * P, (c + 1) * P)
                    cols = slice(c * GU, (c + 1) * GU)
                    ins = product3(pe, gate_up_ps(j), xT_hi[:, j % RING, part], xT_lo[:, j % RING, part],
                                   hi[:, cols], lo[:, cols], c == 0, c == DC - 1)
                ins.then_inc(sem["gate_up_ready"], 1)

            def transpose_hidden(n, j):
                pe.wait_ge(sem["hid_ready"], n + 1)
                if at_least(n, 2):
                    pe.wait_ge(sem["hT_lo_ready"], n - 1)
                pe.transpose(hidT_ps(j)[0:I], hid[:, j % RING, :], const.ident[:]).then_inc(sem["hidT_ready"], 1)

            def down(n, j, e):
                pe.wait_ge(sem["hT_lo_ready"], n + 1)
                if at_least(n, 2):
                    pe.wait_ge(sem["y_copied"], n - 1)
                hi, lo = weights(e, j, DC * GU, C)
                product3(pe, y_ps(j), hT_hi[0:I, j % RING, :], hT_lo[0:I, j % RING, :],
                         hi[0:I], lo[0:I], True, True).then_inc(sem["y_ready"], 1)

            def before():
                for n in range(4):
                    transpose_rows(n, n)
                first = [None] * 2 if split else experts_from(pe, 0)
                for n in range(2):
                    gate_up(n, n, first[n])

            def step(n, j):
                if at_most(n, NS - 5):
                    transpose_rows(n + 4, (j + 4) % ROUND)
                if at_most(n, NS - 3):
                    gate_up(n + 2, (j + 2) % ROUND, expert.get(j + 2))
                transpose_hidden(n, j)
                if at_least(n, 2):
                    down(n - 2, (j - 2) % ROUND, expert.get(j - 2))

            steps(pe, before, step, load)
            for j in (ROUND - 2, ROUND - 1):
                down(NS - ROUND + j, j, expert.get(j))


def gather_stage(nc, tag, x, const, spec, NG, keep, store=None):
    K = spec[3]
    NT = NG * TG
    TB = TG
    COLS = TB * K
    ROUNDS = NT // TB
    with ExitStack() as ctx:
        mem = Pool_(nc, ctx, tag)
        yg = mem.sb("yg", [P, 2, COLS, D])
        slot_cols = mem.sb("slot_cols", [P, 2, COLS], U32)
        gathered = keep.dma_sems.y_gathered
        columns_ready, added, held, rows_stored = (mem.sem(name) for name in
                                                   ("columns_ready", "added", "held", "rows_stored"))
        ctx.callback(mem.clear_sems)
        block = ctx.enter_context(nc.Block())

        @block.gpsimd
        def _(pool):
            def one_round(b):
                for c in range(COLS):
                    pool.indirect_dma_start(yg[:, b, c, :], None, keep.y_flat,
                                            bass.IndirectOffsetOnAxis(slot_cols[:, b, c:c + 1], 0)
                                            ).then_inc(gathered[b * COLS + c], 16)

            pool.wait_ge(columns_ready, 1)
            hold(pool, const).then_inc(held, 1)
            one_round(0)
            one_round(1)
            with pool.Fori(1, ROUNDS // 2) as i:
                for b in range(2):
                    pool.wait_ge(added, i * 2 + b - 1)
                    pool.wait_ge(held, i * 2 + b - 1)
                    hold(pool, const).then_inc(held, 1)
                    one_round(b)

        @block.vector
        def _(dve):
            def one_round(i, b, last):
                for k in range(K):
                    for t in range(TB):
                        dve.wait_ge(gathered[b * COLS + t * K + k], (i - b) * 8 + 16)
                        tile = i * TB + t
                        rows = x[:, bass.ds(tile * D, D)]
                        weight = keep.top_w[:, bass.ds(tile, 1), k:k + 1].rearrange("p a b -> p (a b)")
                        ins = dve.scalar_tensor_tensor(rows, yg[:, b, t * K + k, :], weight, rows,
                                                       ALU.mult, ALU.add)
                    if k < K - 1:
                        dve.drain()
                if not last:
                    ins = dve.tensor_copy(slot_cols[:, b, :], keep.slot_u[:, bass.ds(i * COLS + 2 * COLS, COLS)])
                ins.then_inc(added, 1)

            dve.tensor_copy(slot_cols[:].rearrange("p b c -> p (b c)"), keep.slot_u[:, 0:2 * COLS]).then_inc(
                columns_ready, 1)
            with dve.Fori(0, ROUNDS // 2 - 1) as i:
                for b in range(2):
                    one_round(i * 2 + b, b, False)
            for b in range(2):
                one_round(ROUNDS - 2 + b, b, True)

        if store is not None:
            out_rounds = store.rearrange("b (r s) d -> (b r) s d", s=TB * P)

            @block.sync
            def _(sp):
                with sp.Fori(0, NT // TB) as i:
                    sp.wait_ge(added, i + 1)
                    sp.dma_start(out_rounds[bass.ds(i, 1)].rearrange("b (t p) d -> p (b t) d", p=P),
                                 x[:, bass.ds(i * (TB * D), TB * D)].rearrange("p (n d) -> p n d", d=D)
                                 ).then_inc(rows_stored, 16)
                sp.wait_ge(rows_stored, 16 * (NT // TB))


class GatherSems:

    def __init__(self, nc, ctx, tag, K):
        mem = Pool_(nc, ctx, tag)
        self.scattered = [mem.sem(f"{s}_rounds_scattered") for s in ("even", "odd")]
        self.tokens_in = mem.sem("tokens_in")
        self.rows_gathered = [mem.sem(f"rows_gathered{j}") for j in range(8)]
        self.y_gathered = [mem.sem(f"y_gathered{c}") for c in range(2 * TG * K)]


class Kept:

    def __init__(self, nc, ctx, tag, spec, NG, resident, dma_sems):
        self.dma_sems = dma_sems
        E, SHARED, I, K, _ = spec
        mem = Pool_(nc, ctx, tag)
        NT, C = NG * TG, DC * 2 * I + D
        self.NS = NS = slot_tiles(NT * P, E, K, 16)
        self.w_hi = self.w_lo = self.w_raw = None
        if resident:
            self.w_hi, self.w_lo = (mem.sb(f"w_{s}", [P, (E + SHARED) * C], F32R) for s in ("hi", "lo"))
        else:
            self.w_raw = mem.sb("w_raw", [P, E * C])
        self.top_w = mem.sb("top_w", [P, NT, 8])
        self.slot_u = mem.sb("slot_u", [P, NT * K], U32)
        self.token_u = mem.sb("token_u", [P, NS], U32)
        self.experts_u = mem.sb("experts_u", [P, NS], U32)
        self.lists = nc.dram_tensor(f"{tag}_lists", (E * NT * P, 1), F32).ap()
        self.list_tiles = self.lists.rearrange("(n s) o -> n (s o)", s=P)
        self.xn_rows = nc.dram_tensor(f"{tag}_xn_rows", (NG, SEQ, D), F32).ap()
        self.xn_flat = self.xn_rows.rearrange("b s d -> (b s) d")
        self.y_rows = nc.dram_tensor(f"{tag}_y_rows", (NS, P, D), F32).ap()
        self.y_flat = self.y_rows.rearrange("n p d -> (n p) d")


def top2_weights(dve, top, cum, top_w, row, NT):
    dve.tensor_reduce(row[:], top[:, :, 0:2], X, ALU.add)
    dve.drain()
    dve.tensor_scalar(row[:], row[:], 1e-9, None, ALU.add)
    dve.drain()
    dve.reciprocal(row[:], row[:])
    dve.drain()
    dve.tensor_tensor(top_w[:, :, 0:2], top[:, :, 0:2], row[:].unsqueeze(2).to_broadcast([P, NT, 2]), ALU.mult)


def top8_weights(dve, top, cum, top_w, row, NT):
    def normalise(dst, src):
        dve.tensor_reduce(row[:], src, X, ALU.add)
        dve.drain()
        dve.tensor_scalar(row[:], row[:], 1e-12, None, ALU.max)
        dve.drain()
        dve.reciprocal(row[:], row[:])
        dve.drain()
        dve.tensor_tensor(dst, src, row[:].unsqueeze(2).to_broadcast([P, NT, 8]), ALU.mult)
        dve.drain()

    normalise(top_w[:], top[:])
    dve.tensor_copy(cum[:, :, 0], top_w[:, :, 0])
    for k in range(1, 7):
        dve.drain()
        dve.tensor_tensor(cum[:, :, k], cum[:, :, k - 1], top_w[:, :, k], ALU.add)
    dve.drain()
    dve.scalar_tensor_tensor(top_w[:, :, 1:8], cum[:, :, 0:7], 0.8, top[:, :, 1:8], ALU.is_lt, ALU.mult)
    dve.tensor_copy(top_w[:, :, 0:1], top[:, :, 0:1])
    dve.drain()
    normalise(top_w[:], top_w[:])


def routed_layer(nc, tag, x, psum, const, w_all, w_router, router_bias, spec, NG, resident, dma_sems, store=None):
    with ExitStack() as ctx:
        keep = Kept(nc, ctx, f"{tag}_keep", spec, NG, resident, dma_sems)
        route_stage(nc, f"{tag}_route", x, psum, const, w_all, w_router, router_bias, spec, NG, keep)
        slot_stage(nc, f"{tag}_slots", psum, const, spec, keep)
        gather_stage(nc, f"{tag}_gather", x, const, spec, NG, keep, store)


class Const:
    pass


def two_layers(nc, x_in, wqkv0, wo0, bqkv0, bo0, w_router0, b_router0, w_experts0, wqkv1, wo1, bqkv1, bo1,
               w_router1, w_experts1, ident, mask_sel, mask_rows, mask_rowsT, alibi4, iota, slot_steps, token_id, before, out):
    E0, E1 = w_router0.shape[1], w_router1.shape[1]
    I0 = (w_experts0.shape[2] - D) // (2 * DC)
    I1 = (w_experts1.shape[2] - D) // (2 * DC)
    NG = x_in.shape[0]
    NT = NG * TG
    with ExitStack() as ctx:
        mem = Pool_(nc, ctx, "all")
        x = mem.sb("x", [P, NT * D])
        gather_sems = [GatherSems(nc, ctx, f"moe{layer}", K) for layer, K in enumerate((2, 7))]
        const = Const()
        const.ident = mem.sb("ident", [P, P])
        const.mask_sel = mem.sb("mask_sel", [P, 2, P], BF16)
        const.mask_rows = mem.sb("mask_rows", [P, 2, P], BF16)
        const.mask_rowsT = mem.sb("mask_rowsT", [P, 2, P], BF16)
        const.minus_half = mem.sb("minus_half", [P, TG])
        const.ones = mem.sb("ones", [P, 8])
        const.tick = mem.sb("tick", [P, 19])
        const.iota = mem.sb("iota", [P, iota.shape[1]])
        const.tile_no = const.iota
        const.slot_steps = mem.sb("slot_steps", [P, NT])
        const.token_id = mem.sb("token_id", [P, NT])
        const.before = mem.sb("before", [P, P], BF16)
        const.all_ones = mem.sb("all_ones", [P, P], BF16)
        alibi = mem.sb("alibi", [P, TG, H])
        psum = ctx.enter_context(nc.psum_tensor("psum", [P, 8, BANK], F32))

        with ExitStack() as first:
            mem0 = Pool_(nc, first, "load")
            masks = mem0.sb("masks", [P, 3, 2, P])
            before_raw = mem0.sb("before_raw", [P, P])
            x_loaded = mem0.sem("x_loaded")
            consts_loaded = mem0.sem("consts_loaded")
            first.callback(mem0.clear_sems)
            block = first.enter_context(nc.Block())

            @block.sync
            def _(sp):
                sp.dma_start(const.ident[:], ident).then_inc(consts_loaded, 16)
                sp.dma_start(const.iota[:], iota).then_inc(consts_loaded, 16)
                sp.dma_start(const.slot_steps[:], slot_steps[:, 0:NT]).then_inc(consts_loaded, 16)
                sp.dma_start(const.token_id[:], token_id[:, 0:NT]).then_inc(consts_loaded, 16)
                sp.dma_start(before_raw[:], before).then_inc(consts_loaded, 16)
                sp.dma_start(masks[:, 0], mask_sel).then_inc(consts_loaded, 16)
                sp.dma_start(masks[:, 1], mask_rows).then_inc(consts_loaded, 16)
                sp.dma_start(masks[:, 2], mask_rowsT).then_inc(consts_loaded, 16)
                sp.dma_start(alibi[:], alibi4.rearrange("t p h -> p t h")).then_inc(consts_loaded, 16)
                sp.dma_start(x[:, 0:TG * D].rearrange("p (n d) -> p n d", d=D),
                             x_in[0:1].rearrange("b (t p) d -> p (b t) d", p=P)).then_inc(x_loaded, 16)
                sp.wait_ge(x_loaded, 16)

            @block.vector
            def _(dve):
                dve.memset(const.minus_half[:], -0.5)
                dve.memset(const.ones[:], 1.0)
                dve.memset(const.tick[:], 0.0)
                dve.memset(const.all_ones[:], 1.0)
                dve.wait_ge(consts_loaded, 16 * 9)
                dve.tensor_copy(const.before[:], before_raw[:])
                dve.tensor_copy(const.mask_sel[:], masks[:, 0])
                dve.tensor_copy(const.mask_rows[:], masks[:, 1])
                dve.tensor_copy(const.mask_rowsT[:], masks[:, 2])

        attention_stage(nc, "attn0", x, psum, const, wqkv0, wo0, bqkv0, bo0, alibi[:], NG, x_in=x_in)

        routed_layer(nc, "moe0", x, psum, const, w_experts0, w_router0, b_router0, (E0, 1, I0, 2, top2_weights),
                     NG, True, gather_sems[0])

        attention_stage(nc, "attn1", x, psum, const, wqkv1, wo1, bqkv1, bo1, None, NG)

        routed_layer(nc, "moe1", x, psum, const, w_experts1, w_router1, None, (E1, 0, I1, 7, top8_weights),
                     NG, False, gather_sems[1], store=out)


def laid_out(inputs):
    import numpy as np

    def experts(gate_up, down):
        n, d, gu = gate_up.shape
        out = np.zeros((n, P, DC * gu + d), gate_up.dtype)
        out[:, :, :DC * gu] = gate_up.reshape(n, DC, P, gu).transpose(0, 2, 1, 3).reshape(n, P, DC * gu)
        out[:, :down.shape[1], DC * gu:] = down
        return out

    a = {k: np.asarray(v) for k, v in inputs.items()}
    gu0 = np.concatenate([np.concatenate([a["L0_ffn_Wg"], a["L0_ffn_sWg"][None]], 0),
                          np.concatenate([a["L0_ffn_Wu"], a["L0_ffn_sWu"][None]], 0)], 2)
    dn0 = np.concatenate([a["L0_ffn_Wd"], a["L0_ffn_sWd"][None]], 0)
    i = np.arange(P)
    above = np.where(i[None, :] > i[:, None], np.float32(NEG), np.float32(0))
    slopes = np.float32(2.0 ** (-8.0 / H)) ** np.arange(1, H + 1, dtype=np.float32)
    distances = np.arange(1 - SEQ, 1, dtype=np.float32)
    alibi = (np.float32(HD) ** np.float32(0.5)) * slopes[None, :] * distances[:, None]
    return {
        "x_in": a["L0_attn_x"],
        "wqkv0": np.concatenate([a["L0_attn_Wq"], a["L0_attn_Wk"], a["L0_attn_Wv"]], 1),
        "wo0": a["L0_attn_Wo"],
        "bqkv0": np.concatenate([a["L0_attn_bq"], a["L0_attn_bk"], a["L0_attn_bv"]]),
        "bo0": a["L0_attn_bo"],
        "w_router0": a["L0_ffn_Wr"].T,
        "b_router0": a["L0_ffn_bias"],
        "w_experts0": experts(gu0, dn0),
        "wqkv1": a["L1_attn_W_attn"],
        "wo1": a["L1_attn_W_proj"],
        "bqkv1": a["L1_attn_b_attn"],
        "bo1": a["L1_attn_b_proj"],
        "w_router1": a["L1_ffn_gate_weight"].T,
        "w_experts1": experts(a["L1_ffn_gate_up_proj"].transpose(0, 2, 1), a["L1_ffn_down_proj"].transpose(0, 2, 1)),
        "ident": np.eye(P, dtype=np.float32),
        "mask_sel": np.tile(np.eye(P, dtype=np.float32).reshape(2, P // 2, P), (1, 2, 1)).transpose(1, 0, 2),
        "mask_rows": np.tile(above.reshape(2, P // 2, P), (1, 2, 1)).transpose(1, 0, 2),
        "mask_rowsT": np.tile(above.T.reshape(2, P // 2, P), (1, 2, 1)).transpose(1, 0, 2),
        "alibi4": alibi.astype(np.float32).reshape(TG, P, H),
        "iota": np.broadcast_to(np.arange(256, dtype=np.float32), (P, 256)),
        "slot_steps": np.broadcast_to(P * np.arange(a["L0_attn_x"].shape[0] * TG, dtype=np.float32),
                                      (P, a["L0_attn_x"].shape[0] * TG)),
        "token_id": (P * np.arange(a["L0_attn_x"].shape[0] * TG)[None, :] + i[:, None]).astype(np.float32),
        "before": (i[:, None] < i[None, :]).astype(np.float32),
    }


def kernel(**inputs):
    import numpy as _np
    import concourse.bacc as _bacc
    from concourse.bass_utils import run_bass_kernel_spmd as _run

    nc = _bacc.Bacc("TRN2", target_bir_lowering=False, num_devices=1)
    arrays = {k: _np.ascontiguousarray(v) for k, v in laid_out(inputs).items()}
    args = {k: nc.dram_tensor(k, v.shape, mybir.dt.from_np(v.dtype), kind="ExternalInput").ap()
            for k, v in arrays.items()}
    shape = inputs["L0_attn_x"].shape
    out = nc.dram_tensor("out", shape, F32, kind="ExternalOutput").ap()
    two_layers(nc, **args, out=out)
    r = _run(nc, [arrays], core_ids=[0])
    return r.results[0]["out"]
```
